# Optimizing a Trainium2 kernel written in Bass

```python
import numpy as np
import jax
import jax.numpy as jnp

def _softmax(x, axis=-1):
    return jax.nn.softmax(x, axis=axis)

def _gelu(x):
    return jax.nn.gelu(x, approximate=True)

def _silu(x):
    return jax.nn.silu(x)

def _sigmoid(x):
    return jax.nn.sigmoid(x)

def _layernorm(x, axis=-1, eps=1e-05):
    m = jnp.mean(x, axis=axis, keepdims=True)
    v = jnp.var(x, axis=axis, keepdims=True)
    return (x - m) / jnp.sqrt(v + eps)

def _scatter_add(tgt, idx, src, axis=0):
    return tgt.at[idx].add(src)

def _segment_sum(src, seg, n):
    return jax.ops.segment_sum(src, seg, n)
kernel_name = 'mk_flamingo_gated_d4_seqx_r8_d77ac4'

def setup_inputs(seed: int=0):
    np.random.seed(seed)
    _w = jnp.asarray

    def _rec_inputs():
        import jax
        import jax.numpy as jnp
        _rk = jax.random.key(seed)
        x = -0.0002928 + 1 * jax.random.normal(jax.random.fold_in(_rk, 1), (4, 512, 128), jnp.float32)
        _lenS = 512 - jax.random.randint(jax.random.fold_in(_rk, 7), (4,), 0, max(1, 512 // 4) + 1, jnp.int32)
        _lenS2 = 77 - jax.random.randint(jax.random.fold_in(_rk, 8), (4,), 0, max(1, 77 // 4) + 1, jnp.int32)
        _ctx_1024P = jax.random.normal(jax.random.fold_in(_rk, 11), (4, 16, 128), jnp.float32)
        _ctx_1024c = jax.random.dirichlet(jax.random.fold_in(_rk, 511), 0.3 * jnp.ones((16,), jnp.float32), (4, 77))
        _ctx_1024t = jnp.einsum('bsk,bkd->bsd', _ctx_1024c, _ctx_1024P)
        _ctx_1024t = _ctx_1024t * jax.lax.rsqrt(jnp.mean(jnp.square(_ctx_1024t)) + 1e-12) * 0.953939
        ctx_1024 = -1.39393e-06 + 0.999914 * (_ctx_1024t + 0.3 * jax.random.normal(jax.random.fold_in(_rk, 611), (4, 77, 128), jnp.float32))
        fside_Bx16xSxS2_0 = -6.00028e-06 + 0.100001 * jax.random.normal(jax.random.fold_in(_rk, 12), (4, 16, 512, 77), jnp.float32)
        _validS = jnp.arange(512)[None, :] < _lenS[:, None]
        _validS2 = jnp.arange(77)[None, :] < _lenS2[:, None]
        _causal = jnp.tril(jnp.ones((512, 512), dtype=bool))
        mask_Bx1xSxS2_ik1 = jnp.where(jnp.broadcast_to(_validS2[:, None, None, :], (4, 1, 512, 77)), 1, 0).astype(jnp.int32)
        _g = jax.random.normal(jax.random.fold_in(_rk, 9001), (2, 4), jnp.float32)
        _g = jnp.sign(_g) * jnp.maximum(jnp.abs(_g), 1.0) + (_g == 0) * 1.0
        g_xattn = _g[0]
        g_ffn = _g[1]
        return (x, ctx_1024, fside_Bx16xSxS2_0, mask_Bx1xSxS2_ik1, g_xattn, g_ffn)
    x, ctx_1024, fside_Bx16xSxS2_0, mask_Bx1xSxS2_ik1, g_xattn, g_ffn = _rec_inputs()

    def _L0_xattn_setup():
        import jax, jax.numpy as jnp
        import numpy as np
        import math
        H = 16
        D = 128
        FF = 512
        DK = D // H
        EPS = 1e-05

        def layer_norm(x, g, b):
            mu = jnp.mean(x, axis=-1, keepdims=True)
            var = jnp.var(x, axis=-1, keepdims=True)
            return (x - mu) * jax.lax.rsqrt(var + EPS) * g + b
        key = jax.random.key(seed)
        ks = jax.random.split(key, 16)
        B, S = (2, 256)
        s = 1.0 / math.sqrt(D)
        return {'x_q': jax.random.normal(ks[0], (B, S, D), jnp.float32), 'x_kv': jax.random.normal(ks[1], (B, S, D), jnp.float32), 'bias': jax.random.normal(ks[2], (B, H, S, S), jnp.float32) * 0.1, 'Wq': jax.random.normal(ks[3], (D, D), jnp.float32) * s, 'Wk': jax.random.normal(ks[4], (D, D), jnp.float32) * s, 'Wv': jax.random.normal(ks[5], (D, D), jnp.float32) * s, 'Wo': jax.random.normal(ks[6], (D, D), jnp.float32) * s, 'W1': jax.random.normal(ks[7], (FF, D), jnp.float32) * s, 'b1': jnp.zeros((FF,), jnp.float32), 'W2': jax.random.normal(ks[8], (D, FF), jnp.float32) * (1.0 / math.sqrt(FF)), 'b2': jnp.zeros((D,), jnp.float32), 'g1': jnp.ones((D,), jnp.float32), 'be1': jnp.zeros((D,), jnp.float32), 'g2': jnp.ones((D,), jnp.float32), 'be2': jnp.zeros((D,), jnp.float32)}
    _L0_xattn_all = _L0_xattn_setup()
    _L0_xattn_in = {k: v for k, v in _L0_xattn_all.items() if k in ('Wq', 'Wk', 'Wv', 'Wo', 'W1', 'b1', 'W2', 'b2', 'g1', 'be1', 'g2', 'be2')}
    del _L0_xattn_all

    def _L0_ffn_setup():
        import jax, jax.numpy as jnp
        import numpy as np
        NUM_HEAVY = 128
        N_ITERS = 50
        FETCH_K_RATIO = 9.0 / 8.0
        EPS = 1.0

        def rmsnorm(x, gamma):
            scale = gamma.shape[0] ** 0.5
            normed = x / jnp.maximum(jnp.linalg.norm(x, axis=-1, keepdims=True), 1e-12)
            return normed * scale * gamma

        def feedforward(x, gamma, w1, b1, w2, b2):
            h = rmsnorm(x, gamma)
            h = jax.nn.gelu(h @ w1.T + b1, approximate=False)
            return h @ w2.T + b2

        def coor_descent(s, n_iters, k, eps):
            logk = jnp.log(jnp.asarray(k, s.dtype))
            a0 = jnp.zeros_like(s[..., :1])
            b0 = -s

            def body(carry, _):
                a, b = carry
                a = eps * (logk - jax.nn.logsumexp((s + b) / eps, axis=-1, keepdims=True))
                b = -jax.nn.relu(s + a)
                return ((a, b), None)
            (a, b), _ = jax.lax.scan(body, (a0, b0), None, length=n_iters)
            return jnp.exp((s + a + b) / eps)
        key = jax.random.key(seed)
        ks = jax.random.split(key, 12)
        b, n, dim = (8, 1024, 128)
        d_light, d_heavy = (int(dim * 0.5), dim * 4)

        def lin(k, dout, din):
            bound = 1.0 / np.sqrt(din)
            k1, k2 = jax.random.split(k)
            w = jax.random.uniform(k1, (dout, din), jnp.float32, -bound, bound)
            bb = jax.random.uniform(k2, (dout,), jnp.float32, -bound, bound)
            return (w, bb)
        x = jax.random.normal(ks[0], (b, n, dim), jnp.float32)
        routing_token = jax.random.normal(ks[1], (dim,), jnp.float32)
        w1_l, b1_l = lin(ks[2], d_light, dim)
        w2_l, b2_l = lin(ks[3], dim, d_light)
        w1_h, b1_h = lin(ks[4], d_heavy, dim)
        w2_h, b2_h = lin(ks[5], dim, d_heavy)
        return dict(x=x, routing_token=routing_token, gamma_l=jnp.ones((dim,), jnp.float32), w1_l=w1_l, b1_l=b1_l, w2_l=w2_l, b2_l=b2_l, gamma_h=jnp.ones((dim,), jnp.float32), w1_h=w1_h, b1_h=b1_h, w2_h=w2_h, b2_h=b2_h)
    _L0_ffn_all = _L0_ffn_setup()
    _L0_ffn_in = {k: v for k, v in _L0_ffn_all.items() if k in ('routing_token', 'gamma_l', 'w1_l', 'b1_l', 'w2_l', 'b2_l', 'gamma_h', 'w1_h', 'b1_h', 'w2_h', 'b2_h')}
    del _L0_ffn_all

    def _L1_xattn_setup():
        import jax, jax.numpy as jnp
        import numpy as np
        DIM = 128
        HEADS = 16
        DIM_HEAD = 64
        INNER = HEADS * DIM_HEAD
        EPS = 1e-05

        def _split_heads(t):
            b, n, _ = t.shape
            return t.reshape(b, n, HEADS, DIM_HEAD).transpose(0, 2, 1, 3)
        key = jax.random.key(seed)
        ks = jax.random.split(key, 9)
        b, n, m = (2, 256, 32)
        s = DIM ** (-0.5)
        return {'x': jax.random.normal(ks[0], (b, n, DIM), jnp.float32), 'memories': jax.random.normal(ks[1], (b, m, DIM), jnp.float32), 'ln_g': jnp.ones((DIM,), jnp.float32), 'ln_b': jnp.zeros((DIM,), jnp.float32), 'Wq': jax.random.normal(ks[2], (DIM, INNER), jnp.float32) * s, 'Wkv': jax.random.normal(ks[3], (DIM, 2 * INNER), jnp.float32) * s, 'Wm': jax.random.normal(ks[4], (DIM, INNER), jnp.float32) * s, 'Wo': jax.random.normal(ks[5], (INNER, DIM), jnp.float32) * s, 'bo': jnp.zeros((DIM,), jnp.float32)}
    _L1_xattn_all = _L1_xattn_setup()
    _L1_xattn_in = {k: v for k, v in _L1_xattn_all.items() if k in ('ln_g', 'ln_b', 'Wq', 'Wkv', 'Wm', 'Wo', 'bo')}
    del _L1_xattn_all

    def _L1_ffn_setup():
        import jax, jax.numpy as jnp
        import numpy as np
        B, N, D = (4, 1024, 128)
        HEADS, DH = (8, 64)
        HID = HEADS * DH
        WIN = 128
        NQ, NKV = (128, 256)
        EPS, N_ITERS, FETCH_K = (1.0, 50, 9.0 / 8.0)
        SCALE = DH ** (-0.5)

        def rmsnorm(x, gamma):
            norm = jnp.maximum(jnp.linalg.norm(x, axis=-1, keepdims=True), 1e-12)
            return x / norm * x.shape[-1] ** 0.5 * gamma

        def coor_descent(s, k):
            logk = jnp.log(jnp.asarray(k, s.dtype))

            def body(_, ab):
                a, b = ab
                a = EPS * (logk - jax.nn.logsumexp((s + b) / EPS, axis=-1, keepdims=True))
                b = -jax.nn.relu(s + a)
                return (a, b)
            a, b = jax.lax.fori_loop(0, N_ITERS, body, (jnp.zeros_like(s[..., :1]), -s))
            return jnp.exp((s + a + b) / EPS)

        def route(x, routing_token, num_tokens):
            s = jnp.einsum('bnd,d->bn', x, routing_token)
            k = min(num_tokens * FETCH_K, x.shape[1])
            scores = coor_descent(s, k)
            sel_scores, sel_idx = jax.lax.top_k(scores, num_tokens)
            sel_scores = sel_scores + jax.lax.stop_gradient(1.0 - sel_scores)
            return (sel_scores, sel_idx)

        def light_local_attn(x, gamma, wq, wkv, wo):
            b, n, d = x.shape
            xn = rmsnorm(x, gamma)
            q = xn @ wq
            k, v = jnp.split(xn @ wkv, 2, axis=-1)

            def win(t):
                return t.reshape(b, n // WIN, WIN, HEADS, DH).transpose(0, 1, 3, 2, 4)
            q, k, v = (win(q) * SCALE, win(k), win(v))
            attn = jax.nn.softmax(jnp.einsum('bwhid,bwhjd->bwhij', q, k), axis=-1)
            out = jnp.einsum('bwhij,bwhjd->bwhid', attn, v)
            out = out.transpose(0, 1, 3, 2, 4).reshape(b, n, HID)
            return out @ wo

        def heavy_attn(xq, context, scores_kv, gamma, wq, wkv_t, wo):
            b, nq, d = xq.shape
            nkv = context.shape[1]
            xqn = rmsnorm(xq, gamma)
            ctx = rmsnorm(context, gamma)[:, None]
            q = (xqn @ wq).reshape(b, nq, HEADS, DH).transpose(0, 2, 1, 3) * SCALE
            kvw = wkv_t.reshape(1, HEADS, 2 * DH, d)
            kv = jnp.einsum('rhdi,brni->brhnd', kvw, ctx)
            k, v = jnp.split(kv, 2, axis=-1)
            v = v * scores_kv[:, None, None, :, None]
            k = k.reshape(b, HEADS, nkv, DH)
            v = v.reshape(b, HEADS, nkv, DH)
            attn = jax.nn.softmax(jnp.einsum('bhid,bhjd->bhij', q, k), axis=-1)
            out = jnp.einsum('bhij,bhjd->bhid', attn, v)
            out = out.transpose(0, 2, 1, 3).reshape(b, nq, HID)
            return out @ wo
        key = jax.random.key(seed)
        ks = jax.random.split(key, 10)
        lin = lambda k, shape, fan: jax.random.normal(k, shape, jnp.float32) * fan ** (-0.5)
        return dict(x=jax.random.normal(ks[0], (B, N, D), jnp.float32), gamma_light=jnp.ones((D,), jnp.float32), wq_light=lin(ks[1], (D, HID), D), wkv_light=lin(ks[2], (D, 2 * HID), D), wo_light=lin(ks[3], (HID, D), HID), q_routing_token=jax.random.normal(ks[4], (D,), jnp.float32), kv_routing_token=jax.random.normal(ks[5], (D,), jnp.float32), gamma_heavy=jnp.ones((D,), jnp.float32), wq_heavy=lin(ks[6], (D, HID), D), wkv_heavy=lin(ks[7], (2 * HID, D), D), wo_heavy=lin(ks[8], (HID, D), HID))
    _L1_ffn_all = _L1_ffn_setup()
    _L1_ffn_in = {k: v for k, v in _L1_ffn_all.items() if k in ('gamma_light', 'wq_light', 'wkv_light', 'wo_light', 'q_routing_token', 'kv_routing_token', 'gamma_heavy', 'wq_heavy', 'wkv_heavy', 'wo_heavy')}
    del _L1_ffn_all

    def _L2_xattn_setup():
        import jax, jax.numpy as jnp
        import numpy as np
        DIM = 128
        NUM_HEADS = 16
        HEAD_DIM = DIM // NUM_HEADS
        SCALE = HEAD_DIM ** (-0.5)
        key = jax.random.key(seed)
        ks = jax.random.split(key, 13)
        B, L, S = (2, 256, 256)
        inp = {'query': jax.random.normal(ks[0], (B, L, DIM), jnp.float32), 'key': jax.random.normal(ks[1], (B, S, DIM), jnp.float32), 'value': jax.random.normal(ks[2], (B, S, DIM), jnp.float32), 'mask': jax.random.randint(ks[3], (B, 1, L, S), 0, 2, jnp.int32), 'attn_bias': jax.random.normal(ks[4], (B, NUM_HEADS, L, S), jnp.float32), 'Wq': jax.random.normal(ks[5], (DIM, DIM), jnp.float32) * DIM ** (-0.5), 'bq': jax.random.normal(ks[6], (DIM,), jnp.float32) * 0.02, 'Wk': jax.random.normal(ks[7], (DIM, DIM), jnp.float32) * DIM ** (-0.5), 'bk': jax.random.normal(ks[8], (DIM,), jnp.float32) * 0.02, 'Wv': jax.random.normal(ks[9], (DIM, DIM), jnp.float32) * DIM ** (-0.5), 'bv': jax.random.normal(ks[10], (DIM,), jnp.float32) * 0.02, 'Wo': jax.random.normal(ks[11], (DIM, DIM), jnp.float32) * DIM ** (-0.5), 'bo': jax.random.normal(ks[12], (DIM,), jnp.float32) * 0.02}
        return inp
    _L2_xattn_all = _L2_xattn_setup()
    _L2_xattn_in = {k: v for k, v in _L2_xattn_all.items() if k in ('Wq', 'bq', 'Wk', 'bk', 'Wv', 'bv', 'Wo', 'bo')}
    del _L2_xattn_all

    def _L2_ffn_setup():
        import jax, jax.numpy as jnp
        import numpy as np
        B, S, H = (2, 128, 128)
        E, F = (8, 512)
        GATE_TEMP = 0.1
        key = jax.random.key(seed)
        ks = jax.random.split(key, 6)
        s_h = 1.0 / np.sqrt(H)
        s_f = 1.0 / np.sqrt(F)
        return {'hidden_states': jax.random.normal(ks[0], (B, S, H), dtype=jnp.float32), 'w_router': jax.random.normal(ks[1], (H, E), dtype=jnp.float32) * s_h, 'w_gating': jax.random.normal(ks[2], (H, E), dtype=jnp.float32) * s_h, 'w_gate': jax.random.normal(ks[3], (E, H, F), dtype=jnp.float32) * s_h, 'w_up': jax.random.normal(ks[4], (E, H, F), dtype=jnp.float32) * s_h, 'w_down': jax.random.normal(ks[5], (E, F, H), dtype=jnp.float32) * s_f}
    _L2_ffn_all = _L2_ffn_setup()
    _L2_ffn_in = {k: v for k, v in _L2_ffn_all.items() if k in ('w_router', 'w_gating', 'w_gate', 'w_up', 'w_down')}
    del _L2_ffn_all

    def _L3_xattn_setup():
        import jax, jax.numpy as jnp
        import numpy as np
        EMBED_DIM = 128
        NUM_HEADS = 16
        HEAD_DIM = EMBED_DIM // NUM_HEADS
        key = jax.random.key(seed)
        ks = jax.random.split(key, 12)
        B, S, D = (4, 256, EMBED_DIM)
        scale = 1.0 / np.sqrt(D)
        inp = {'query': jax.random.normal(ks[0], (B, S, D), jnp.float32), 'key': jax.random.normal(ks[1], (B, S, D), jnp.float32), 'value': jax.random.normal(ks[2], (B, S, D), jnp.float32), 'Wq': jax.random.normal(ks[3], (D, D), jnp.float32) * scale, 'bq': jnp.zeros((D,), jnp.float32), 'Wk': jax.random.normal(ks[4], (D, D), jnp.float32) * scale, 'bk': jnp.zeros((D,), jnp.float32), 'Wv': jax.random.normal(ks[5], (D, D), jnp.float32) * scale, 'bv': jnp.zeros((D,), jnp.float32), 'Wo': jax.random.normal(ks[6], (D, D), jnp.float32) * scale, 'bo': jnp.zeros((D,), jnp.float32)}
        return inp
    _L3_xattn_all = _L3_xattn_setup()
    _L3_xattn_in = {k: v for k, v in _L3_xattn_all.items() if k in ('Wq', 'bq', 'Wk', 'bk', 'Wv', 'bv', 'Wo', 'bo')}
    del _L3_xattn_all

    def _L3_ffn_setup():
        import jax, jax.numpy as jnp
        import numpy as np
        D_MODEL = 128
        FFN = 512
        N_EXPERTS = 8
        TOPK = 2
        B, L = (4, 256)

        def _moe(x, gate_w, gate_b, w1, b1, w2, b2):
            bs, l, d = x.shape
            T = bs * l
            xf = x.reshape(T, d)
            logits = xf @ gate_w + gate_b
            top_vals, top_idx = jax.lax.top_k(logits, TOPK)
            rows = jnp.arange(T)[:, None]
            sparse = jnp.full_like(logits, -jnp.inf).at[rows, top_idx].set(top_vals)
            gates = jax.nn.softmax(sparse, axis=-1)
            out = jnp.zeros_like(xf)
            for e in range(N_EXPERTS):
                h = jax.nn.gelu(xf @ w1[e] + b1[e], approximate=False)
                y = h @ w2[e] + b2[e]
                out = out + gates[:, e:e + 1] * y
            return out.reshape(bs, l, d)
        key = jax.random.key(seed)
        ks = jax.random.split(key, 8)
        s_in = 1.0 / np.sqrt(D_MODEL)
        s_ffn = 1.0 / np.sqrt(FFN)
        x = jax.random.normal(ks[0], (B, L, D_MODEL), dtype=jnp.float32)
        gate_w = jax.random.uniform(ks[1], (D_MODEL, N_EXPERTS), jnp.float32, -s_in, s_in)
        gate_b = jax.random.uniform(ks[2], (N_EXPERTS,), jnp.float32, -s_in, s_in)
        w1 = jax.random.uniform(ks[3], (N_EXPERTS, D_MODEL, FFN), jnp.float32, -s_in, s_in)
        b1 = jax.random.uniform(ks[4], (N_EXPERTS, FFN), jnp.float32, -s_in, s_in)
        w2 = jax.random.uniform(ks[5], (N_EXPERTS, FFN, D_MODEL), jnp.float32, -s_ffn, s_ffn)
        b2 = jax.random.uniform(ks[6], (N_EXPERTS, D_MODEL), jnp.float32, -s_ffn, s_ffn)
        return {'x': x, 'gate_w': gate_w, 'gate_b': gate_b, 'w1': w1, 'b1': b1, 'w2': w2, 'b2': b2}
    _L3_ffn_all = _L3_ffn_setup()
    _L3_ffn_in = {k: v for k, v in _L3_ffn_all.items() if k in ('gate_w', 'gate_b', 'w1', 'b1', 'w2', 'b2')}
    del _L3_ffn_all
    return {'x': x, 'ctx_1024': ctx_1024, 'fside_Bx16xSxS2_0': fside_Bx16xSxS2_0, 'mask_Bx1xSxS2_ik1': mask_Bx1xSxS2_ik1, 'g_xattn': g_xattn, 'g_ffn': g_ffn, 'L0_xattn_Wq': _L0_xattn_in['Wq'], 'L0_xattn_Wk': _L0_xattn_in['Wk'], 'L0_xattn_Wv': _L0_xattn_in['Wv'], 'L0_xattn_Wo': _L0_xattn_in['Wo'], 'L0_xattn_W1': _L0_xattn_in['W1'], 'L0_xattn_b1': _L0_xattn_in['b1'], 'L0_xattn_W2': _L0_xattn_in['W2'], 'L0_xattn_b2': _L0_xattn_in['b2'], 'L0_xattn_g1': _L0_xattn_in['g1'], 'L0_xattn_be1': _L0_xattn_in['be1'], 'L0_xattn_g2': _L0_xattn_in['g2'], 'L0_xattn_be2': _L0_xattn_in['be2'], 'L0_ffn_routing_token': _L0_ffn_in['routing_token'], 'L0_ffn_gamma_l': _L0_ffn_in['gamma_l'], 'L0_ffn_w1_l': _L0_ffn_in['w1_l'], 'L0_ffn_b1_l': _L0_ffn_in['b1_l'], 'L0_ffn_w2_l': _L0_ffn_in['w2_l'], 'L0_ffn_b2_l': _L0_ffn_in['b2_l'], 'L0_ffn_gamma_h': _L0_ffn_in['gamma_h'], 'L0_ffn_w1_h': _L0_ffn_in['w1_h'], 'L0_ffn_b1_h': _L0_ffn_in['b1_h'], 'L0_ffn_w2_h': _L0_ffn_in['w2_h'], 'L0_ffn_b2_h': _L0_ffn_in['b2_h'], 'L1_xattn_ln_g': _L1_xattn_in['ln_g'], 'L1_xattn_ln_b': _L1_xattn_in['ln_b'], 'L1_xattn_Wq': _L1_xattn_in['Wq'], 'L1_xattn_Wkv': _L1_xattn_in['Wkv'], 'L1_xattn_Wm': _L1_xattn_in['Wm'], 'L1_xattn_Wo': _L1_xattn_in['Wo'], 'L1_xattn_bo': _L1_xattn_in['bo'], 'L1_ffn_gamma_light': _L1_ffn_in['gamma_light'], 'L1_ffn_wq_light': _L1_ffn_in['wq_light'], 'L1_ffn_wkv_light': _L1_ffn_in['wkv_light'], 'L1_ffn_wo_light': _L1_ffn_in['wo_light'], 'L1_ffn_q_routing_token': _L1_ffn_in['q_routing_token'], 'L1_ffn_kv_routing_token': _L1_ffn_in['kv_routing_token'], 'L1_ffn_gamma_heavy': _L1_ffn_in['gamma_heavy'], 'L1_ffn_wq_heavy': _L1_ffn_in['wq_heavy'], 'L1_ffn_wkv_heavy': _L1_ffn_in['wkv_heavy'], 'L1_ffn_wo_heavy': _L1_ffn_in['wo_heavy'], 'L2_xattn_Wq': _L2_xattn_in['Wq'], 'L2_xattn_bq': _L2_xattn_in['bq'], 'L2_xattn_Wk': _L2_xattn_in['Wk'], 'L2_xattn_bk': _L2_xattn_in['bk'], 'L2_xattn_Wv': _L2_xattn_in['Wv'], 'L2_xattn_bv': _L2_xattn_in['bv'], 'L2_xattn_Wo': _L2_xattn_in['Wo'], 'L2_xattn_bo': _L2_xattn_in['bo'], 'L2_ffn_w_router': _L2_ffn_in['w_router'], 'L2_ffn_w_gating': _L2_ffn_in['w_gating'], 'L2_ffn_w_gate': _L2_ffn_in['w_gate'], 'L2_ffn_w_up': _L2_ffn_in['w_up'], 'L2_ffn_w_down': _L2_ffn_in['w_down'], 'L3_xattn_Wq': _L3_xattn_in['Wq'], 'L3_xattn_bq': _L3_xattn_in['bq'], 'L3_xattn_Wk': _L3_xattn_in['Wk'], 'L3_xattn_bk': _L3_xattn_in['bk'], 'L3_xattn_Wv': _L3_xattn_in['Wv'], 'L3_xattn_bv': _L3_xattn_in['bv'], 'L3_xattn_Wo': _L3_xattn_in['Wo'], 'L3_xattn_bo': _L3_xattn_in['bo'], 'L3_ffn_gate_w': _L3_ffn_in['gate_w'], 'L3_ffn_gate_b': _L3_ffn_in['gate_b'], 'L3_ffn_w1': _L3_ffn_in['w1'], 'L3_ffn_b1': _L3_ffn_in['b1'], 'L3_ffn_w2': _L3_ffn_in['w2'], 'L3_ffn_b2': _L3_ffn_in['b2']}

def reference(x, ctx_1024, fside_Bx16xSxS2_0, mask_Bx1xSxS2_ik1, g_xattn, g_ffn, L0_xattn_Wq, L0_xattn_Wk, L0_xattn_Wv, L0_xattn_Wo, L0_xattn_W1, L0_xattn_b1, L0_xattn_W2, L0_xattn_b2, L0_xattn_g1, L0_xattn_be1, L0_xattn_g2, L0_xattn_be2, L0_ffn_routing_token, L0_ffn_gamma_l, L0_ffn_w1_l, L0_ffn_b1_l, L0_ffn_w2_l, L0_ffn_b2_l, L0_ffn_gamma_h, L0_ffn_w1_h, L0_ffn_b1_h, L0_ffn_w2_h, L0_ffn_b2_h, L1_xattn_ln_g, L1_xattn_ln_b, L1_xattn_Wq, L1_xattn_Wkv, L1_xattn_Wm, L1_xattn_Wo, L1_xattn_bo, L1_ffn_gamma_light, L1_ffn_wq_light, L1_ffn_wkv_light, L1_ffn_wo_light, L1_ffn_q_routing_token, L1_ffn_kv_routing_token, L1_ffn_gamma_heavy, L1_ffn_wq_heavy, L1_ffn_wkv_heavy, L1_ffn_wo_heavy, L2_xattn_Wq, L2_xattn_bq, L2_xattn_Wk, L2_xattn_bk, L2_xattn_Wv, L2_xattn_bv, L2_xattn_Wo, L2_xattn_bo, L2_ffn_w_router, L2_ffn_w_gating, L2_ffn_w_gate, L2_ffn_w_up, L2_ffn_w_down, L3_xattn_Wq, L3_xattn_bq, L3_xattn_Wk, L3_xattn_bk, L3_xattn_Wv, L3_xattn_bv, L3_xattn_Wo, L3_xattn_bo, L3_ffn_gate_w, L3_ffn_gate_b, L3_ffn_w1, L3_ffn_b1, L3_ffn_w2, L3_ffn_b2):
    import jax
    import jax.numpy as jnp

    def _L0_xattn_ref(x_q, x_kv, bias, Wq, Wk, Wv, Wo, W1, b1, W2, b2, g1, be1, g2, be2):
        import jax, jax.numpy as jnp
        import numpy as np
        import math
        H = 16
        D = 128
        FF = 512
        DK = D // H
        EPS = 1e-05

        def layer_norm(x, g, b):
            mu = jnp.mean(x, axis=-1, keepdims=True)
            var = jnp.var(x, axis=-1, keepdims=True)
            return (x - mu) * jax.lax.rsqrt(var + EPS) * g + b
        B, S, _ = x_q.shape

        def split(x):
            return x.reshape(B, -1, H, DK).transpose(0, 2, 1, 3)
        q = split(x_q @ Wq.T)
        k = split(x_kv @ Wk.T)
        v = split(x_kv @ Wv.T)
        scores = jnp.einsum('bhqd,bhkd->bhqk', q, k) / math.sqrt(DK) + bias
        p = jax.nn.softmax(scores, axis=-1)
        o = jnp.einsum('bhqk,bhkd->bhqd', p, v)
        o = o.transpose(0, 2, 1, 3).reshape(B, S, D)
        x = x_q + o @ Wo.T
        h = jax.nn.gelu(layer_norm(x, g1, be1) @ W1.T + b1, approximate=False)
        x = x + h @ W2.T + b2
        return layer_norm(x, g2, be2)

    def _L0_ffn_ref(x, routing_token, gamma_l, w1_l, b1_l, w2_l, b2_l, gamma_h, w1_h, b1_h, w2_h, b2_h):
        import jax, jax.numpy as jnp
        import numpy as np
        NUM_HEAVY = 128
        N_ITERS = 50
        FETCH_K_RATIO = 9.0 / 8.0
        EPS = 1.0

        def rmsnorm(x, gamma):
            scale = gamma.shape[0] ** 0.5
            normed = x / jnp.maximum(jnp.linalg.norm(x, axis=-1, keepdims=True), 1e-12)
            return normed * scale * gamma

        def feedforward(x, gamma, w1, b1, w2, b2):
            h = rmsnorm(x, gamma)
            h = jax.nn.gelu(h @ w1.T + b1, approximate=False)
            return h @ w2.T + b2

        def coor_descent(s, n_iters, k, eps):
            logk = jnp.log(jnp.asarray(k, s.dtype))
            a0 = jnp.zeros_like(s[..., :1])
            b0 = -s

            def body(carry, _):
                a, b = carry
                a = eps * (logk - jax.nn.logsumexp((s + b) / eps, axis=-1, keepdims=True))
                b = -jax.nn.relu(s + a)
                return ((a, b), None)
            (a, b), _ = jax.lax.scan(body, (a0, b0), None, length=n_iters)
            return jnp.exp((s + a + b) / eps)
        b, n, dim = x.shape
        light_out = feedforward(x, gamma_l, w1_l, b1_l, w2_l, b2_l)
        s = jnp.einsum('bnd,d->bn', x, routing_token)
        effective_k = min(NUM_HEAVY * FETCH_K_RATIO, n)
        scores = coor_descent(s, N_ITERS, effective_k, EPS)
        selected_scores, selected_indices = jax.lax.top_k(scores, NUM_HEAVY)
        selected_scores = selected_scores + jax.lax.stop_gradient(1.0 - selected_scores)
        routed = jnp.take_along_axis(x, selected_indices[..., None], axis=1)
        routed_out = feedforward(routed, gamma_h, w1_h, b1_h, w2_h, b2_h)
        routed_out = routed_out * selected_scores[..., None]
        batch_range = jnp.arange(b)[:, None]
        heavy_out = jnp.zeros_like(x).at[batch_range, selected_indices].set(routed_out)
        return light_out + heavy_out

    def _L1_xattn_ref(x, memories, ln_g, ln_b, Wq, Wkv, Wm, Wo, bo):
        import jax, jax.numpy as jnp
        import numpy as np
        DIM = 128
        HEADS = 16
        DIM_HEAD = 64
        INNER = HEADS * DIM_HEAD
        EPS = 1e-05

        def _split_heads(t):
            b, n, _ = t.shape
            return t.reshape(b, n, HEADS, DIM_HEAD).transpose(0, 2, 1, 3)
        mu = jnp.mean(x, axis=-1, keepdims=True)
        var = jnp.mean(jnp.square(x - mu), axis=-1, keepdims=True)
        xn = (x - mu) * jax.lax.rsqrt(var + EPS) * ln_g + ln_b
        q = _split_heads(xn @ Wq)
        kv = xn @ Wkv
        k = _split_heads(kv[..., :INNER])
        v = _split_heads(kv[..., INNER:])
        mem = _split_heads(memories @ Wm)
        k = jnp.concatenate([k, mem], axis=2)
        v = jnp.concatenate([v, mem], axis=2)
        scale = DIM_HEAD ** (-0.5)
        dots = jnp.einsum('bhid,bhjd->bhij', q, k) * scale
        attn = jax.nn.softmax(dots, axis=-1)
        out = jnp.einsum('bhij,bhjd->bhid', attn, v)
        b, h, n, d = out.shape
        out = out.transpose(0, 2, 1, 3).reshape(b, n, h * d)
        return out @ Wo + bo

    def _L1_ffn_ref(x, gamma_light, wq_light, wkv_light, wo_light, q_routing_token, kv_routing_token, gamma_heavy, wq_heavy, wkv_heavy, wo_heavy):
        import jax, jax.numpy as jnp
        import numpy as np
        B, N, D = (4, 1024, 128)
        HEADS, DH = (8, 64)
        HID = HEADS * DH
        WIN = 128
        NQ, NKV = (128, 256)
        EPS, N_ITERS, FETCH_K = (1.0, 50, 9.0 / 8.0)
        SCALE = DH ** (-0.5)

        def rmsnorm(x, gamma):
            norm = jnp.maximum(jnp.linalg.norm(x, axis=-1, keepdims=True), 1e-12)
            return x / norm * x.shape[-1] ** 0.5 * gamma

        def coor_descent(s, k):
            logk = jnp.log(jnp.asarray(k, s.dtype))

            def body(_, ab):
                a, b = ab
                a = EPS * (logk - jax.nn.logsumexp((s + b) / EPS, axis=-1, keepdims=True))
                b = -jax.nn.relu(s + a)
                return (a, b)
            a, b = jax.lax.fori_loop(0, N_ITERS, body, (jnp.zeros_like(s[..., :1]), -s))
            return jnp.exp((s + a + b) / EPS)

        def route(x, routing_token, num_tokens):
            s = jnp.einsum('bnd,d->bn', x, routing_token)
            k = min(num_tokens * FETCH_K, x.shape[1])
            scores = coor_descent(s, k)
            sel_scores, sel_idx = jax.lax.top_k(scores, num_tokens)
            sel_scores = sel_scores + jax.lax.stop_gradient(1.0 - sel_scores)
            return (sel_scores, sel_idx)

        def light_local_attn(x, gamma, wq, wkv, wo):
            b, n, d = x.shape
            xn = rmsnorm(x, gamma)
            q = xn @ wq
            k, v = jnp.split(xn @ wkv, 2, axis=-1)

            def win(t):
                return t.reshape(b, n // WIN, WIN, HEADS, DH).transpose(0, 1, 3, 2, 4)
            q, k, v = (win(q) * SCALE, win(k), win(v))
            attn = jax.nn.softmax(jnp.einsum('bwhid,bwhjd->bwhij', q, k), axis=-1)
            out = jnp.einsum('bwhij,bwhjd->bwhid', attn, v)
            out = out.transpose(0, 1, 3, 2, 4).reshape(b, n, HID)
            return out @ wo

        def heavy_attn(xq, context, scores_kv, gamma, wq, wkv_t, wo):
            b, nq, d = xq.shape
            nkv = context.shape[1]
            xqn = rmsnorm(xq, gamma)
            ctx = rmsnorm(context, gamma)[:, None]
            q = (xqn @ wq).reshape(b, nq, HEADS, DH).transpose(0, 2, 1, 3) * SCALE
            kvw = wkv_t.reshape(1, HEADS, 2 * DH, d)
            kv = jnp.einsum('rhdi,brni->brhnd', kvw, ctx)
            k, v = jnp.split(kv, 2, axis=-1)
            v = v * scores_kv[:, None, None, :, None]
            k = k.reshape(b, HEADS, nkv, DH)
            v = v.reshape(b, HEADS, nkv, DH)
            attn = jax.nn.softmax(jnp.einsum('bhid,bhjd->bhij', q, k), axis=-1)
            out = jnp.einsum('bhij,bhjd->bhid', attn, v)
            out = out.transpose(0, 2, 1, 3).reshape(b, nq, HID)
            return out @ wo
        b = x.shape[0]
        light_out = light_local_attn(x, gamma_light, wq_light, wkv_light, wo_light)
        scores_q, idx_q = route(x, q_routing_token, NQ)
        scores_kv, idx_kv = route(x, kv_routing_token, NKV)
        routed_q = jnp.take_along_axis(x, idx_q[..., None], axis=1)
        routed_kv = jnp.take_along_axis(x, idx_kv[..., None], axis=1)
        routed_out = heavy_attn(routed_q, routed_kv, scores_kv, gamma_heavy, wq_heavy, wkv_heavy, wo_heavy)
        routed_out = routed_out * scores_q[..., None]
        heavy_out = jnp.zeros_like(x).at[jnp.arange(b)[:, None], idx_q].set(routed_out)
        return light_out + heavy_out

    def _L2_xattn_ref(query, key, value, mask, attn_bias, Wq, bq, Wk, bk, Wv, bv, Wo, bo):
        import jax, jax.numpy as jnp
        import numpy as np
        DIM = 128
        NUM_HEADS = 16
        HEAD_DIM = DIM // NUM_HEADS
        SCALE = HEAD_DIM ** (-0.5)
        B, L, _ = query.shape
        S = key.shape[1]
        H, D = (NUM_HEADS, HEAD_DIM)
        q = (query @ Wq + bq).reshape(B, L, H, D).transpose(0, 2, 1, 3)
        k = (key @ Wk + bk).reshape(B, S, H, D).transpose(0, 2, 1, 3)
        v = (value @ Wv + bv).reshape(B, S, H, D).transpose(0, 2, 1, 3)
        scores = jnp.einsum('bhld,bhsd->bhls', q, k) * SCALE + attn_bias
        scores = jnp.where(mask == 0, -jnp.inf, scores)
        probs = jax.nn.softmax(scores, axis=-1)
        out = jnp.einsum('bhls,bhsd->bhld', probs, v)
        out = out.transpose(0, 2, 1, 3).reshape(B, L, DIM)
        return out @ Wo + bo

    def _L2_ffn_ref(hidden_states, w_router, w_gating, w_gate, w_up, w_down):
        import jax, jax.numpy as jnp
        import numpy as np
        B, S, H = (2, 128, 128)
        E, F = (8, 512)
        GATE_TEMP = 0.1
        x = hidden_states
        router_probs = jax.nn.softmax(jnp.einsum('bsh,he->bse', x, w_router), axis=-1)
        gate_weights = jax.nn.softmax(jnp.einsum('bsh,he->bse', x, w_gating) / GATE_TEMP, axis=-1)
        g = jnp.einsum('bsh,ehf->ebsf', x, w_gate)
        u = jnp.einsum('bsh,ehf->ebsf', x, w_up)
        h = jax.nn.silu(g) * u
        expert_out = jnp.einsum('ebsf,efh->ebsh', h, w_down)
        cw = router_probs * gate_weights
        cw = cw / (jnp.sum(cw, axis=-1, keepdims=True) + 1e-09)
        out = jnp.einsum('ebsh,bse->bsh', expert_out, cw)
        return out

    def _L3_xattn_ref(query, key, value, Wq, bq, Wk, bk, Wv, bv, Wo, bo):
        import jax, jax.numpy as jnp
        import numpy as np
        EMBED_DIM = 128
        NUM_HEADS = 16
        HEAD_DIM = EMBED_DIM // NUM_HEADS
        B, Sq, D = query.shape
        Sk = key.shape[1]
        H, Dh = (NUM_HEADS, HEAD_DIM)

        def proj(x, W, b):
            y = jnp.einsum('bsd,ed->bse', x, W) + b
            return y.reshape(x.shape[0], x.shape[1], H, Dh).transpose(0, 2, 1, 3)
        q = proj(query, Wq, bq)
        k = proj(key, Wk, bk)
        v = proj(value, Wv, bv)
        scores = jnp.einsum('bhqd,bhkd->bhqk', q, k) / jnp.sqrt(jnp.float32(Dh)).astype(q.dtype)
        attn = jax.nn.sigmoid(scores)
        out = jnp.einsum('bhqk,bhkd->bhqd', attn, v)
        out = out.transpose(0, 2, 1, 3).reshape(B, Sq, D)
        return jnp.einsum('bsd,ed->bse', out, Wo) + bo

    def _L3_ffn_ref(x, gate_w, gate_b, w1, b1, w2, b2):
        import jax, jax.numpy as jnp
        import numpy as np
        D_MODEL = 128
        FFN = 512
        N_EXPERTS = 8
        TOPK = 2
        B, L = (4, 256)

        def _moe(x, gate_w, gate_b, w1, b1, w2, b2):
            bs, l, d = x.shape
            T = bs * l
            xf = x.reshape(T, d)
            logits = xf @ gate_w + gate_b
            top_vals, top_idx = jax.lax.top_k(logits, TOPK)
            rows = jnp.arange(T)[:, None]
            sparse = jnp.full_like(logits, -jnp.inf).at[rows, top_idx].set(top_vals)
            gates = jax.nn.softmax(sparse, axis=-1)
            out = jnp.zeros_like(xf)
            for e in range(N_EXPERTS):
                h = jax.nn.gelu(xf @ w1[e] + b1[e], approximate=False)
                y = h @ w2[e] + b2[e]
                out = out + gates[:, e:e + 1] * y
            return out.reshape(bs, l, d)
        return _moe(x, gate_w, gate_b, w1, b1, w2, b2)
    x = x + jnp.tanh(g_xattn[0]) * _L0_xattn_ref(_layernorm(x, axis=-1), ctx_1024, fside_Bx16xSxS2_0, L0_xattn_Wq, L0_xattn_Wk, L0_xattn_Wv, L0_xattn_Wo, L0_xattn_W1, L0_xattn_b1, L0_xattn_W2, L0_xattn_b2, L0_xattn_g1, L0_xattn_be1, L0_xattn_g2, L0_xattn_be2)
    x = x + jnp.tanh(g_ffn[0]) * _L0_ffn_ref(_layernorm(x, axis=-1), L0_ffn_routing_token, L0_ffn_gamma_l, L0_ffn_w1_l, L0_ffn_b1_l, L0_ffn_w2_l, L0_ffn_b2_l, L0_ffn_gamma_h, L0_ffn_w1_h, L0_ffn_b1_h, L0_ffn_w2_h, L0_ffn_b2_h)
    x = x + jnp.tanh(g_xattn[1]) * _L1_xattn_ref(_layernorm(x, axis=-1), ctx_1024, L1_xattn_ln_g, L1_xattn_ln_b, L1_xattn_Wq, L1_xattn_Wkv, L1_xattn_Wm, L1_xattn_Wo, L1_xattn_bo)
    x = x + jnp.tanh(g_ffn[1]) * _L1_ffn_ref(_layernorm(x, axis=-1), L1_ffn_gamma_light, L1_ffn_wq_light, L1_ffn_wkv_light, L1_ffn_wo_light, L1_ffn_q_routing_token, L1_ffn_kv_routing_token, L1_ffn_gamma_heavy, L1_ffn_wq_heavy, L1_ffn_wkv_heavy, L1_ffn_wo_heavy)
    x = x + jnp.tanh(g_xattn[2]) * _L2_xattn_ref(_layernorm(x, axis=-1), ctx_1024, ctx_1024, mask_Bx1xSxS2_ik1, fside_Bx16xSxS2_0, L2_xattn_Wq, L2_xattn_bq, L2_xattn_Wk, L2_xattn_bk, L2_xattn_Wv, L2_xattn_bv, L2_xattn_Wo, L2_xattn_bo)
    x = x + jnp.tanh(g_ffn[2]) * _L2_ffn_ref(_layernorm(x, axis=-1), L2_ffn_w_router, L2_ffn_w_gating, L2_ffn_w_gate, L2_ffn_w_up, L2_ffn_w_down)
    x = x + jnp.tanh(g_xattn[3]) * _L3_xattn_ref(_layernorm(x, axis=-1), ctx_1024, ctx_1024, L3_xattn_Wq, L3_xattn_bq, L3_xattn_Wk, L3_xattn_bk, L3_xattn_Wv, L3_xattn_bv, L3_xattn_Wo, L3_xattn_bo)
    x = x + jnp.tanh(g_ffn[3]) * _L3_ffn_ref(_layernorm(x, axis=-1), L3_ffn_gate_w, L3_ffn_gate_b, L3_ffn_w1, L3_ffn_b1, L3_ffn_w2, L3_ffn_b2)
    return x

_drawn_inputs = setup_inputs


def setup_inputs(seed=0):
    import zlib

    import numpy as np

    out = dict(_drawn_inputs(seed))
    spreads = {'L0_xattn_b1': (0.0, 0.672),
     'L0_xattn_b2': (0.0, 0.382),
     'L0_xattn_g1': (1.0, 0.6),
     'L0_xattn_be1': (0.0, 0.679),
     'L0_xattn_g2': (1.0, 0.2),
     'L0_xattn_be2': (0.0, 0.279),
     'L0_ffn_gamma_l': (1.0, 0.6),
     'L0_ffn_gamma_h': (1.0, 0.6),
     'L1_xattn_ln_g': (1.0, 0.2),
     'L1_xattn_ln_b': (0.0, 0.1),
     'L1_xattn_bo': (0.0, 0.391),
     'L1_ffn_gamma_light': (1.0, 0.6),
     'L1_ffn_gamma_heavy': (1.0, 0.6),
     'L3_xattn_bq': (0.0, 0.1),
     'L3_xattn_bk': (0.0, 0.1),
     'L3_xattn_bv': (0.0, 0.1),
     'L3_xattn_bo': (0.0, 0.8)}
    factors = {'fside_Bx16xSxS2_0': 8.0,
     'g_ffn': 8.0,
     'L0_ffn_routing_token': 4.169,
     'L0_ffn_b1_l': 8.0,
     'L0_ffn_w1_h': 3.695,
     'L0_ffn_b1_h': 8.0,
     'L0_ffn_w2_h': 3.306,
     'L0_ffn_b2_h': 8.0,
     'L1_ffn_kv_routing_token': 7.473,
     'L1_ffn_wq_heavy': 5.83,
     'L2_xattn_bq': 42.471,
     'L2_xattn_bk': 64.0,
     'L2_xattn_bv': 8.0,
     'L2_xattn_bo': 8.0,
     'L2_ffn_w_router': 4.359,
     'L3_ffn_gate_w': 8.0,
     'L3_ffn_gate_b': 8.0,
     'L3_ffn_w1': 7.0,
     'L3_ffn_b1': 8.0,
     'L3_ffn_w2': 7.044,
     'L3_ffn_b2': 45.988}
    for name, (base, spread) in spreads.items():
        noise = np.random.default_rng([zlib.crc32(name.encode()), seed]).standard_normal(out[name].shape)
        drawn = base * np.exp(spread * noise) if base else spread * noise
        out[name] = jnp.asarray(drawn.astype(out[name].dtype))
    for name, factor in factors.items():
        out[name] = (out[name] * factor).astype(out[name].dtype)
    return out
```

```python
from contextlib import ExitStack, contextmanager

import numpy as np
import concourse.bass as bass
from concourse import mybir

F32 = mybir.dt.float32
I32 = mybir.dt.int32
U32 = mybir.dt.uint32
ALU = mybir.AluOpType
ACT = mybir.ActivationFunctionType
X = mybir.AxisListType.X
ds = bass.ds

P = 128
B = 4
S = 512
T = S // P
NT = B * T
D = 128
KC = 77
FF = 512
NF = FF // P
H = 16
DK = D // H
HH = H // 2
HK = HH * KC
NCH = -(-HK // P)
LASTR = HK - (NCH - 1) * P
DH = 64
NBLK = H * DH // P
HF = 8
NBF = HF * DH // P
NKEY = S + KC
NQ, NKV = 128, 256
E = 8
DESCENT = 50
EPS = 1e-5
MASKED = -3.0e38

COLS = [("L0_xattn_g1", 1), ("L0_xattn_be1", 1), ("L0_xattn_b1", 4), ("L0_ffn_gamma_l", 1), ("L0_ffn_gamma_h", 1),
        ("L0_ffn_b1_l", 1), ("L0_ffn_b1_h", 4), ("L1_xattn_ln_g", 1), ("L1_xattn_ln_b", 1), ("L1_ffn_gamma_light", 1),
        ("L1_ffn_gamma_heavy", 1), ("L2_xattn_bq", 1), ("L2_xattn_bk", 1), ("L3_xattn_bq", 1), ("L3_xattn_bk", 1),
        ("L0_ffn_routing_token", 1), ("L1_ffn_q_routing_token", 1), ("L1_ffn_kv_routing_token", 1)]
ROWS = [("L0_xattn_b2", 128), ("L0_xattn_g2", 128), ("L0_xattn_be2", 128), ("L0_ffn_b2_l", 128), ("L0_ffn_b2_h", 128),
        ("L1_xattn_bo", 128), ("L2_xattn_bv", 128), ("L2_xattn_bo", 128), ("L3_xattn_bv", 128), ("L3_xattn_bo", 128),
        ("L3_ffn_b2", 1024), ("L3_ffn_gate_b", 8), ("g_xattn", 4), ("g_ffn", 4)]
MATS = [("L0_xattn_Wq", 128), ("L0_xattn_Wk", 128), ("L0_xattn_Wv", 128), ("L0_xattn_Wo", 128), ("L0_xattn_W1", 512),
        ("L0_xattn_W2", 512), ("L0_ffn_w1_l", 64), ("L0_ffn_w2_l", 128), ("L0_ffn_w1_h", 512), ("L0_ffn_w2_h", 512),
        ("L1_xattn_Wq", 1024), ("L1_xattn_Wk", 1024), ("L1_xattn_Wv", 1024), ("L1_xattn_Wm", 1024),
        ("L1_xattn_Wo", 1024),
        ("L1_ffn_wq_light", 512), ("L1_ffn_wk_light", 512), ("L1_ffn_wv_light", 512), ("L1_ffn_wo_light", 512),
        ("L1_ffn_wq_heavy", 512), ("L1_ffn_wk_heavy", 512), ("L1_ffn_wv_heavy", 512), ("L1_ffn_wo_heavy", 512),
        ("L2_xattn_Wq", 128), ("L2_xattn_Wk", 128), ("L2_xattn_Wv", 128), ("L2_xattn_Wo", 128),
        ("L2_ffn_w_router", 8), ("L2_ffn_w_gating", 8),
        ("L3_xattn_Wq", 128), ("L3_xattn_Wk", 128), ("L3_xattn_Wv", 128), ("L3_xattn_Wo", 128), ("L3_ffn_gate_w", 8)]


def offsets(table):
    at, out = 0, {}
    for name, n in table:
        out[name] = (at, n)
        at += n
    return out, at


COL_AT, NCOL = offsets(COLS)
ROW_AT, NROW = offsets(ROWS)
MAT_AT, NMAT = offsets(MATS)
MAT_PARTS = [("L0_xattn_Wq", "L0_ffn_w1_l"), ("L0_ffn_w1_l", "L1_xattn_Wq"), ("L1_xattn_Wq", "L1_ffn_wq_light"),
             ("L1_ffn_wq_light", "L2_xattn_Wq"), ("L2_xattn_Wq", None)]


class Signal:

    def __init__(self, sem, per, ahead=0):
        self.sem, self.per, self.ahead = sem, per, ahead

    def at(self, turn, k):
        return turn * self.per + (k + self.ahead)


class Steps:

    def __init__(self, engine, sem):
        self.engine, self.sem, self.base, self.turn, self.per, self.k = engine, sem, 0, 0, 0, 0

    def mark(self, ins):
        ins.then_inc(self.sem, 1)
        self.k += 1

    def wait(self):
        self.engine.wait_ge(self.sem, self.turn * self.per + (self.base + self.k))

    def __call__(self, ins):
        self.mark(ins)
        self.wait()

    @contextmanager
    def loop(self, turns, per):
        self.base, self.k, self.per = self.base + self.k, 0, per
        with self.engine.Fori(0, turns) as turn:
            self.turn = turn
            yield turn
        assert self.k == per, f"the loop's steps: {self.k}, not {per}"
        self.base, self.k, self.turn, self.per = self.base + turns * per, 0, 0, 0


def flamingo_kernel(nc, ins, out, stages):
    ctx = ExitStack()

    def sb(name, shape, dt=F32):
        return ctx.enter_context(nc.sbuf_tensor(name, shape, dt))

    def sem(name):
        return ctx.enter_context(nc.semaphore(name))

    with ctx:
        mats = sb("mats", [P, NMAT])
        cols = sb("cols", [P, NCOL])
        rows = sb("rows", [P, NROW])
        ctxT = sb("ctxT", [P, B, KC])
        ident = sb("ident", [P, P])
        head_of_row = sb("head_of_row", [P, H])
        head_of_key = sb("head_of_key", [P, NCH, HH])
        earlier = sb("earlier", [P, T, S])
        slot_no = sb("slot_no", [P, NKV])
        expo = sb("expo", [P, NT])
        row_of = sb("row_of", [2 * B, 2 * B, P])
        tokens = sb("tokens", [P, 3, B, 2 * B])
        pick = sb("pick", [P, 8])
        tg = sb("tg", [P, 8])

        x = sb("x", [P, NT, D])
        xn = sb("xn", [P, NT, D])
        xnT = sb("xnT", [P, NT * P])
        rn = sb("rn", [P, NT, D])
        stat = sb("stat", [P, NT, 6])
        mv = sb("mv", [P, NT, 2])
        varr = sb("varr", [P, NT])
        rstd = sb("rstd", [P, NT])
        x_in = sb("x_in", [P, S])
        junk = sb("junk", [P, S])
        spare = sb("spare", [P, 2])
        work = sb("work", [P, 21504])
        psum = ctx.enter_context(nc.psum_tensor("psum", [P, 8 * 512], F32))

        def bank(i, n=1):
            return psum[:, 512 * i:512 * (i + n)]

        def carve(sizes):
            at, out = 0, {}
            for name, n in sizes.items():
                out[name] = work[:, at:at + n]
                at += n
            assert at <= 21504, at
            return out

        def col(name, i=0, n=P):
            return cols[0:n, COL_AT[name][0] + i:COL_AT[name][0] + i + 1]

        def row(name, i=0, n=D, parts=P):
            return rows[0:parts, ROW_AT[name][0] + i:ROW_AT[name][0] + i + n]

        def mat(name, i=0, n=P, parts=P):
            return mats[0:parts, MAT_AT[name][0] + i:MAT_AT[name][0] + i + n]

        dve_step, act_step, pool_step = sem("dve_step"), sem("act_step"), sem("pool_step")
        x_loaded, small_loaded = sem("x_loaded"), sem("small_loaded")
        mats_loaded = [sem(f"mats_loaded{i}") for i in range(len(MAT_PARTS))]
        consts_ready, gates_ready = sem("consts_ready"), sem("gates_ready")
        turn_done = sem("turn_done")
        var_ready, rstd_ready = sem("var_ready"), sem("rstd_ready")
        xn_ready, rn_ready = sem("xn_ready"), sem("rn_ready")
        xn_turned, xnT_ready = sem("xn_turned"), sem("xnT_ready")
        stored = sem("stored")

        CONSTS = 9
        LAYERS = [("norm", 0), ("small", 0), ("norm", 1), ("route0", 0), ("norm", 2), ("self", 0), ("norm", 3),
                  ("route1", 0), ("norm", 4), ("small", 1), ("norm", 5), ("moe2", 0), ("norm", 6), ("small", 2),
                  ("norm", 7), ("moe3", 0)][:2 * stages]
        TURNS = {"norm": 0, "small": B, "route0": B, "self": B, "route1": B, "moe2": 1, "moe3": 1}
        RMS = (1, 3)
        TWICE = 2

        def before(kind_counts, call):
            return sum(kind_counts(c) for c in range(call))

        n_rstd = lambda c: 2 if c in RMS or c == TWICE else 1
        n_turn = lambda c: 2 * B if c in RMS else B

        xnT_count = lambda call: before(n_turn, call + 1)

        def norm_vector(dve, step, call, done):
            dve.wait_ge(turn_done, done)
            if call == 0:
                dve.wait_ge(x_loaded, 16)
            rounds = before(n_rstd, call)
            for again in range(2 if call == TWICE else 1):
                src = xn if again else x
                with step.loop(B, T) as b:
                    for t in range(T):
                        step.mark(dve.bn_stats(stat[:, ds(b * T + t, 1), :], src[:, ds(b * T + t, 1), :]))
                step.wait()
                for t in range(NT):
                    ins_ = dve.bn_aggr(mv[:, t, :], stat[:, t, :])
                step(ins_)
                dve.tensor_scalar(varr[:, :], mv[:, :, 1], EPS, None, ALU.add).then_inc(var_ready, 1)
                rounds += 1
                dve.wait_ge(rstd_ready, rounds)
                with step.loop(B, T) as b:
                    for t in range(T):
                        step.mark(dve.tensor_scalar(
                            xn[:, ds(b * T + t, 1), :], src[:, ds(b * T + t, 1), :], mv[:, ds(b * T + t, 1), 0],
                            rstd[:, ds(b * T + t, 1)], ALU.subtract, ALU.mult))
                step.wait()
            dve.sem_inc(xn_ready, 1)
            if call in RMS:
                with step.loop(B, T) as b:
                    for t in range(T):
                        ins = dve.scalar_tensor_tensor(
                            out=junk[:, t * P:t * P + P], in0=xn[:, ds(b * T + t, 1), :], scalar=1.0,
                            in1=xn[:, ds(b * T + t, 1), :], op0=ALU.mult, op1=ALU.mult,
                            accum_out=mv[:, ds(b * T + t, 1), 0])
                        step.mark(ins)
                    step.wait()
                dve.tensor_scalar(varr[:, :], mv[:, :, 0], 1e-24, 1.0 / D, ALU.max, ALU.mult).then_inc(var_ready, 1)
                rounds += 1
                dve.wait_ge(rstd_ready, rounds)
                with step.loop(B, T) as b:
                    for t in range(T):
                        step.mark(dve.tensor_scalar(
                            rn[:, ds(b * T + t, 1), :], xn[:, ds(b * T + t, 1), :], rstd[:, ds(b * T + t, 1)], None,
                            ALU.mult))
                step.wait()
                dve.sem_inc(rn_ready, 1)

        def norm_pool(pool, step, call, done):
            rounds = before(n_rstd, call)
            if call == 0:
                pool.wait_ge(consts_ready, CONSTS)
            for _ in range(n_rstd(call)):
                rounds += 1
                pool.wait_ge(var_ready, rounds)
                pool.tensor_tensor(rstd[:, :], varr[:, :], expo[:, :], ALU.pow).then_inc(rstd_ready, 1)

        def turn_batch(pe, src, b, turned):
            if turned >= 2:
                pe.wait_ge(xnT_ready, turned - 1)
            for t in range(T):
                ins = pe.transpose(bank(turned % 2)[:, t * P:t * P + P], src[:, b * T + t, :], ident[:, :])
            ins.then_inc(xn_turned, 1)

        def norm_tensor(pe, call, done):
            pe.wait_ge(turn_done, done)
            if call == 0:
                pe.wait_ge(consts_ready, CONSTS)
            turned = before(n_turn, call)
            pe.wait_ge(xn_ready, call + 1)
            for b in range(B):
                turn_batch(pe, xn, b, turned + b)
            if call in RMS:
                which = 0 if call == RMS[0] else 1
                pe.wait_ge(xnT_ready, turned + B)
                kinds = (0,) if which == 0 else (1, 2)
                n = 0
                for kind in kinds:
                    for b in range(B):
                        ins = pe.matmul(bank(2)[0:2 * B, :], tokens[:, kind, b, :], xnT[:, b * S:b * S + S],
                                        start=(n == 0), stop=(n == len(kinds) * B - 1))
                        n += 1
                ins.then_inc(logits_ready, 1)
                pe.wait_ge(rn_ready, which + 1)
                for b in range(B):
                    turn_batch(pe, rn, b, turned + B + b)

        def norm_scalar(act, step, call, done):
            turned = before(n_turn, call)
            act.wait_ge(turn_done, done)
            for b in range(B):
                act.wait_ge(xn_turned, turned + b + 1)
                src, dst = bank((turned + b) % 2), xnT[:, b * S:b * S + S]
                if call == TWICE:
                    ins = act.activation(dst, src, ACT.Identity, bias=col("L1_xattn_ln_b"), scale=col("L1_xattn_ln_g"))
                else:
                    ins = act.copy(dst, src)
                ins.then_inc(xnT_ready, 1)
            if call in RMS:
                which = 0 if call == RMS[0] else 1
                act.wait_ge(logits_ready, which + 1)
                gain = col("L0_ffn_gamma_l" if which == 0 else "L1_ffn_gamma_light")
                for b in range(B):
                    act.wait_ge(xn_turned, turned + B + b + 1)
                    act.mul(xnT[:, b * S:b * S + S], bank((turned + B + b) % 2), gain).then_inc(xnT_ready, 1)

        logits_ready = sem("logits_ready")

        sw = carve({"kT": KC, "Kbd": H * KC, "ctx8": HK, "vs": NCH * D, "Vbd": 2 * NCH * HH * 9, "qT": S,
                    "bias": 2 * H * KC, "mask": 2 * KC, "maskf": 2 * KC, "sc": 2 * HK, "mx": 2 * HH, "pr": 2 * HK,
                    "pT": 2 * NCH * P, 
                    "rec": 2 * HH, "o": T * D, "oT": S, "x1": S, "y": S, "yT": S, "h": NF * S})
        Kbd = sw["Kbd"].rearrange("p (h k) -> p h k", h=H)
        ctx8 = sw["ctx8"].rearrange("p (h k) -> p h k", h=HH)
        vs = sw["vs"].rearrange("p (c d) -> p c d", c=NCH)
        Vbd = sw["Vbd"].rearrange("p (f c h e) -> p f c h e", f=2, c=NCH, h=HH)
        qT_s = sw["qT"]
        bias_s = sw["bias"].rearrange("p (n h k) -> p n h k", n=2, h=H)
        mask_s = sw["mask"].rearrange("p (n k) -> p n k", n=2)
        maskf = sw["maskf"].rearrange("p (n k) -> p n k", n=2)
        sc_s = sw["sc"].rearrange("p (n h k) -> p n h k", n=2, h=HH)
        mx_s = sw["mx"].rearrange("p (n h) -> p n h", n=2)
        pr_s = sw["pr"].rearrange("p (n k) -> p n k", n=2)
        pT_s = sw["pT"].rearrange("p (n k) -> p n k", n=2)
        rec_s = sw["rec"].rearrange("p (n h) -> p n h", n=2)
        o_s = sw["o"].rearrange("p (n d) -> p n d", n=T)
        sigT = work[:, 12000:12000 + 2 * NCH * S].rearrange("p (u q) -> p u q", u=2 * NCH)
        x1 = sw["x1"].rearrange("p (t d) -> p t d", t=T)
        y_s = sw["y"].rearrange("p (t d) -> p t d", t=T)
        h_s = sw["h"].rearrange("p (f q) -> p f q", f=NF)
        U = 2 * T

        bias_in = [Signal(sem(f"bias_in{i}"), 2 * 16) for i in range(2)]
        mask_in = [Signal(sem(f"mask_in{i}"), 2 * 16) for i in range(2)]
        ctx_here = Signal(sem("ctx_here"), 1)
        kv_proj = Signal(sem("kv_proj"), 1)
        kv_ready = Signal(sem("kv_ready"), 1)
        masked = Signal(sem("masked"), T)
        s_scores = Signal(sem("s_scores"), U)
        s_read = Signal(sem("s_read"), U)
        s_shift = Signal(sem("s_shift"), U)
        s_probs = Signal(sem("s_probs"), U)
        s_turned = Signal(sem("s_turned"), U)
        s_pT = Signal(sem("s_pT"), U)
        s_av = Signal(sem("s_av"), U)
        s_o = Signal(sem("s_o"), U)
        s_oturn = Signal(sem("s_oturn"), 1)
        s_oT = Signal(sem("s_oT"), 1)
        s_out = Signal(sem("s_out"), 1)
        g_scores = Signal(sem("g_scores"), 2 * NCH)
        g_sig = Signal(sem("g_sig"), 2 * NCH)
        f_x1, f_var, f_rstd = Signal(sem("f_x1"), 1), Signal(sem("f_var"), 2), Signal(sem("f_rstd"), 2)
        f_y, f_turn, f_yT = Signal(sem("f_y"), 1), Signal(sem("f_turn"), 1), Signal(sem("f_yT"), 1)
        f_h, f_gelu, f_out = Signal(sem("f_h"), NF), Signal(sem("f_gelu"), NF), Signal(sem("f_out"), 1)

        SMALL = ["L0_xattn", "L2_xattn", "L3_xattn"]
        NB = (0, 1)
        rows_of = [P] * (NCH - 1) + [LASTR]

        def small_sync(sp, use, done):
            if use not in NB:
                return
            sp.wait_ge(turn_done, done)
            with sp.Fori(0, B) as b:
                g = b + use * B
                for t in range(T):
                    if t >= 2:
                        sp.wait_ge(s_read.sem, s_read.at(g, 2 * (t - 1)))
                    elif t == 0:
                        sp.wait_ge(turn_done, b + done)
                    sp.dma_start(bias_s[:, t % 2], ins["bias"][ds(b * T + t, 1)].rearrange(
                        "a p (h k) -> p (a h) k", h=H)).then_inc(bias_in[t % 2].sem, 16)
                    if use == 1:
                        sp.dma_start(mask_s[:, t % 2].bitcast(I32), ins["mask"][ds(b * T + t, 1)].rearrange(
                            "a p k -> p (a k)")).then_inc(mask_in[t % 2].sem, 16)

        def small_pool(pool, step, use, done):
            per = 2 + T if use == 1 else 2
            pool.wait_ge(turn_done, done)
            pool.memset(sw["vs"], 0.0).then_inc(ones_set, 1)
            for half in range(2):
                step(pool.tensor_copy(Vbd[:, half, :, :, 8:9], head_of_key[:, :, :].unsqueeze(3)))
            pool.sem_inc(ones_set, 1)
            with step.loop(B, per - 2) as b:
                g = b + use * B
                pool.wait_ge(turn_done, b + done)
                pool.tensor_copy(ctx8, ctxT[:, ds(b, 1), :].to_broadcast([P, HH, KC])).then_inc(ctx_here.sem, 1)
                if use == 0:
                    for k in (1, 2):
                        pool.wait_ge(f_var.sem, f_var.at(b, k))
                        pool.tensor_tensor(rstd[:, 0:T], varr[:, 0:T], expo[:, 0:T], ALU.pow).then_inc(f_rstd.sem, 1)
                if use == 1:
                    for t in range(T):
                        pool.wait_ge(mask_in[t % 2].sem, mask_in[t % 2].at(b, 16 * (t // 2 + 1)))
                        pool.sem_inc(mask_seen, 1)
                        step(pool.tensor_scalar(maskf[:, t % 2], mask_s[:, t % 2].bitcast(I32), 0, MASKED,
                                                ALU.is_equal, ALU.mult))
                        pool.wait_ge(bias_in[t % 2].sem, bias_in[t % 2].at(g, 16 * (t // 2 + 1)))
                        pool.tensor_tensor(bias_s[:, t % 2], bias_s[:, t % 2],
                                           maskf[:, t % 2].unsqueeze(1).to_broadcast([P, H, KC]), ALU.add)\
                            .then_inc(masked.sem, 1)

        ones_set = sem("ones_set")
        mask_seen = sem("mask_seen")

        def small_tensor(pe, use, done):
            name = SMALL[use]
            if use == 0:
                pe.wait_ge(mats_loaded[0], 16)
                pe.wait_ge(small_loaded, 48)
            if use == 1:
                pe.wait_ge(mats_loaded[4], 16)
            pe.wait_ge(xnT_ready, xnT_count([0, 4, 6][use]))

            def scores(g, u):
                t, half = divmod(u, 2)
                if u >= 2:
                    pe.wait_ge(s_read.sem, s_read.at(g, u - 1))
                for j in range(2):
                    ins_ = pe.matmul(bank(2 * (u % 2) + j)[:, 0:4 * KC], qT_s[:, t * P:t * P + P],
                                     Kbd[:, half * HH + 4 * j:half * HH + 4 * j + 4, :], start=True, stop=True)
                ins_.then_inc(s_scores.sem, 1)

            def turn_probs(g, u):
                pe.wait_ge(s_probs.sem, s_probs.at(g, u + 1))
                if u >= 1:
                    pe.wait_ge(s_pT.sem, s_pT.at(g, u))
                for c, n in enumerate(rows_of):
                    to = bank(4)[:, c * P:c * P + P] if c < 4 else bank(5)[0:n, 0:P]
                    ins_ = pe.transpose(to, pr_s[:, u % 2, c * P:c * P + n], ident[:, :])
                ins_.then_inc(s_turned.sem, 1)

            def av(g, u):
                t, half = divmod(u, 2)
                if use in NB:
                    pe.wait_ge(s_pT.sem, s_pT.at(g, u + 1))
                if u >= 2:
                    pe.wait_ge(s_o.sem, s_o.at(g, u - 1))
                for c, n in enumerate(rows_of):
                    lhsT = pT_s[0:n, u % 2, c * P:c * P + P] if use in NB \
                        else sigT[0:n, half * NCH + c, t * P:t * P + P]
                    ins_ = pe.matmul(bank(6 + u % 2)[:, 0:72], lhsT, Vbd[0:n, half, c, :, :],
                                     start=(c == 0), stop=(c == NCH - 1))
                ins_.then_inc(s_av.sem, 1)

            def turn_o(g):
                pe.wait_ge(s_o.sem, s_o.at(g, U))
                for t in range(T):
                    ins_ = pe.transpose(bank(1)[:, t * P:t * P + P], o_s[:, t, :], ident[:, :])
                ins_.then_inc(s_oturn.sem, 1)

            with pe.Fori(0, B) as b:
                g = b + use * B
                pe.wait_ge(turn_done, b + done)
                pe.wait_ge(ctx_here.sem, ctx_here.at(g, 1))
                pe.matmul(bank(0)[:, 0:KC], mat(name + "_Wk"), ctxT[:, ds(b, 1), :], start=True, stop=True)
                for c, n in enumerate(rows_of):
                    to = bank(1)[:, c * P:c * P + P] if c < 4 else bank(2)[0:n, 0:P]
                    pe.matmul(to, sw["ctx8"][:, c * P:c * P + n], mat(name + "_Wv"), start=True, stop=True)
                pe.matmul(bank(3), mat(name + "_Wq"), xnT[:, ds(b * S, S)], start=True, stop=True).then_inc(kv_proj.sem, 1)
                pe.wait_ge(kv_ready.sem, kv_ready.at(g, 1))
                if use in NB:
                    for u in range(U + 2):
                        if u < U:
                            scores(g, u)
                        if u >= 2:
                            av(g, u - 2)
                        if 1 <= u <= U:
                            turn_probs(g, u - 1)
                else:
                    for u in range(2 * NCH):
                        half, c = divmod(u, NCH)
                        if u >= 4:
                            pe.wait_ge(g_sig.sem, g_sig.at(b, u - 3))
                        flat = Kbd[:, half * HH:half * HH + HH, :].rearrange("p h k -> p (h k)")
                        pe.matmul(bank(u % 4)[0:rows_of[c], :], flat[:, c * P:c * P + rows_of[c]], qT_s,
                                  start=True, stop=True).then_inc(g_scores.sem, 1)
                    for t in range(T):
                        for half in range(2):
                            pe.wait_ge(g_sig.sem, g_sig.at(b, NCH * (half + 1)))
                            av(g, 2 * t + half)
                turn_o(g)
                pe.wait_ge(s_oT.sem, s_oT.at(g, 1))
                for t in range(T):
                    ins_ = pe.matmul(bank(0)[:, t * P:t * P + P], sw["oT"][:, t * P:t * P + P], mat(name + "_Wo"),
                                     start=True, stop=True)
                ins_.then_inc(s_out.sem, 1)
                if use == 0:
                    pe.wait_ge(f_y.sem, f_y.at(b, 1))
                    for t in range(T):
                        ins_ = pe.transpose(bank(1)[:, t * P:t * P + P], y_s[:, t, :], ident[:, :])
                    ins_.then_inc(f_turn.sem, 1)
                    pe.wait_ge(f_yT.sem, f_yT.at(b, 1))
                    for f in range(NF):
                        pe.matmul(bank(2 + f), mat("L0_xattn_W1", f * P), sw["yT"], start=True, stop=True)\
                            .then_inc(f_h.sem, 1)
                    pe.wait_ge(f_gelu.sem, f_gelu.at(b, NF))
                    for t in range(T):
                        for f in range(NF):
                            ins_ = pe.matmul(bank(6)[:, t * P:t * P + P], h_s[:, f, t * P:t * P + P],
                                             mat("L0_xattn_W2", f * P), start=(f == 0), stop=(f == NF - 1))
                    ins_.then_inc(f_out.sem, 1)

        def small_scalar(act, step, use, done):
            def probs(g, u):
                act.wait_ge(s_shift.sem, s_shift.at(g, u + 1))
                if u >= 2:
                    act.wait_ge(s_turned.sem, s_turned.at(g, u - 1))
                act.activation(pr_s[:, u % 2], sc_s[:, u % 2], ACT.Exp).then_inc(s_probs.sem, 1)

            def copy_pT(g, u):
                act.wait_ge(s_turned.sem, s_turned.at(g, u + 1))
                if u >= 2:
                    act.wait_ge(s_av.sem, s_av.at(g, u - 1))
                act.copy(pT_s[:, u % 2, 0:4 * P], bank(4))
                act.copy(pT_s[0:LASTR, u % 2, 4 * P:5 * P], bank(5)[0:LASTR, 0:P])\
                    .then_inc(s_pT.sem, 1)


            with act.Fori(0, B) as b:
                g = b + use * B
                act.wait_ge(turn_done, b + done)
                if use in NB:
                    for u in range(U + 1):
                        if u < U:
                            probs(g, u)
                        if u >= 1:
                            copy_pT(g, u - 1)
                else:
                    for u in range(2 * NCH):
                        n = rows_of[u % NCH]
                        act.wait_ge(g_scores.sem, g_scores.at(b, u + 1))
                        act.activation(sigT[0:n, u, :], bank(u % 4)[0:n, :], ACT.Sigmoid).then_inc(g_sig.sem, 1)
                act.wait_ge(s_oturn.sem, s_oturn.at(g, 1))
                act.copy(sw["oT"], bank(1)).then_inc(s_oT.sem, 1)
                if use == 0:
                    for f in range(NF):
                        act.wait_ge(f_h.sem, f_h.at(b, f + 1))
                        act.activation(h_s[:, f, :], bank(2 + f), ACT.Gelu, bias=col("L0_xattn_b1", f))\
                            .then_inc(f_gelu.sem, 1)

        def small_vector(dve, step, use, done):
            name = SMALL[use]
            if use == 0:
                dve.wait_ge(small_loaded, 48)
            dve.wait_ge(ones_set, 2 * (use + 1))

            def shift(g, u):
                t, half = divmod(u, 2)
                dve.wait_ge(s_scores.sem, s_scores.at(g, u + 1))
                if use == 0:
                    dve.wait_ge(bias_in[t % 2].sem, bias_in[t % 2].at(g, 16 * (t // 2 + 1)))
                else:
                    dve.wait_ge(masked.sem, masked.at(g - B, t + 1))
                if u >= 2:
                    dve.wait_ge(s_probs.sem, s_probs.at(g, u - 1))
                two = bank(2 * (u % 2), 2).rearrange("p (j n) -> p j n", j=2)[:, :, 0:4 * KC]
                dve.tensor_tensor(sc_s[:, u % 2].rearrange("p (j h) k -> p j (h k)", j=2), two,
                                  bias_s[:, t % 2, half * HH:half * HH + HH].rearrange("p (j h) k -> p j (h k)", j=2),
                                  ALU.add).then_inc(s_read.sem, 1)
                dve.wait_ge(s_read.sem, s_read.at(g, u + 1))
                step(dve.tensor_reduce(mx_s[:, u % 2], sc_s[:, u % 2], X, ALU.max))
                dve.tensor_tensor(sc_s[:, u % 2], sc_s[:, u % 2], mx_s[:, u % 2].unsqueeze(2).to_broadcast([P, HH, KC]),
                                  ALU.subtract).then_inc(s_shift.sem, 1)

            def norm_o(g, u):
                t, half = divmod(u, 2)
                o9 = bank(6 + u % 2)[:, 0:72].rearrange("p (h e) -> p h e", e=9)
                dve.wait_ge(s_av.sem, s_av.at(g, u + 1))
                dst = o_s[:, t, half * 64:half * 64 + 64].rearrange("p (h e) -> p h e", e=DK)
                if use in NB:
                    step(dve.reciprocal(rec_s[:, u % 2].unsqueeze(2), o9[:, :, 8:9]))
                    dve.tensor_tensor(dst, o9[:, :, 0:8], rec_s[:, u % 2].unsqueeze(2).to_broadcast([P, HH, DK]),
                                      ALU.mult).then_inc(s_o.sem, 1)
                else:
                    dve.tensor_copy(dst, o9[:, :, 0:8]).then_inc(s_o.sem, 1)

            def token_norm(src, dst, b, k):
                for t in range(T):
                    step.mark(dve.bn_stats(stat[:, t, :], src[:, t, :]))
                step.wait()
                dve.memset(spare[:, :], 0.0)
                for t in range(T):
                    step.mark(dve.bn_aggr(mv[:, t, :], stat[:, t, :]))
                step.wait()
                dve.tensor_scalar(varr[:, 0:T], mv[:, 0:T, 1], EPS, None, ALU.add).then_inc(f_var.sem, 1)
                dve.wait_ge(f_rstd.sem, f_rstd.at(b, k))
                for t in range(T):
                    step.mark(dve.tensor_scalar(dst[:, t, :], src[:, t, :], mv[:, t, 0:1], rstd[:, t:t + 1],
                                                ALU.subtract, ALU.mult))
                step.wait()

            per = {0: 3 + 2 * U + 29, 1: 3 + 2 * U + 1, 2: 3 + 1}[use]
            with step.loop(B, per) as b:
                g = b + use * B
                dve.wait_ge(turn_done, b + done)
                dve.wait_ge(kv_proj.sem, kv_proj.at(g, 1))
                if use == 0:
                    step(dve.tensor_copy(sw["kT"], bank(0)[:, 0:KC]))
                    step(dve.tensor_copy(vs[:, 0:4, :], bank(1).rearrange("p (c d) -> p c d", c=4)))
                    step(dve.tensor_copy(vs[0:LASTR, 4, :], bank(2)[0:LASTR, 0:P]))
                    dve.tensor_scalar(qT_s, bank(3), float(DK) ** -0.5, None, ALU.mult)
                else:
                    bq = col(name + "_bq")
                    bv = row(name + "_bv")
                    step(dve.tensor_scalar(sw["kT"], bank(0)[:, 0:KC], col(name + "_bk"), None, ALU.add))
                    step(dve.tensor_tensor(vs[:, 0:4, :], bank(1).rearrange("p (c d) -> p c d", c=4),
                                           bv.unsqueeze(1).to_broadcast([P, 4, D]), ALU.add))
                    step(dve.tensor_tensor(vs[0:LASTR, 4, :], bank(2)[0:LASTR, 0:P], bv[0:LASTR], ALU.add))
                    dve.tensor_scalar(qT_s, bank(3), bq, float(DK) ** -0.5, ALU.add, ALU.mult)
                dve.tensor_tensor(Kbd, sw["kT"].unsqueeze(1).to_broadcast([P, H, KC]),
                                  head_of_row[:, :].unsqueeze(2).to_broadcast([P, H, KC]), ALU.mult)
                for half in range(2):
                    last = dve.tensor_tensor(
                        Vbd[:, half, :, :, 0:8],
                        vs[:, :, half * 64:half * 64 + 64].rearrange("p c (h e) -> p c h e", e=DK),
                        head_of_key[:, :, :].unsqueeze(3).to_broadcast([P, NCH, HH, DK]), ALU.mult)
                last.then_inc(kv_ready.sem, 1)
                if use in NB:
                    for u in range(U + 2):
                        if u < U:
                            shift(g, u)
                        if u >= 2:
                            norm_o(g, u - 2)
                else:
                    for u in range(U):
                        norm_o(g, u)
                dve.wait_ge(s_out.sem, s_out.at(g, 1))
                out4 = bank(0).rearrange("p (t d) -> p t d", t=T)
                xb = x[:, ds(b * T, T), :]
                if use > 0:
                    step(dve.tensor_tensor(x1, out4, row(name + "_bo").unsqueeze(1).to_broadcast([P, T, D]), ALU.add))
                    dve.scalar_tensor_tensor(out=xb, in0=x1, scalar=tg[:, use + 1:use + 2], in1=xb, op0=ALU.mult,
                                             op1=ALU.add).then_inc(turn_done, 1)
                else:
                    step(dve.tensor_tensor(x1, out4, xn[:, ds(b * T, T), :], ALU.add))
                    token_norm(x1, y_s, b, 1)
                    dve.sem_inc(f_y.sem, 1)
                    dve.wait_ge(f_turn.sem, f_turn.at(b, 1))
                    dve.tensor_scalar(sw["yT"], bank(1), col("L0_xattn_g1"), col("L0_xattn_be1"), ALU.mult, ALU.add)\
                        .then_inc(f_yT.sem, 1)
                    dve.wait_ge(f_out.sem, f_out.at(b, 1))
                    step(dve.tensor_tensor(x1, bank(6).rearrange("p (t d) -> p t d", t=T), x1, ALU.add))
                    step(dve.tensor_tensor(x1, x1, row("L0_xattn_b2").unsqueeze(1).to_broadcast([P, T, D]), ALU.add))
                    token_norm(x1, y_s, b, 2)
                    step(dve.tensor_tensor(y_s, y_s, row("L0_xattn_g2").unsqueeze(1).to_broadcast([P, T, D]), ALU.mult))
                    step(dve.tensor_tensor(y_s, y_s, row("L0_xattn_be2").unsqueeze(1).to_broadcast([P, T, D]), ALU.add))
                    dve.scalar_tensor_tensor(out=xb, in0=y_s, scalar=tg[:, 0:1], in1=xb, op0=ALU.mult,
                                             op1=ALU.add).then_inc(turn_done, 1)

        ROUND, ROUNDS = 12, 4
        assert 2 + ROUND * ROUNDS == DESCENT
        R8 = 2 * B
        K_OF = [(NQ * 9 / 8, NQ * 9 / 8), (NQ * 9 / 8, NKV * 9 / 8)]
        k_inv = sb("k_inv", [R8, 2, S])
        k_log = sb("k_log", [R8, 2])
        k_col = sb("k_col", [R8, 2])
        d_s, d_e = sb("d_s", [R8, S]), sb("d_e", [R8, S])
        d_sum = sb("d_sum", [R8, 2])
        d_c, d_m, d_ln = sb("d_c", [R8, 1]), sb("d_m", [R8, 1]), sb("d_ln", [R8, 1])
        col_s = sb("col_s", [P, T, R8])
        col_w = sb("col_w", [P, T, R8])
        d_arg = Signal(sem("d_arg"), ROUNDS + 2)
        d_exp = Signal(sem("d_exp"), ROUNDS + 2)
        d_total = Signal(sem("d_total"), ROUNDS + 1)
        d_log = Signal(sem("d_log"), ROUNDS + 1)
        c_turned, c_read = sem("c_turned"), sem("c_read")
        b_spread, b_read = sem("b_spread"), sem("b_read")

        def descent_vector(dve, step, which, bc, nrow):
            k1 = lambda: k_inv[:, which, :]
            dve.wait_ge(logits_ready, which + 1)
            step(dve.tensor_copy(d_s[:, :], bank(2)[0:R8, :]))
            step(dve.tensor_scalar(d_c[:, :], k_log[:, which:which + 1], -1.0, float(np.log(S)), ALU.mult, ALU.add))
            step(dve.tensor_scalar(d_e[:, :], d_s[:, :], d_c[:, :], None, ALU.min))
            step(dve.tensor_reduce(d_m[:, :], d_e[:, :], X, ALU.max))
            dve.tensor_scalar(d_e[:, :], d_e[:, :], d_m[:, :], None, ALU.subtract).then_inc(d_arg.sem, 1)
            dve.wait_ge(d_exp.sem, d_exp.at(which, 1))
            dve.tensor_reduce(d_sum[:, 0:1], d_e[:, :], X, ALU.add).then_inc(d_total.sem, 1)
            dve.wait_ge(d_log.sem, d_log.at(which, 1))
            step(dve.tensor_tensor(d_c[:, :], d_m[:, :], d_ln[:, :], ALU.add))
            with step.loop(ROUNDS, ROUND + 2) as r:
                step(dve.tensor_scalar(d_e[:, :], d_s[:, :], d_c[:, :], 60.0, ALU.subtract, ALU.min))
                dve.sem_inc(d_arg.sem, 1)
                dve.wait_ge(d_exp.sem, r + d_exp.at(which, 2))
                total = k_col[:, which:which + 1]
                for i in range(ROUND):
                    nxt = d_sum[:, i % 2:i % 2 + 1]
                    step(dve.scalar_tensor_tensor(out=junk[0:R8, :], in0=d_e[:, :], scalar=total, in1=k1(),
                                                  op0=ALU.min, op1=ALU.mult, accum_out=nxt))
                    total = nxt
                dve.sem_inc(d_total.sem, 1)
                dve.wait_ge(d_log.sem, r + d_log.at(which, 2))
                step(dve.tensor_tensor(d_c[:, :], d_c[:, :], d_ln[:, :], ALU.add))
            dve.tensor_scalar(d_e[:, :], d_s[:, :], d_c[:, :], 0.0, ALU.subtract, ALU.min).then_inc(d_arg.sem, 1)
            dve.wait_ge(c_turned, which + 1)
            dve.tensor_copy(col_s[:, :, :], bank(3)[:, 0:T * R8].rearrange("p (t r) -> p t r", t=T)).then_inc(c_read, 1)
            dve.wait_ge(c_read, which + 1)
            step(dve.tensor_scalar(col_w[:, :, :], col_s[:, :, :], -1.0, 1.0, ALU.mult, ALU.add))
            dve.tensor_tensor(col_w[:, :, :], col_w[:, :, :], col_s[:, :, :], ALU.add).then_inc(w_ready, 1)
            for r in range(nrow):
                dve.wait_ge(b_spread, which * B + r + 1)
                ins_ = dve.tensor_copy(bc[:, r, :], bank(4 + r % 2))
                ins_.then_inc(b_read, 1)
            dve.wait_ge(b_read, which * B + nrow)

        w_ready = sem("w_ready")

        def descent_scalar(act, which):
            def exp(value, wait, **kw):
                act.wait_ge(d_arg.sem, wait)
                act.activation(value, d_e[:, :], ACT.Exp, **kw).then_inc(d_exp.sem, 1)

            def log(wait, i):
                act.wait_ge(d_total.sem, wait)
                act.activation(d_ln[:, :], d_sum[:, i:i + 1], ACT.Ln, scale=k_inv[:, which, 0:1]).then_inc(d_log.sem, 1)

            exp(d_e[:, :], d_arg.at(which, 1))
            log(d_total.at(which, 1), 0)
            with act.Fori(0, ROUNDS) as r:
                exp(d_e[:, :], r + d_arg.at(which, 2), bias=k_log[:, which:which + 1])
                log(r + d_total.at(which, 2), (ROUND - 1) % 2)
            exp(d_e[:, :], d_arg.at(which, ROUNDS + 2))

        def descent_tensor(pe, which, nrow):
            pe.wait_ge(d_exp.sem, d_exp.at(which, ROUNDS + 2))
            for t in range(T):
                ins_ = pe.transpose(bank(3)[:, t * R8:t * R8 + R8], d_e[:, t * P:t * P + P], ident[0:R8, 0:R8])
            ins_.then_inc(c_turned, 1)
            for r in range(nrow):
                if r >= 2:
                    pe.wait_ge(b_read, which * B + r - 1)
                pe.matmul(bank(4 + r % 2), row_of[:, r, :], d_e[:, :], start=True, stop=True).then_inc(b_spread, 1)

        def rank_and_place(dve, step, bc, r, place, n):
            for t in range(T):
                score = col_s[:, t, ds(r, 1)]
                step(dve.tensor_scalar(junk[:, :], bc[:, ds(r, 1), :], score, 0.0, ALU.is_gt, ALU.add,
                                            accum_out=over[:, t:t + 1]))
                step(dve.scalar_tensor_tensor(out=junk[:, :], in0=bc[:, ds(r, 1), :], scalar=score,
                                                   in1=earlier[:, t, :], op0=ALU.is_equal, op1=ALU.mult,
                                                   accum_out=ties[:, t:t + 1]))
            step(dve.tensor_tensor(over[:, :], over[:, :], ties[:, :], ALU.add))
            for t in range(T):
                step.mark(dve.tensor_scalar(place[:, t, :], slot_no[:, 0:n], over[:, t:t + 1], None, ALU.is_equal))
            step.wait()

        RANK_STEPS = 3 * T + 1
        over, ties = sb("over", [P, T]), sb("ties", [P, T])

        rw = carve({"bc": B * S, "place": T * NQ, "rn": T * D, "w": T, "ws": 1, "xg": NQ, "placeT": T * P, "hl": S,
                    "hh": NF * NQ, "routed": D, "sum": T * D})
        bc0 = rw["bc"].rearrange("p (r q) -> p r q", r=B)
        place0 = rw["place"].rearrange("p (t i) -> p t i", t=T)
        rn0 = rw["rn"].rearrange("p (t d) -> p t d", t=T)
        hh = rw["hh"].rearrange("p (f i) -> p f i", f=NF)
        sum0 = rw["sum"].rearrange("p (t d) -> p t d", t=T)
        r_copied = Signal(sem("r_copied"), 1)
        r_placed = Signal(sem("r_placed"), 1)
        r_gath = Signal(sem("r_gath"), 1)
        r_light = Signal(sem("r_light"), 1)
        r_lgelu = Signal(sem("r_lgelu"), 1)
        r_xg = Signal(sem("r_xg"), 1)
        r_h = Signal(sem("r_h"), 1)
        r_hgelu = Signal(sem("r_hgelu"), 1)
        r_heavy = Signal(sem("r_heavy"), 1)
        r_routed = Signal(sem("r_routed"), 1)
        r_out = Signal(sem("r_out"), 1)

        def route0_pool(pool, step, use, done):
            pool.wait_ge(w_ready, 1)
            with pool.Fori(0, B) as b:
                pool.wait_ge(turn_done, b + done)
                pool.tensor_copy(rn0, rn[:, ds(b * T, T), :])
                pool.tensor_copy(rw["w"].unsqueeze(2), col_w[:, :, ds(b, 1)]).then_inc(r_copied.sem, 1)

        def route0_tensor(pe, use, done):
            pe.wait_ge(mats_loaded[1], 16)
            descent_tensor(pe, 0, B)
            pe.wait_ge(xnT_ready, xnT_count(1))
            pe.wait_ge(b_read, B)
            with pe.Fori(0, B) as b:
                pe.wait_ge(turn_done, b + done)
                pe.matmul(bank(3)[0:64, :], mat("L0_ffn_w1_l", 0, 64), xnT[:, ds(b * S, S)], start=True, stop=True)\
                    .then_inc(r_light.sem, 1)
                pe.wait_ge(r_copied.sem, r_copied.at(b, 1))
                pe.wait_ge(r_placed.sem, r_placed.at(b, 1))
                for t in range(T):
                    pe.matmul(bank(0)[:, 0:NQ], rn0[:, t, :], place0[:, t, :], start=(t == 0), stop=(t == T - 1))
                for t in range(T):
                    pe.matmul(bank(1)[:, 0:1], place0[:, t, :], rw["w"][:, t:t + 1], start=(t == 0), stop=(t == T - 1))
                for t in range(T):
                    ins_ = pe.transpose(bank(2)[:, t * P:t * P + P], place0[:, t, :], ident[:, :])
                ins_.then_inc(r_gath.sem, 1)
                pe.wait_ge(r_xg.sem, r_xg.at(b, 1))
                for f in range(NF):
                    ins_ = pe.matmul(bank(4)[:, f * P:f * P + P], mat("L0_ffn_w1_h", f * P), rw["xg"],
                                     start=True, stop=True)
                ins_.then_inc(r_h.sem, 1)
                pe.wait_ge(r_hgelu.sem, r_hgelu.at(b, 1))
                for f in range(NF):
                    ins_ = pe.matmul(bank(5)[:, 0:D], hh[:, f, :], mat("L0_ffn_w2_h", f * P),
                                     start=(f == 0), stop=(f == NF - 1))
                ins_.then_inc(r_heavy.sem, 1)
                pe.wait_ge(r_lgelu.sem, r_lgelu.at(b, 1))
                pe.wait_ge(r_routed.sem, r_routed.at(b, 1))
                for t in range(T):
                    pe.matmul(bank(6)[:, t * P:t * P + P], rw["hl"][0:64, t * P:t * P + P],
                              mat("L0_ffn_w2_l", 0, D, 64), start=True, stop=False)
                    ins_ = pe.matmul(bank(6)[:, t * P:t * P + P], rw["placeT"][:, t * P:t * P + P], rw["routed"],
                                     start=False, stop=True)
                ins_.then_inc(r_out.sem, 1)

        def route0_scalar(act, step, use, done):
            descent_scalar(act, 0)
            with act.Fori(0, B) as b:
                act.wait_ge(turn_done, b + done)
                act.wait_ge(r_gath.sem, r_gath.at(b, 1))
                act.mul(rw["xg"], bank(0)[:, 0:NQ], col("L0_ffn_gamma_h"))
                act.copy(rw["placeT"], bank(2)).then_inc(r_xg.sem, 1)
                act.wait_ge(r_light.sem, r_light.at(b, 1))
                act.activation(rw["hl"][0:64, :], bank(3)[0:64, :], ACT.Gelu, bias=col("L0_ffn_b1_l", 0, 64))\
                    .then_inc(r_lgelu.sem, 1)
                act.wait_ge(r_h.sem, r_h.at(b, 1))
                for f in range(NF):
                    ins_ = act.activation(hh[:, f, :], bank(4)[:, f * P:f * P + P], ACT.Gelu,
                                          bias=col("L0_ffn_b1_h", f))
                ins_.then_inc(r_hgelu.sem, 1)

        def route0_vector(dve, step, use, done):
            descent_vector(dve, step, 0, bc0, B)
            with step.loop(B, RANK_STEPS + 2) as b:
                dve.wait_ge(turn_done, b + done)
                rank_and_place(dve, step, bc0, b, place0, NQ)
                dve.sem_inc(r_placed.sem, 1)
                dve.wait_ge(r_gath.sem, r_gath.at(b, 1))
                dve.tensor_copy(rw["ws"], bank(1)[:, 0:1])
                dve.wait_ge(r_heavy.sem, r_heavy.at(b, 1))
                step(dve.tensor_tensor(rw["routed"], bank(5)[:, 0:D], row("L0_ffn_b2_h"), ALU.add))
                dve.tensor_scalar(rw["routed"], rw["routed"], rw["ws"], None, ALU.mult).then_inc(r_routed.sem, 1)
                dve.wait_ge(r_out.sem, r_out.at(b, 1))
                step(dve.tensor_tensor(sum0, bank(6).rearrange("p (t d) -> p t d", t=T),
                                       row("L0_ffn_b2_l").unsqueeze(1).to_broadcast([P, T, D]), ALU.add))
                xb = x[:, ds(b * T, T), :]
                dve.scalar_tensor_tensor(out=xb, in0=sum0, scalar=tg[:, 4:5], in1=xb, op0=ALU.mult, op1=ALU.add)\
                    .then_inc(turn_done, 1)

        aw = carve({"qT": NBLK * S, "kT": NBLK * NKEY, "v": 5 * H * DH, "ctx": KC, "pr": 2 * NKEY, "pT": 2 * 5 * P,
                    "nm": 4, "sums": T * H, "rec": 4, "o": T * H * DH, "sum": T * D})
        qT_a = aw["qT"].rearrange("p (i q) -> p i q", i=NBLK)
        kT_a = aw["kT"].rearrange("p (i k) -> p i k", i=NBLK)
        v_a = aw["v"].rearrange("p (c n) -> p c n", c=5)
        pr_a = aw["pr"].rearrange("p (n k) -> p n k", n=2)
        pT_a = aw["pT"].rearrange("p (n k) -> p n k", n=2)
        o_a = aw["o"].rearrange("p (t n) -> p t n", t=T)
        oT_a = qT_a
        sum_a = aw["sum"].rearrange("p (t d) -> p t d", t=T)
        ITEMS = [("q", i) for i in range(NBLK)] + [("k", i) for i in range(NBLK)] + [("km", 0), ("km", 1)] + \
                [("v", i) for i in range(2 * T)] + [("vm", 0), ("vm", 1)]
        HALF_ITEMS = len(ITEMS) // 2
        UA = T * H
        GA = UA // 4
        a_in = Signal(sem("a_in"), 1)
        a_proj = Signal(sem("a_proj"), len(ITEMS))
        a_even = Signal(sem("a_even"), HALF_ITEMS)
        a_odd = Signal(sem("a_odd"), HALF_ITEMS)
        a_scores = Signal(sem("a_scores"), UA)
        a_max = Signal(sem("a_max"), UA)
        a_probs = Signal(sem("a_probs"), UA)
        a_turned = Signal(sem("a_turned"), UA)
        a_pT = Signal(sem("a_pT"), UA)
        a_av = Signal(sem("a_av"), UA)
        a_o = Signal(sem("a_o"), GA)
        a_oturn = Signal(sem("a_oturn"), NBLK)
        a_oe = Signal(sem("a_oe"), NBLK // 2)
        a_oo = Signal(sem("a_oo"), NBLK // 2)
        a_out = Signal(sem("a_out"), 1)
        key_rows = [P] * T + [KC]

        def self_pool(pool, step, use, done):
            pool.wait_ge(xnT_ready, xnT_count(TWICE))
            with pool.Fori(0, B) as b:
                pool.wait_ge(turn_done, b + done)
                pool.tensor_copy(x_in[:, :], xnT[:, ds(b * S, S)])
                pool.tensor_copy(aw["ctx"].unsqueeze(1), ctxT[:, ds(b, 1), :]).then_inc(a_in.sem, 1)

        def item_place(kind, i, n):
            to = bank(n % 8)
            if kind == "q":
                return to, qT_a[:, i, :]
            if kind == "k":
                return to, kT_a[:, i, 0:S]
            if kind == "km":
                return to[:, 0:4 * KC].rearrange("p (j k) -> p j k", j=4), kT_a[:, 4 * i:4 * i + 4, S:NKEY]
            if kind == "v":
                return to, v_a[:, i // 2, (i % 2) * S:(i % 2) * S + S]
            return to[0:KC, :], v_a[0:KC, T, i * S:i * S + S]

        def self_tensor(pe, use, done):
            pe.wait_ge(mats_loaded[2], 16)

            def item(g, n):
                kind, i = ITEMS[n]
                to, _ = item_place(kind, i, n)
                if n >= 8:
                    s = (a_even, a_odd)[n % 2]
                    pe.wait_ge(s.sem, s.at(g, (n - 8) // 2 + 1))
                if kind in "qk":
                    ins_ = pe.matmul(to, mat("L1_xattn_W" + kind, i * P), x_in[:, :], start=True, stop=True)
                elif kind == "km":
                    for j in range(4):
                        ins_ = pe.matmul(to[:, j, :], mat("L1_xattn_Wm", (4 * i + j) * P), aw["ctx"],
                                         start=True, stop=True)
                elif kind == "v":
                    ins_ = pe.matmul(to, x_in[:, (i // 2) * P:(i // 2) * P + P], mat("L1_xattn_Wv", (i % 2) * S, S),
                                     start=True, stop=True)
                else:
                    ins_ = pe.matmul(to, aw["ctx"], mat("L1_xattn_Wm", i * S, S), start=True, stop=True)
                ins_.then_inc(a_proj.sem, 1)

            def scores(g, u):
                t, h = divmod(u, H)
                if u >= 2:
                    pe.wait_ge(a_probs.sem, a_probs.at(g, u - 1))
                at = slice(DH * (h % 2), DH * (h % 2) + DH)
                q = qT_a[at, h // 2, t * P:t * P + P]
                pe.matmul(bank(2 * (u % 2)), q, kT_a[at, h // 2, 0:S], start=True, stop=True)
                pe.matmul(bank(2 * (u % 2) + 1)[:, 0:KC], q, kT_a[at, h // 2, S:NKEY], start=True, stop=True)\
                    .then_inc(a_scores.sem, 1)

            def turn_probs(g, u):
                pe.wait_ge(a_probs.sem, a_probs.at(g, u + 1))
                if u >= 1:
                    pe.wait_ge(a_pT.sem, a_pT.at(g, u))
                for c, n in enumerate(key_rows):
                    to = bank(4)[:, c * P:c * P + P] if c < T else bank(5)[0:n, 0:P]
                    ins_ = pe.transpose(to, pr_a[:, u % 2, c * P:c * P + n], ident[:, :])
                ins_.then_inc(a_turned.sem, 1)

            def av(g, u):
                h, group = u % H, u // 4
                pe.wait_ge(a_pT.sem, a_pT.at(g, u + 1))
                if u % 4 == 0 and group >= 2:
                    pe.wait_ge(a_o.sem, a_o.at(g, group - 1))
                for c, n in enumerate(key_rows):
                    ins_ = pe.matmul(bank(6 + group % 2)[:, (u % 4) * DH:(u % 4) * DH + DH],
                                     pT_a[0:n, u % 2, c * P:c * P + P], v_a[0:n, c, h * DH:h * DH + DH],
                                     start=(c == 0), stop=(c == T))
                ins_.then_inc(a_av.sem, 1)

            with pe.Fori(0, B) as b:
                pe.wait_ge(turn_done, b + done)
                pe.wait_ge(a_in.sem, a_in.at(b, 1))
                for n in range(len(ITEMS)):
                    item(b, n)
                pe.wait_ge(a_even.sem, a_even.at(b, HALF_ITEMS))
                pe.wait_ge(a_odd.sem, a_odd.at(b, HALF_ITEMS))
                for u in range(UA + 2):
                    if u < UA:
                        scores(b, u)
                    if u >= 2:
                        av(b, u - 2)
                    if 1 <= u <= UA:
                        turn_probs(b, u - 1)
                pe.wait_ge(a_o.sem, a_o.at(b, GA))
                for i in range(NBLK):
                    for t in range(T):
                        ins_ = pe.transpose(bank(i)[:, t * P:t * P + P], o_a[:, t, i * P:i * P + P], ident[:, :])
                    ins_.then_inc(a_oturn.sem, 1)
                pe.wait_ge(a_oe.sem, a_oe.at(b, NBLK // 2))
                pe.wait_ge(a_oo.sem, a_oo.at(b, NBLK // 2))
                for t in range(T):
                    for i in range(NBLK):
                        ins_ = pe.matmul(bank(0)[:, t * P:t * P + P], oT_a[:, i, t * P:t * P + P],
                                         mat("L1_xattn_Wo", i * P), start=(i == 0), stop=(i == NBLK - 1))
                ins_.then_inc(a_out.sem, 1)

        def self_scalar(act, step, use, done):
            with act.Fori(0, B) as b:
                act.wait_ge(turn_done, b + done)
                for n in range(0, len(ITEMS), 2):
                    src, dst = item_place(*ITEMS[n], n)
                    act.wait_ge(a_proj.sem, a_proj.at(b, n + 1))
                    (act.mul(dst, src, DH ** -0.5) if ITEMS[n][0] == "q" else act.copy(dst, src)).then_inc(a_even.sem, 1)
                for u in range(UA):
                    act.wait_ge(a_max.sem, a_max.at(b, u + 1))
                    if u >= 2:
                        act.wait_ge(a_turned.sem, a_turned.at(b, u - 1))
                    act.activation(pr_a[:, u % 2], bank(2 * (u % 2), 2)[:, 0:NKEY], ACT.Exp,
                                   bias=aw["nm"][:, u % 4:u % 4 + 1], accum_out=aw["sums"][:, u:u + 1])\
                        .then_inc(a_probs.sem, 1)
                for i in range(0, NBLK, 2):
                    act.wait_ge(a_oturn.sem, a_oturn.at(b, i + 1))
                    act.copy(oT_a[:, i, :], bank(i)).then_inc(a_oe.sem, 1)

        def self_vector(dve, step, use, done):
            def max_of(g, u):
                dve.wait_ge(a_scores.sem, a_scores.at(g, u + 1))
                dve.tensor_reduce(aw["nm"][:, u % 4:u % 4 + 1], bank(2 * (u % 2), 2)[:, 0:NKEY], X, ALU.max,
                                  negate=True).then_inc(a_max.sem, 1)

            def copy_pT(g, u):
                dve.wait_ge(a_turned.sem, a_turned.at(g, u + 1))
                if u >= 2:
                    dve.wait_ge(a_av.sem, a_av.at(g, u - 1))
                dve.tensor_copy(pT_a[:, u % 2, 0:T * P], bank(4))
                dve.tensor_copy(pT_a[0:KC, u % 2, T * P:T * P + P], bank(5)[0:KC, 0:P]).then_inc(a_pT.sem, 1)

            def norm_o(g, i):
                t, j = divmod(i, 4)
                dve.wait_ge(a_av.sem, a_av.at(g, 4 * i + 4))
                step(dve.reciprocal(aw["rec"], aw["sums"][:, 4 * i:4 * i + 4]))
                dve.tensor_tensor(o_a[:, t, j * 4 * DH:(j + 1) * 4 * DH].rearrange("p (h e) -> p h e", h=4),
                                  bank(6 + i % 2)[:, 0:4 * DH].rearrange("p (h e) -> p h e", h=4),
                                  aw["rec"].unsqueeze(2).to_broadcast([P, 4, DH]), ALU.mult).then_inc(a_o.sem, 1)

            with step.loop(B, GA + 1) as b:
                dve.wait_ge(turn_done, b + done)
                for n in range(1, len(ITEMS), 2):
                    src, dst = item_place(*ITEMS[n], n)
                    dve.wait_ge(a_proj.sem, a_proj.at(b, n + 1))
                    if ITEMS[n][0] == "q":
                        dve.tensor_scalar(dst, src, DH ** -0.5, None, ALU.mult).then_inc(a_odd.sem, 1)
                    else:
                        dve.tensor_copy(dst, src).then_inc(a_odd.sem, 1)
                for u in range(UA + 3):
                    if u < UA:
                        max_of(b, u)
                    if 1 <= u <= UA:
                        copy_pT(b, u - 1)
                    if u >= 6 and (u - 6) % 4 == 0:
                        norm_o(b, (u - 6) // 4)
                for i in range(1, NBLK, 2):
                    dve.wait_ge(a_oturn.sem, a_oturn.at(b, i + 1))
                    dve.tensor_copy(oT_a[:, i, :], bank(i)).then_inc(a_oo.sem, 1)
                dve.wait_ge(a_out.sem, a_out.at(b, 1))
                step(dve.tensor_tensor(sum_a, bank(0).rearrange("p (t d) -> p t d", t=T),
                                       row("L1_xattn_bo").unsqueeze(1).to_broadcast([P, T, D]), ALU.add))
                xb = x[:, ds(b * T, T), :]
                dve.scalar_tensor_tensor(out=xb, in0=sum_a, scalar=tg[:, 1:2], in1=xb, op0=ALU.mult, op1=ALU.add)\
                    .then_inc(turn_done, 1)

        NKC = NKV // P
        lw = carve({"bc": R8 * S, "placeq": T * NQ, "placek": T * NKV, "rn": T * D, "w": T * 2, "ws": 1 + NKC,
                    "qT": NBF * S, "kT": NBF * S, "v": T * HF * DH, "pr": 2 * 4 * P, "pT": 2 * 4 * P, "nm": 2 * 4,
                    "sums": 2 * 4, "rec": 2 * 4, "o": T * HF * DH, "placeT": T * P, "xq": NQ, "xk": NKV,
                    "oh": HF * DH, "ohT": HF * DH,
                    "routed": D})
        bc1 = lw["bc"].rearrange("p (r q) -> p r q", r=R8)
        placeq = lw["placeq"].rearrange("p (t i) -> p t i", t=T)
        placek = lw["placek"].rearrange("p (t i) -> p t i", t=T)
        rn1 = lw["rn"].rearrange("p (t d) -> p t d", t=T)
        w1 = lw["w"].rearrange("p (k t) -> p t k", k=2)
        qT_l = lw["qT"].rearrange("p (i q) -> p i q", i=NBF)
        kT_l = lw["kT"].rearrange("p (i q) -> p i q", i=NBF)
        v_l = lw["v"].rearrange("p (t n) -> p t n", t=T)
        pr_l = lw["pr"].rearrange("p (n k) -> p n k", n=2)
        pT_l = lw["pT"].rearrange("p (n k) -> p n k", n=2)
        nm_l = lw["nm"].rearrange("p (n k) -> p n k", n=2)
        sums_l = lw["sums"].rearrange("p (n k) -> p n k", n=2)
        rec_l = lw["rec"].rearrange("p (n k) -> p n k", n=2)
        o_l = lw["o"].rearrange("p (t n) -> p t n", t=T)
        oT_l = qT_l
        kh_flat = lw["kT"][:, 0:NBF * NKV]
        kh = kh_flat.rearrange("p (i k) -> p i k", i=NBF)
        qh_flat = lw["kT"][:, NBF * NKV:NBF * NKV + NBF * NQ]
        qh = qh_flat.rearrange("p (i q) -> p i q", i=NBF)
        vh = lw["v"][:, 0:NKC * HF * DH].rearrange("p (c n) -> p c n", c=NKC)
        LITEMS = [("q", i) for i in range(NBF)] + [("k", i) for i in range(NBF)] + [("v", i) for i in range(T)]
        HL = len(LITEMS) // 2
        UL, UH = 2 * T, 4
        UT = UL + UH
        l_in = Signal(sem("l_in"), 1)
        l_proj = Signal(sem("l_proj"), len(LITEMS))
        l_even, l_odd = Signal(sem("l_even"), HL), Signal(sem("l_odd"), HL)
        l_placed = Signal(sem("l_placed"), 1)
        l_gath = Signal(sem("l_gath"), 1)
        l_gout = Signal(sem("l_gout"), 2)
        l_hproj = Signal(sem("l_hproj"), 1)
        l_hout = Signal(sem("l_hout"), 2)
        l_scores, l_max = Signal(sem("l_scores"), UT), Signal(sem("l_max"), UT)
        l_probs, l_turned = Signal(sem("l_probs"), UT), Signal(sem("l_turned"), UT)
        l_pT, l_av, l_o = Signal(sem("l_pT"), UT), Signal(sem("l_av"), UT), Signal(sem("l_o"), UT)
        l_oturn = Signal(sem("l_oturn"), 1)
        l_oT = Signal(sem("l_oT"), 2)
        l_heavy = Signal(sem("l_heavy"), 1)
        l_routed = Signal(sem("l_routed"), 1)
        l_out = Signal(sem("l_out"), 1)

        def blocks_of(u):
            if u < UL:
                return [(2 * i + u % 2, 0) for i in range(4)], u // 2
            j = u - UL
            return [(4 * (j // 2) + 2 * i + j % 2, c) for i in range(2) for c in range(NKC)], None

        def route1_pool(pool, step, use, done):
            pool.wait_ge(w_ready, 2)
            pool.wait_ge(xnT_ready, xnT_count(3))
            with pool.Fori(0, B) as b:
                pool.wait_ge(turn_done, b + done)
                pool.tensor_copy(x_in[:, :], xnT[:, ds(b * S, S)])
                pool.tensor_copy(rn1, rn[:, ds(b * T, T), :])
                for kind in range(2):
                    ins_ = pool.tensor_copy(w1[:, :, kind:kind + 1], col_w[:, :, ds(b + kind * B, 1)])
                ins_.then_inc(l_in.sem, 1)

        def route1_tensor(pe, use, done):
            pe.wait_ge(mats_loaded[3], 16)
            descent_tensor(pe, 1, R8)
            pe.wait_ge(b_read, B + R8)

            def scores(g, u):
                if u >= 4:
                    pe.wait_ge(l_probs.sem, l_probs.at(g, u - 3))
                blocks, w = blocks_of(u)
                for i in range(4 if u < UL else 2):
                    h = blocks[i * (1 if u < UL else NKC)][0]
                    at = slice(DH * (h % 2), DH * (h % 2) + DH)
                    if u < UL:
                        q, k, n = qT_l[at, h // 2, w * P:w * P + P], kT_l[at, h // 2, w * P:w * P + P], P
                    else:
                        q, k, n = qh[at, h // 2, :], kh[at, h // 2, :], NKV
                    ins_ = pe.matmul(bank(u % 4)[:, i * n:i * n + n], q, k, start=True, stop=True)
                ins_.then_inc(l_scores.sem, 1)

            def turn_probs(g, u):
                pe.wait_ge(l_probs.sem, l_probs.at(g, u + 1))
                if u >= 2:
                    pe.wait_ge(l_pT.sem, l_pT.at(g, u - 1))
                for i in range(4):
                    ins_ = pe.transpose(bank(4 + u % 2)[:, i * P:i * P + P], pr_l[:, u % 2, i * P:i * P + P], ident[:, :])
                ins_.then_inc(l_turned.sem, 1)

            def av(g, u):
                pe.wait_ge(l_pT.sem, l_pT.at(g, u + 1))
                if u >= 2:
                    pe.wait_ge(l_o.sem, l_o.at(g, u - 1))
                blocks, w = blocks_of(u)
                for i, (h, c) in enumerate(blocks):
                    v = v_l[:, w, h * DH:h * DH + DH] if u < UL else vh[:, c, h * DH:h * DH + DH]
                    j = i if u < UL else i // NKC
                    ins_ = pe.matmul(bank(6 + u % 2)[:, j * DH:j * DH + DH], pT_l[:, u % 2, i * P:i * P + P], v,
                                     start=(u < UL or c == 0), stop=(u < UL or c == NKC - 1))
                ins_.then_inc(l_av.sem, 1)

            def run(g, first, past):
                for u in range(first, past + 2):
                    if u < past:
                        scores(g, u)
                    if u >= first + 2:
                        av(g, u - 2)
                    if first + 1 <= u <= past:
                        turn_probs(g, u - 1)

            with pe.Fori(0, B) as b:
                pe.wait_ge(turn_done, b + done)
                pe.wait_ge(l_in.sem, l_in.at(b, 1))
                for n, (kind, i) in enumerate(LITEMS):
                    if n >= 8:
                        s = (l_even, l_odd)[n % 2]
                        pe.wait_ge(s.sem, s.at(b, (n - 8) // 2 + 1))
                    if kind == "v":
                        ins_ = pe.matmul(bank(n % 8), x_in[:, i * P:i * P + P], mat("L1_ffn_wv_light", 0, HF * DH),
                                         start=True, stop=True)
                    else:
                        ins_ = pe.matmul(bank(n % 8), mat(f"L1_ffn_w{kind}_light", i * P), x_in[:, :],
                                         start=True, stop=True)
                    ins_.then_inc(l_proj.sem, 1)
                pe.wait_ge(l_even.sem, l_even.at(b, HL))
                pe.wait_ge(l_odd.sem, l_odd.at(b, HL))
                run(b, 0, UL)
                pe.wait_ge(l_placed.sem, l_placed.at(b, 1))
                for t in range(T):
                    pe.matmul(bank(0)[:, 0:NQ], rn1[:, t, :], placeq[:, t, :], start=(t == 0), stop=(t == T - 1))
                for t in range(T):
                    pe.matmul(bank(1)[:, 0:NKV], rn1[:, t, :], placek[:, t, :], start=(t == 0), stop=(t == T - 1))
                for j in range(1 + NKC):
                    for t in range(T):
                        place = placeq[:, t, :] if j == 0 else placek[:, t, (j - 1) * P:j * P]
                        pe.matmul(bank(2)[:, j:j + 1], place, w1[:, t, 0:1] if j == 0 else w1[:, t, 1:2],
                                  start=(t == 0), stop=(t == T - 1))
                for t in range(T):
                    ins_ = pe.transpose(bank(3)[:, t * P:t * P + P], placeq[:, t, :], ident[:, :])
                ins_.then_inc(l_gath.sem, 1)
                pe.wait_ge(l_gout.sem, l_gout.at(b, 2))
                for i in range(NBF):
                    pe.matmul(bank(0)[:, i * NQ:i * NQ + NQ], mat("L1_ffn_wq_heavy", i * P), lw["xq"],
                              start=True, stop=True)
                for i in range(NBF):
                    pe.matmul(bank(1 + i // 2)[:, (i % 2) * NKV:(i % 2) * NKV + NKV], mat("L1_ffn_wk_heavy", i * P),
                              lw["xk"], start=True, stop=True)
                for c in range(NKC):
                    ins_ = pe.matmul(bank(3 + c), lw["xk"][:, c * P:c * P + P], mat("L1_ffn_wv_heavy", 0, HF * DH),
                                     start=True, stop=True)
                ins_.then_inc(l_hproj.sem, 1)
                pe.wait_ge(l_hout.sem, l_hout.at(b, 2))
                run(b, UL, UT)
                pe.wait_ge(l_o.sem, l_o.at(b, UT))
                for i in range(NBF):
                    for t in range(T):
                        pe.transpose(bank(i)[:, t * P:t * P + P], o_l[:, t, i * P:i * P + P], ident[:, :])
                for i in range(NBF):
                    ins_ = pe.transpose(bank(4)[:, i * P:i * P + P], lw["oh"][:, i * P:i * P + P], ident[:, :])
                ins_.then_inc(l_oturn.sem, 1)
                pe.wait_ge(l_oT.sem, l_oT.at(b, 2))
                for i in range(NBF):
                    ins_ = pe.matmul(bank(5)[:, 0:D], lw["ohT"][:, i * P:i * P + P], mat("L1_ffn_wo_heavy", i * P),
                                     start=(i == 0), stop=(i == NBF - 1))
                ins_.then_inc(l_heavy.sem, 1)
                pe.wait_ge(l_routed.sem, l_routed.at(b, 1))
                for t in range(T):
                    for i in range(NBF):
                        pe.matmul(bank(6)[:, t * P:t * P + P], oT_l[:, i, t * P:t * P + P],
                                  mat("L1_ffn_wo_light", i * P), start=(i == 0), stop=False)
                    ins_ = pe.matmul(bank(6)[:, t * P:t * P + P], lw["placeT"][:, t * P:t * P + P], lw["routed"],
                                     start=False, stop=True)
                ins_.then_inc(l_out.sem, 1)

        def route1_scalar(act, step, use, done):
            descent_scalar(act, 1)

            def probs(g, u):
                act.wait_ge(l_max.sem, l_max.at(g, u + 1))
                if u >= 2:
                    act.wait_ge(l_turned.sem, l_turned.at(g, u - 1))
                    act.wait_ge(l_o.sem, l_o.at(g, u - 1))
                n = P if u < UL else NKV
                for i in range(4 * P // n):
                    ins_ = act.activation(pr_l[:, u % 2, i * n:i * n + n], bank(u % 4)[:, i * n:i * n + n], ACT.Exp,
                                          bias=nm_l[:, u % 2, i:i + 1], accum_out=sums_l[:, u % 2, i:i + 1])
                ins_.then_inc(l_probs.sem, 1)

            with act.Fori(0, B) as b:
                act.wait_ge(turn_done, b + done)
                for n in range(0, len(LITEMS), 2):
                    kind, i = LITEMS[n]
                    act.wait_ge(l_proj.sem, l_proj.at(b, n + 1))
                    dst = {"q": qT_l, "k": kT_l, "v": v_l}[kind][:, i, :]
                    (act.mul(dst, bank(n % 8), DH ** -0.5) if kind == "q" else act.copy(dst, bank(n % 8)))\
                        .then_inc(l_even.sem, 1)
                for u in range(UL):
                    probs(b, u)
                act.wait_ge(l_gath.sem, l_gath.at(b, 1))
                act.mul(lw["xq"], bank(0)[:, 0:NQ], col("L1_ffn_gamma_heavy"))
                act.mul(lw["xk"], bank(1)[:, 0:NKV], col("L1_ffn_gamma_heavy")).then_inc(l_gout.sem, 1)
                act.wait_ge(l_hproj.sem, l_hproj.at(b, 1))
                act.mul(qh_flat, bank(0), DH ** -0.5)
                act.copy(kh_flat[:, 0:S], bank(1))
                act.copy(kh_flat[:, S:2 * S], bank(2)).then_inc(l_hout.sem, 1)
                for u in range(UL, UT):
                    probs(b, u)
                act.wait_ge(l_oturn.sem, l_oturn.at(b, 1))
                act.copy(lw["ohT"], bank(4))
                act.copy(oT_l[:, 0, :], bank(0))
                act.copy(oT_l[:, 1, :], bank(1)).then_inc(l_oT.sem, 1)

        def route1_vector(dve, step, use, done):
            descent_vector(dve, step, 1, bc1, R8)

            def max_of(g, u):
                dve.wait_ge(l_scores.sem, l_scores.at(g, u + 1))
                if u >= 2:
                    dve.wait_ge(l_probs.sem, l_probs.at(g, u - 1))
                n = 4 if u < UL else 2
                dve.tensor_reduce(nm_l[:, u % 2, 0:n], bank(u % 4).rearrange("p (i k) -> p i k", i=n), X, ALU.max,
                                  negate=True).then_inc(l_max.sem, 1)

            def copy_pT(g, u):
                dve.wait_ge(l_turned.sem, l_turned.at(g, u + 1))
                if u >= 2:
                    dve.wait_ge(l_av.sem, l_av.at(g, u - 1))
                dve.tensor_copy(pT_l[:, u % 2, :], bank(4 + u % 2)).then_inc(l_pT.sem, 1)

            def norm_o(g, u):
                dve.wait_ge(l_av.sem, l_av.at(g, u + 1))
                blocks, w = blocks_of(u)
                n = 4 if u < UL else 2
                step(dve.reciprocal(rec_l[:, u % 2, 0:n], sums_l[:, u % 2, 0:n]))
                if u < UL:
                    dst = o_l[:, w, :].rearrange("p (i r e) -> p i r e", r=2, e=DH)[:, :, u % 2, :]
                else:
                    j = u - UL
                    dst = lw["oh"][:, (j // 2) * 256:(j // 2) * 256 + 256].rearrange("p (i r e) -> p i r e", r=2, e=DH)[:, :, j % 2, :]
                dve.tensor_tensor(dst, bank(6 + u % 2)[:, 0:n * DH].rearrange("p (i e) -> p i e", i=n),
                                  rec_l[:, u % 2, 0:n].unsqueeze(2).to_broadcast([P, n, DH]), ALU.mult)\
                    .then_inc(l_o.sem, 1)

            def run(g, first, past):
                for u in range(first, past + 2):
                    if u < past:
                        max_of(g, u)
                    if first + 1 <= u <= past:
                        copy_pT(g, u - 1)
                    if u >= first + 2:
                        norm_o(g, u - 2)

            with step.loop(B, 2 * RANK_STEPS + UT) as b:
                dve.wait_ge(turn_done, b + done)
                for n in range(1, len(LITEMS), 2):
                    kind, i = LITEMS[n]
                    dve.wait_ge(l_proj.sem, l_proj.at(b, n + 1))
                    dst = {"q": qT_l, "k": kT_l, "v": v_l}[kind][:, i, :]
                    (dve.tensor_scalar(dst, bank(n % 8), DH ** -0.5, None, ALU.mult) if kind == "q"
                     else dve.tensor_copy(dst, bank(n % 8))).then_inc(l_odd.sem, 1)
                run(b, 0, UL)
                rank_and_place(dve, step, bc1, b, placeq, NQ)
                rank_and_place(dve, step, bc1, b + B, placek, NKV)
                dve.sem_inc(l_placed.sem, 1)
                dve.wait_ge(l_gath.sem, l_gath.at(b, 1))
                dve.tensor_copy(lw["ws"], bank(2)[:, 0:1 + NKC])
                dve.tensor_copy(lw["placeT"], bank(3)).then_inc(l_gout.sem, 1)
                dve.wait_ge(l_hproj.sem, l_hproj.at(b, 1))
                for c in range(NKC):
                    ins_ = dve.tensor_scalar(vh[:, c, :], bank(3 + c), lw["ws"][:, 1 + c:2 + c], None, ALU.mult)
                ins_.then_inc(l_hout.sem, 1)
                run(b, UL, UT)
                dve.wait_ge(l_oturn.sem, l_oturn.at(b, 1))
                dve.tensor_copy(oT_l[:, 2, :], bank(2))
                dve.tensor_copy(oT_l[:, 3, :], bank(3)).then_inc(l_oT.sem, 1)
                dve.wait_ge(l_heavy.sem, l_heavy.at(b, 1))
                dve.tensor_scalar(lw["routed"], bank(5)[:, 0:D], lw["ws"][:, 0:1], None, ALU.mult)\
                    .then_inc(l_routed.sem, 1)
                dve.wait_ge(l_out.sem, l_out.at(b, 1))
                xb = x[:, ds(b * T, T), :]
                dve.scalar_tensor_tensor(out=xb, in0=bank(6).rearrange("p (t d) -> p t d", t=T), scalar=tg[:, 5:6],
                                         in1=xb, op0=ALU.mult, op1=ALU.add).then_inc(turn_done, 1)

        W2, W3 = 3 * FF, 2 * FF + NF
        mw = carve({"w": 2 * W2, "h": 2 * NF * S, "sg": 2 * S, "acc": NT * D, "y": 2 * T * D, "lg": NT * 16, "pr": NT * 16,
                    "mx": NT * 2, "sm": NT * 2, "cw": NT * E, "top": NT * E, "idx": NT * E, "idxf": NT * E,
                    "hot": NT * E})
        wts = mw["w"].rearrange("p (n k) -> p n k", n=2)
        h_m = mw["h"].rearrange("p (n f q) -> p n f q", n=2, f=NF)
        sg = mw["sg"].rearrange("p (n q) -> p n q", n=2)
        acc = mw["acc"].rearrange("p (n d) -> p n d", n=NT)
        y_m = mw["y"].rearrange("p (n t d) -> p n t d", n=2, t=T)
        cw = mw["cw"].rearrange("p (n e) -> p n e", n=NT)
        IB = 2 * B

        class Experts:

            def __init__(self, n):
                self.loaded = [sem(f"e{n}_loaded{i}") for i in range(2)]
                self.logits = sem(f"e{n}_logits")
                self.lgread = sem(f"e{n}_lgread")
                self.sm = sem(f"e{n}_sm")
                self.exps = sem(f"e{n}_exps")
                self.pre = Signal(sem(f"e{n}_pre"), IB * NF)
                self.act = Signal(sem(f"e{n}_act"), IB * NF)
                self.h = Signal(sem(f"e{n}_h"), IB * NF)
                self.y = Signal(sem(f"e{n}_y"), IB, 2)
                self.acc = Signal(sem(f"e{n}_acc"), IB, 2)

        ex = [Experts(2), Experts(3)]

        def moe_sync(sp, which, done):
            src, n = (ins["experts2"], W2) if which == 0 else (ins["experts3"], W3)
            s = ex[which]
            sp.wait_ge(turn_done, done)
            for i in range(2):
                sp.dma_start(wts[:, i, 0:n], src[:, i, :]).then_inc(s.loaded[i], 16)
            with sp.Fori(0, E // 2 - 1) as r:
                for i in range(2):
                    sp.wait_ge(s.y.sem, s.y.at(r, (i + 1) * B))
                    sp.dma_start(wts[:, i, 0:n], src[:, ds(2 * r + (2 + i), 1), :].rearrange("p a n -> p (a n)"))\
                        .then_inc(s.loaded[i], 16)

        def moe_tensor(pe, which, done):
            s = ex[which]
            pe.wait_ge(turn_done, done)
            pe.wait_ge(xnT_ready, xnT_count(5 + 2 * which))
            pe.wait_ge(mats_loaded[4], 16)
            pe.sem_inc(s.y.sem, s.y.ahead)
            n = 16 if which == 0 else 8
            name = "L2_ffn_w_router" if which == 0 else "L3_ffn_gate_w"
            for i in range(NT):
                ins_ = pe.matmul(bank(7)[:, i * n:i * n + n], xnT[:, i * P:i * P + P], mat(name, 0, n),
                                 start=True, stop=True)
            ins_.then_inc(s.logits, 1)

            def up(r, i):
                e, b = divmod(i, B)
                if b == 0:
                    pe.wait_ge(s.loaded[e], r * 16 + 16)
                for f in range(NF):
                    k = i * NF + f
                    if which == 0:
                        if k >= 2:
                            pe.wait_ge(s.h.sem, s.h.at(r, k - 1))
                        pe.matmul(bank(2 * (k % 2)), wts[:, e, f * P:f * P + P], xnT[:, b * S:b * S + S],
                                  start=True, stop=True)
                        ins_ = pe.matmul(bank(2 * (k % 2) + 1), wts[:, e, FF + f * P:FF + f * P + P],
                                         xnT[:, b * S:b * S + S], start=True, stop=True)
                    else:
                        if k >= 4:
                            pe.wait_ge(s.act.sem, s.act.at(r, k - 3))
                        ins_ = pe.matmul(bank(k % 4), wts[:, e, f * P:f * P + P], xnT[:, b * S:b * S + S],
                                         start=True, stop=True)
                    ins_.then_inc(s.pre.sem, 1)

            def down(r, i):
                e = i // B
                pe.wait_ge(s.acc.sem, s.acc.at(r, i - 1))
                ready = s.h if which == 0 else s.act
                pe.wait_ge(ready.sem, ready.at(r, (i + 1) * NF))
                off = 2 * FF if which == 0 else FF
                for t in range(T):
                    for f in range(NF):
                        ins_ = pe.matmul(bank(4 + i % 2)[:, t * P:t * P + P], h_m[:, i % 2, f, t * P:t * P + P],
                                         wts[:, e, off + f * P:off + f * P + P], start=(f == 0), stop=(f == NF - 1))
                ins_.then_inc(s.y.sem, 1)

            with pe.Fori(0, E // 2) as r:
                for i in range(IB + 1):
                    if i < IB:
                        up(r, i)
                    if i >= 1:
                        down(r, i - 1)

        def moe_scalar(act, which, done):
            s = ex[which]
            act.wait_ge(s.sm, 1)
            lg = mw["lg"].rearrange("p (n k e) -> p n k e", n=NT, e=E)
            pr = mw["pr"].rearrange("p (n k e) -> p n k e", n=NT, e=E)
            if which == 0:
                act.activation(pr[:, :, 0, :], lg[:, :, 0, :], ACT.Exp)
                act.activation(pr[:, :, 1, :], lg[:, :, 1, :], ACT.Exp, scale=1.0 / 0.1).then_inc(s.exps, 1)
            else:
                act.activation(mw["pr"][:, 0:NT * E], mw["lg"][:, 0:NT * E], ACT.Exp).then_inc(s.exps, 1)
            with act.Fori(0, E // 2) as r:
                for i in range(IB):
                    for f in range(NF):
                        k = i * NF + f
                        act.wait_ge(s.pre.sem, s.pre.at(r, k + 1))
                        if which == 0:
                            if k >= 2:
                                act.wait_ge(s.h.sem, s.h.at(r, k - 1))
                            act.activation(sg[:, k % 2, :], bank(2 * (k % 2)), ACT.Silu).then_inc(s.act.sem, 1)
                        else:
                            if f == 0:
                                act.wait_ge(s.y.sem, s.y.at(r, i - 1))
                            act.activation(h_m[:, i % 2, f, :], bank(k % 4), ACT.Gelu, bias=wts[:, i // B, 2 * FF + f:2 * FF + f + 1])\
                                .then_inc(s.act.sem, 1)

        def moe_vector(dve, step, which, done):
            s = ex[which]
            dve.wait_ge(turn_done, done)
            step(dve.memset(mw["acc"], 0.0))
            dve.sem_inc(s.acc.sem, s.acc.ahead)
            dve.wait_ge(s.logits, 1)
            if which == 0:
                lg = mw["lg"].rearrange("p (n e) -> p n e", e=E)
                pr = mw["pr"].rearrange("p (n e) -> p n e", e=E)
                mx, sm = mw["mx"], mw["sm"]
                n2 = 2 * NT
                step(dve.tensor_copy(mw["lg"], bank(7)[:, 0:NT * 16]))
                step(dve.tensor_reduce(mx, lg, X, ALU.max))
                dve.tensor_tensor(lg, lg, mx.unsqueeze(2).to_broadcast([P, n2, E]), ALU.subtract).then_inc(s.sm, 1)
                dve.wait_ge(s.exps, 1)
                step(dve.tensor_reduce(sm, pr, X, ALU.add))
                step(dve.reciprocal(sm, sm))
                step(dve.tensor_tensor(pr, pr, sm.unsqueeze(2).to_broadcast([P, n2, E]), ALU.mult))
                both = mw["pr"].rearrange("p (n k e) -> p n k e", n=NT, e=E)
                step(dve.tensor_tensor(cw, both[:, :, 0, :], both[:, :, 1, :], ALU.mult))
                step(dve.tensor_reduce(sm[:, 0:NT], cw, X, ALU.add))
                step(dve.tensor_scalar(sm[:, 0:NT], sm[:, 0:NT], 1e-9, None, ALU.add))
                step(dve.reciprocal(sm[:, 0:NT], sm[:, 0:NT]))
                step(dve.tensor_tensor(cw, cw, sm[:, 0:NT].unsqueeze(2).to_broadcast([P, NT, E]), ALU.mult))
            else:
                lg = mw["lg"][:, 0:NT * E].rearrange("p (n e) -> p n e", e=E)
                top = mw["top"].rearrange("p (n e) -> p n e", e=E)
                idx = mw["idx"].bitcast(U32).rearrange("p (n e) -> p n e", e=E)
                idxf = mw["idxf"].rearrange("p (n e) -> p n e", e=E)
                hot = mw["hot"].rearrange("p (n e) -> p n e", e=E)
                ex8 = mw["pr"][:, 0:NT * E].rearrange("p (n e) -> p n e", e=E)
                sm = mw["sm"][:, 0:NT]
                step(dve.tensor_tensor(lg, bank(7)[:, 0:NT * E].rearrange("p (n e) -> p n e", e=E),
                                       row("L3_ffn_gate_b", 0, E).unsqueeze(1).to_broadcast([P, NT, E]), ALU.add))
                for i in range(NT):
                    step.mark(dve.max(top[:, i, :], lg[:, i, :]))
                step.wait()
                for i in range(NT):
                    step.mark(dve.max_index(idx[:, i, :], top[:, i, :], lg[:, i, :]))
                step.wait()
                step(dve.tensor_copy(mw["idxf"], mw["idx"].bitcast(U32)))
                picks = pick[:, :].unsqueeze(1).to_broadcast([P, NT, E])
                step(dve.tensor_tensor(hot, picks, idxf[:, :, 0:1].to_broadcast([P, NT, E]), ALU.is_equal))
                step(dve.tensor_tensor(cw, picks, idxf[:, :, 1:2].to_broadcast([P, NT, E]), ALU.is_equal))
                step(dve.tensor_tensor(hot, hot, cw, ALU.add))
                dve.tensor_tensor(lg, lg, top[:, :, 0:1].to_broadcast([P, NT, E]), ALU.subtract).then_inc(s.sm, 1)
                dve.wait_ge(s.exps, 1)
                step(dve.tensor_tensor(cw, ex8, hot, ALU.mult))
                step(dve.tensor_reduce(sm, cw, X, ALU.add))
                step(dve.reciprocal(sm, sm))
                step(dve.tensor_tensor(cw, cw, sm.unsqueeze(2).to_broadcast([P, NT, E]), ALU.mult))

            def gate(r, i):
                for f in range(NF):
                    k = i * NF + f
                    dve.wait_ge(s.act.sem, s.act.at(r, k + 1))
                    if f == 0:
                        dve.wait_ge(s.y.sem, s.y.at(r, i - 1))
                    dve.tensor_tensor(h_m[:, i % 2, f, :], sg[:, k % 2, :], bank(2 * (k % 2) + 1), ALU.mult)\
                        .then_inc(s.h.sem, 1)

            def add_up(r, i):
                e, b = divmod(i, B)
                dve.wait_ge(s.y.sem, s.y.at(r, i + 1))
                src = bank(4 + i % 2).rearrange("p (t d) -> p t d", t=T)
                if which == 1:
                    bias = rows[:, ds(ROW_AT["L3_ffn_b2"][0] + (2 * r + e) * D, D)].unsqueeze(1).to_broadcast([P, T, D])
                    step(dve.tensor_tensor(y_m[:, i % 2], src, bias, ALU.add))
                    src = y_m[:, i % 2]
                for t in range(T):
                    n = b * T + t
                    ins_ = dve.scalar_tensor_tensor(out=acc[:, n, :], in0=src[:, t, :], scalar=cw[:, n, ds(2 * r + e, 1)],
                                                    in1=acc[:, n, :], op0=ALU.mult, op1=ALU.add)
                ins_.then_inc(s.acc.sem, 1)

            with step.loop(E // 2, IB * which) as r:
                for i in range(IB + 1):
                    if which == 0 and i < IB:
                        gate(r, i)
                    if i >= 1:
                        add_up(r, i - 1)
            dve.wait_ge(s.acc.sem, s.acc.at(E // 2 - 1, IB))
            n = 6 + which
            dve.scalar_tensor_tensor(out=x[:, :, :], in0=acc, scalar=tg[:, n:n + 1], in1=x[:, :, :], op0=ALU.mult,
                                     op1=ALU.add).then_inc(turn_done, 1)

        def moe2_sync(sp, use, done):
            moe_sync(sp, 0, done)

        def moe3_sync(sp, use, done):
            moe_sync(sp, 1, done)

        def moe2_tensor(pe, use, done):
            moe_tensor(pe, 0, done)

        def moe3_tensor(pe, use, done):
            moe_tensor(pe, 1, done)

        def moe2_scalar(act, step, use, done):
            moe_scalar(act, 0, done)

        def moe3_scalar(act, step, use, done):
            moe_scalar(act, 1, done)

        def moe2_vector(dve, step, use, done):
            moe_vector(dve, step, 0, done)

        def moe3_vector(dve, step, use, done):
            moe_vector(dve, step, 1, done)

        def setup_pool(pool, step):
            pool.memset(ident[:, :], 0.0)
            pool.memset(head_of_row[:, :], 1.0)
            pool.memset(head_of_key[:, :, :], 1.0)
            pool.memset(earlier[:, :, :], 1.0)
            pool.memset(expo[:, :], -0.5)
            pool.memset(tokens[:, :, :, :], 0.0)
            pool.memset(junk[:, :], 0.0)
            for which in range(2):
                pool.memset(k_inv[:, which, :], 1.0 / K_OF[which][1])
                pool.memset(k_col[:, which:which + 1], K_OF[which][1])
                pool.memset(k_log[:, which:which + 1], float(np.log(K_OF[which][1])))
            step(pool.memset(row_of[:, :, :], 1.0))
            for which in range(2):
                k = K_OF[which][0]
                for buf, n, v in ((k_inv[:, which, :], S, 1.0 / k), (k_col[:, which:which + 1], 1, k),
                                  (k_log[:, which:which + 1], 1, float(np.log(k)))):
                    ins_ = pool.affine_select(out=buf, in_=buf, compare_op=ALU.is_ge, fill=v, base=-B,
                                              pattern=[[0, n]], channel_multiplier=1)
            step(ins_)
            pool.affine_select(out=ident[:, :], in_=ident[:, :], compare_op=ALU.not_equal, fill=1.0, base=0,
                               pattern=[[-1, P]], channel_multiplier=1).then_inc(consts_ready, 1)
            step(pool.affine_select(out=head_of_row[:, :], in_=head_of_row[:, :], compare_op=ALU.is_ge, fill=0.0, base=0,
                                    pattern=[[-DK, H]], channel_multiplier=1))
            pool.affine_select(out=head_of_row[:, :], in_=head_of_row[:, :], compare_op=ALU.is_ge, fill=0.0,
                               base=DK - 1, pattern=[[DK, H]], channel_multiplier=-1).then_inc(consts_ready, 1)
            step(pool.affine_select(out=head_of_key[:, :, :], in_=head_of_key[:, :, :], compare_op=ALU.is_ge, fill=0.0,
                                    base=0, pattern=[[P, NCH], [-KC, HH]], channel_multiplier=1))
            pool.affine_select(out=head_of_key[:, :, :], in_=head_of_key[:, :, :], compare_op=ALU.is_ge, fill=0.0,
                               base=KC - 1, pattern=[[-P, NCH], [KC, HH]], channel_multiplier=-1)\
                .then_inc(consts_ready, 1)
            pool.affine_select(out=earlier[:, :, :], in_=earlier[:, :, :], compare_op=ALU.is_gt, fill=0.0, base=0,
                               pattern=[[P, T], [-1, S]], channel_multiplier=1).then_inc(consts_ready, 1)
            step(pool.affine_select(out=row_of[:, :, :], in_=row_of[:, :, :], compare_op=ALU.is_equal, fill=0.0, base=0,
                                    pattern=[[-1, 2 * B], [0, P]], channel_multiplier=1))
            pool.sem_inc(consts_ready, 1)
            pool.iota(slot_no[:, :], [[1, NKV]], base=0, channel_multiplier=0, allow_small_or_imprecise_dtypes=True)\
                .then_inc(consts_ready, 1)
            pool.iota(pick[:, :], [[1, 8]], base=0, channel_multiplier=0, allow_small_or_imprecise_dtypes=True)\
                .then_inc(consts_ready, 1)
            pool.wait_ge(small_loaded, 48)
            for kind, (name, base) in enumerate((("L0_ffn_routing_token", 0), ("L1_ffn_q_routing_token", 0),
                                                 ("L1_ffn_kv_routing_token", B))):
                for b in range(B):
                    ins_ = pool.tensor_copy(tokens[:, kind, b, base + b:base + b + 1], col(name))
            step(ins_)
            pool.sem_inc(consts_ready, 2)

        def setup_sync(sp):
            sp.dma_start(x[:, :, :], ins["x"]).then_inc(x_loaded, 16)
            sp.dma_start(ctxT[:, :, :], ins["ctxT"]).then_inc(small_loaded, 16)
            sp.dma_start(cols[:, :], ins["cols"]).then_inc(small_loaded, 16)
            sp.dma_start(rows[:, :], ins["rows"].to_broadcast([P, NROW])).then_inc(small_loaded, 16)
            for i, (first, past) in enumerate(MAT_PARTS):
                a, z = MAT_AT[first][0], MAT_AT[past][0] if past else NMAT
                sp.dma_start(mats[:, a:z], ins["mats"][:, a:z]).then_inc(mats_loaded[i], 16)

        def setup_scalar(act):
            act.wait_ge(small_loaded, 48)
            act.activation(tg[:, :], row("g_xattn", 0, 8), ACT.Tanh).then_inc(gates_ready, 1)

        def setup_vector(dve):
            dve.wait_ge(consts_ready, CONSTS)
            dve.wait_ge(gates_ready, 1)
            dve.wait_ge(x_loaded, 16)
            dve.sem_inc(turn_done, 1)

        ENGINE_PARTS = {
            "sync": {"small": small_sync, "moe2": moe2_sync, "moe3": moe3_sync},
            "gpsimd": {"norm": norm_pool, "small": small_pool, "route0": route0_pool, "self": self_pool,
                       "route1": route1_pool},
            "scalar": {"norm": norm_scalar, "small": small_scalar, "route0": route0_scalar, "self": self_scalar,
                       "route1": route1_scalar, "moe2": moe2_scalar, "moe3": moe3_scalar},
            "tensor": {"norm": norm_tensor, "small": small_tensor, "route0": route0_tensor, "self": self_tensor,
                       "route1": route1_tensor, "moe2": moe2_tensor, "moe3": moe3_tensor},
            "vector": {"norm": norm_vector, "small": small_vector, "route0": route0_vector, "self": self_vector,
                       "route1": route1_vector, "moe2": moe2_vector, "moe3": moe3_vector},
        }

        def layers(name, *args):
            done = 1
            for part, use in LAYERS:
                f = ENGINE_PARTS[name].get(part)
                if f:
                    f(*args, use, done)
                done += TURNS[part]
            return done

        block = ctx.enter_context(nc.Block())

        @block.sync
        def _(sp):
            setup_sync(sp)
            done = layers("sync", sp)
            sp.wait_ge(turn_done, done)
            sp.dma_start(out, x[:, :, :]).then_inc(stored, 16)
            sp.wait_ge(stored, 16)

        @block.gpsimd
        def _(pool):
            step = Steps(pool, pool_step)
            setup_pool(pool, step)
            layers("gpsimd", pool, step)

        @block.scalar
        def _(act):
            setup_scalar(act)
            layers("scalar", act, Steps(act, act_step))

        @block.tensor
        def _(pe):
            layers("tensor", pe)

        @block.vector
        def _(dve):
            setup_vector(dve)
            layers("vector", dve, Steps(dve, dve_step))


def _blocks(w):
    n = w.shape[0] // 128
    return w.reshape(n, 128, -1).transpose(1, 0, 2).reshape(128, -1)


def _rows128(w):
    out = np.zeros((128, w.shape[1]), w.dtype)
    out[:w.shape[0]] = w
    return out


def lay_out(v):
    v = {k: np.asarray(a) for k, a in v.items()}
    m = {n: v[n].T for n in ("L0_xattn_Wq", "L0_xattn_Wk", "L0_xattn_Wv", "L0_xattn_Wo", "L0_xattn_W1",
                             "L0_ffn_w1_l", "L0_ffn_w1_h", "L3_xattn_Wq", "L3_xattn_Wk", "L3_xattn_Wv", "L3_xattn_Wo")}
    m["L0_xattn_W2"] = _blocks(v["L0_xattn_W2"].T)
    m["L0_ffn_w2_l"] = _rows128(v["L0_ffn_w2_l"].T)
    m["L0_ffn_w2_h"] = _blocks(v["L0_ffn_w2_h"].T)
    inner = v["L1_xattn_Wq"].shape[1]
    m["L1_xattn_Wk"], m["L1_xattn_Wv"] = v["L1_xattn_Wkv"][:, :inner], v["L1_xattn_Wkv"][:, inner:]
    hid = v["L1_ffn_wq_light"].shape[1]
    m["L1_ffn_wk_light"], m["L1_ffn_wv_light"] = v["L1_ffn_wkv_light"][:, :hid], v["L1_ffn_wkv_light"][:, hid:]
    kv = v["L1_ffn_wkv_heavy"].reshape(HF, 2, DH, D)
    m["L1_ffn_wk_heavy"], m["L1_ffn_wv_heavy"] = (kv[:, i].reshape(hid, D).T for i in range(2))
    for n in ("L1_xattn_Wo", "L1_ffn_wo_light", "L1_ffn_wo_heavy"):
        m[n] = _blocks(v[n])
    mats = np.concatenate([m[n] if n in m else v[n] for n, _ in MATS], axis=1)
    cols = np.concatenate([v[n].reshape(-1, 128).T if v[n].size >= 128 else _rows128(v[n].reshape(-1, 1))
                           for n, _ in COLS], axis=1)
    rows = np.concatenate([v[n].reshape(-1) for n, _ in ROWS]).reshape(1, -1)
    w1 = v["L3_ffn_w1"].transpose(1, 0, 2)
    up = [v["L2_ffn_w_gate"].transpose(1, 0, 2), v["L2_ffn_w_up"].transpose(1, 0, 2)]
    down = [v[n].reshape(E, NF, 128, D).transpose(2, 0, 1, 3).reshape(128, E, NF * D)
            for n in ("L2_ffn_w_down", "L3_ffn_w2")]
    return {
        "x": v["x"].reshape(NT, P, D).transpose(1, 0, 2),
        "ctxT": v["ctx_1024"].transpose(2, 0, 1),
        "bias": v["fside_Bx16xSxS2_0"].reshape(B, H, T, P, KC).transpose(0, 2, 3, 1, 4).reshape(NT, P, H * KC),
        "mask": v["mask_Bx1xSxS2_ik1"].reshape(NT, P, KC),
        "mats": mats, "cols": cols, "rows": rows,
        "experts2": np.concatenate([up[0], up[1], down[0]], axis=2),
        "experts3": np.concatenate([w1, down[1], v["L3_ffn_b1"].reshape(E, NF, 128).transpose(2, 0, 1)], axis=2),
    }


def build(nc, arrays, stages):
    ins = {n: nc.dram_tensor(f"in_{n}_dram", a.shape, mybir.dt.from_np(a.dtype), kind="ExternalInput").ap()
           for n, a in arrays.items()}
    out = nc.dram_tensor("out_0_dram", (P, NT, D), F32, kind="ExternalOutput").ap()
    flamingo_kernel(nc, ins, out, stages)


def kernel(**inputs):
    import concourse.bacc as _bacc
    from concourse.bass_utils import run_bass_kernel_spmd as _run

    arrays = {n: np.ascontiguousarray(a) for n, a in lay_out(inputs).items()}
    nc = _bacc.Bacc("TRN2", target_bir_lowering=False, num_devices=1)
    build(nc, arrays, 8)
    r = _run(nc, [{f"in_{n}_dram": a for n, a in arrays.items()}], core_ids=[0])
    return r.results[0]["out_0_dram"].transpose(1, 0, 2).reshape(B, S, D)
```

```python
from contextlib import ExitStack, contextmanager

import numpy as np
import concourse.bass as bass
from concourse import mybir

F32 = mybir.dt.float32
I32 = mybir.dt.int32
U32 = mybir.dt.uint32
ALU = mybir.AluOpType
ACT = mybir.ActivationFunctionType
X = mybir.AxisListType.X
ds = bass.ds

P = 128
B = 4
S = 512
T = S // P
NT = B * T
D = 128
KC = 77
FF = 512
NF = FF // P
H = 16
DK = D // H
HH = H // 2
HK = HH * KC
NCH = -(-HK // P)
LASTR = HK - (NCH - 1) * P
DH = 64
NBLK = H * DH // P
HF = 8
NBF = HF * DH // P
NKEY = S + KC
NQ, NKV = 128, 256
E = 8
DESCENT = 50
EPS = 1e-5
MASKED = -3.0e38

COLS = [("L0_xattn_g1", 1), ("L0_xattn_be1", 1), ("L0_xattn_b1", 4), ("L0_ffn_gamma_l", 1), ("L0_ffn_gamma_h", 1),
        ("L0_ffn_b1_l", 1), ("L0_ffn_b1_h", 4), ("L1_xattn_ln_g", 1), ("L1_xattn_ln_b", 1), ("L1_ffn_gamma_light", 1),
        ("L1_ffn_gamma_heavy", 1), ("L2_xattn_bq", 1), ("L2_xattn_bk", 1), ("L3_xattn_bq", 1), ("L3_xattn_bk", 1),
        ("L0_ffn_routing_token", 1), ("L1_ffn_q_routing_token", 1), ("L1_ffn_kv_routing_token", 1)]
ROWS = [("L0_xattn_b2", 128), ("L0_xattn_g2", 128), ("L0_xattn_be2", 128), ("L0_ffn_b2_l", 128), ("L0_ffn_b2_h", 128),
        ("L1_xattn_bo", 128), ("L2_xattn_bv", 128), ("L2_xattn_bo", 128), ("L3_xattn_bv", 128), ("L3_xattn_bo", 128),
        ("L3_ffn_b2", 1024), ("L3_ffn_gate_b", 8), ("g_xattn", 4), ("g_ffn", 4)]
MATS = [("L0_xattn_Wq", 128), ("L0_xattn_Wk", 128), ("L0_xattn_Wv", 128), ("L0_xattn_Wo", 128), ("L0_xattn_W1", 512),
        ("L0_xattn_W2", 512), ("L0_ffn_w1_l", 64), ("L0_ffn_w2_l", 128), ("L0_ffn_w1_h", 512), ("L0_ffn_w2_h", 512),
        ("L1_xattn_Wq", 1024), ("L1_xattn_Wk", 1024), ("L1_xattn_Wv", 1024), ("L1_xattn_Wm", 1024),
        ("L1_xattn_Wo", 1024),
        ("L1_ffn_wq_light", 512), ("L1_ffn_wk_light", 512), ("L1_ffn_wv_light", 512), ("L1_ffn_wo_light", 512),
        ("L1_ffn_wq_heavy", 512), ("L1_ffn_wk_heavy", 512), ("L1_ffn_wv_heavy", 512), ("L1_ffn_wo_heavy", 512),
        ("L2_xattn_Wq", 128), ("L2_xattn_Wk", 128), ("L2_xattn_Wv", 128), ("L2_xattn_Wo", 128),
        ("L2_ffn_w_router", 8), ("L2_ffn_w_gating", 8),
        ("L3_xattn_Wq", 128), ("L3_xattn_Wk", 128), ("L3_xattn_Wv", 128), ("L3_xattn_Wo", 128), ("L3_ffn_gate_w", 8)]


def offsets(table):
    at, out = 0, {}
    for name, n in table:
        out[name] = (at, n)
        at += n
    return out, at


COL_AT, NCOL = offsets(COLS)
ROW_AT, NROW = offsets(ROWS)
MAT_AT, NMAT = offsets(MATS)
MAT_PARTS = [("L0_xattn_Wq", "L0_ffn_w1_l"), ("L0_ffn_w1_l", "L1_xattn_Wq"), ("L1_xattn_Wq", "L1_ffn_wq_light"),
             ("L1_ffn_wq_light", "L2_xattn_Wq"), ("L2_xattn_Wq", None)]


class Signal:

    def __init__(self, sem, per, ahead=0):
        self.sem, self.per, self.ahead = sem, per, ahead

    def at(self, turn, k):
        return turn * self.per + (k + self.ahead)


class Steps:

    def __init__(self, engine, sem):
        self.engine, self.sem, self.base, self.turn, self.per, self.k = engine, sem, 0, 0, 0, 0

    def mark(self, ins):
        ins.then_inc(self.sem, 1)
        self.k += 1

    def wait(self):
        self.engine.wait_ge(self.sem, self.turn * self.per + (self.base + self.k))

    def __call__(self, ins):
        self.mark(ins)
        self.wait()

    @contextmanager
    def loop(self, turns, per, start=0):
        self.base, self.k, self.per = self.base + self.k - start * per, 0, per
        with self.engine.Fori(start, start + turns) as turn:
            self.turn = turn
            yield turn
        assert self.k == per, f"the loop's steps: {self.k}, not {per}"
        self.base, self.k, self.turn, self.per = self.base + (start + turns) * per, 0, 0, 0


def flamingo_kernel(nc, ins, out, stages):
    ctx = ExitStack()

    def sb(name, shape, dt=F32):
        return ctx.enter_context(nc.sbuf_tensor(name, shape, dt))

    def sem(name):
        return ctx.enter_context(nc.semaphore(name))

    with ctx:
        mats = sb("mats", [P, NMAT])
        cols = sb("cols", [P, NCOL])
        rows = sb("rows", [P, NROW])
        ctxT = sb("ctxT", [P, B, KC])
        ident = sb("ident", [P, P])
        head_of_row = sb("head_of_row", [P, H])
        head_of_key = sb("head_of_key", [P, NCH, HH])
        earlier = sb("earlier", [P, T, S])
        slot_no = sb("slot_no", [P, NKV])
        expo = sb("expo", [P, NT])
        row_of = sb("row_of", [2 * B, 2 * B, P])
        tokens = sb("tokens", [P, 3, B, 2 * B])
        pick = sb("pick", [P, 8])
        tg = sb("tg", [P, 8])

        x = sb("x", [P, NT, D])
        xn = sb("xn", [P, NT, D])
        xnT = sb("xnT", [P, NT * P])
        rn = sb("rn", [P, NT, D])
        stat = sb("stat", [P, NT, 6])
        mv = sb("mv", [P, NT, 2])
        varr = sb("varr", [P, NT])
        rstd = sb("rstd", [P, NT])
        x_in = sb("x_in", [P, S])
        junk = sb("junk", [P, S])
        spare = sb("spare", [P, 2])
        bq_s = sb("bq_s", [P, 2])
        work = sb("work", [P, 21504])
        psum = ctx.enter_context(nc.psum_tensor("psum", [P, 8 * 512], F32))

        def bank(i, n=1):
            return psum[:, 512 * i:512 * (i + n)]

        def carve(sizes):
            at, out = 0, {}
            for name, n in sizes.items():
                out[name] = work[:, at:at + n]
                at += n
            assert at <= 21504, at
            return out

        def col(name, i=0, n=P):
            return cols[0:n, COL_AT[name][0] + i:COL_AT[name][0] + i + 1]

        def row(name, i=0, n=D, parts=P):
            return rows[0:parts, ROW_AT[name][0] + i:ROW_AT[name][0] + i + n]

        def mat(name, i=0, n=P, parts=P):
            return mats[0:parts, MAT_AT[name][0] + i:MAT_AT[name][0] + i + n]

        dve_step, act_step, pool_step = sem("dve_step"), sem("act_step"), sem("pool_step")
        x_loaded, small_loaded = sem("x_loaded"), sem("small_loaded")
        mats_loaded = [sem(f"mats_loaded{i}") for i in range(len(MAT_PARTS))]
        consts_ready, gates_ready = sem("consts_ready"), sem("gates_ready")
        turn_done = sem("turn_done")
        var_ready, rstd_ready = sem("var_ready"), sem("rstd_ready")
        xn_ready, rn_ready = sem("xn_ready"), sem("rn_ready")
        xn_turned, xnT_ready = sem("xn_turned"), sem("xnT_ready")
        stored = sem("stored")

        CONSTS = 9
        LAYERS = [("kv", 0), ("norm", 0), ("attend", 0), ("ffn0", 0), ("norm", 1), ("route0", 0),
                  ("norm", 2), ("self", 0), ("norm", 3), ("route1", 0),
                  ("kv", 1), ("norm", 4), ("attend", 1), ("norm", 5), ("moe2", 0),
                  ("kv", 2), ("norm", 6), ("gated", 2), ("norm", 7), ("moe3", 0)]
        LAYERS = LAYERS[:[4, 6, 8, 10, 13, 15, 18, 20][stages - 1]]
        TURNS = {"kv": 0, "norm": 0, "attend": B, "gated": B, "ffn0": B, "route0": B, "self": B, "route1": B,
                 "moe2": 1, "moe3": 1}
        RMS = (1, 3)
        TWICE = 2

        def before(kind_counts, call):
            return sum(kind_counts(c) for c in range(call))

        n_rstd = lambda c: 2 if c in RMS or c == TWICE else 1
        n_turn = lambda c: 2 * B if c in RMS else B

        xnT_count = lambda call: before(n_turn, call + 1)

        def norm_vector(dve, step, call, done):
            dve.wait_ge(turn_done, done)
            if call == 0:
                dve.wait_ge(x_loaded, 16)
            rounds = before(n_rstd, call)
            for again in range(2 if call == TWICE else 1):
                src = xn if again else x
                with step.loop(B, T) as b:
                    for t in range(T):
                        step.mark(dve.bn_stats(stat[:, ds(b * T + t, 1), :], src[:, ds(b * T + t, 1), :]))
                step.wait()
                for t in range(NT):
                    ins_ = dve.bn_aggr(mv[:, t, :], stat[:, t, :])
                step(ins_)
                dve.tensor_scalar(varr[:, :], mv[:, :, 1], EPS, None, ALU.add).then_inc(var_ready, 1)
                rounds += 1
                dve.wait_ge(rstd_ready, rounds)
                with step.loop(B, T) as b:
                    for t in range(T):
                        step.mark(dve.tensor_scalar(
                            xn[:, ds(b * T + t, 1), :], src[:, ds(b * T + t, 1), :], mv[:, ds(b * T + t, 1), 0],
                            rstd[:, ds(b * T + t, 1)], ALU.subtract, ALU.mult))
                step.wait()
            dve.sem_inc(xn_ready, 1)
            if call in RMS:
                with step.loop(B, T) as b:
                    for t in range(T):
                        ins = dve.scalar_tensor_tensor(
                            out=junk[:, t * P:t * P + P], in0=xn[:, ds(b * T + t, 1), :], scalar=1.0,
                            in1=xn[:, ds(b * T + t, 1), :], op0=ALU.mult, op1=ALU.mult,
                            accum_out=mv[:, ds(b * T + t, 1), 0])
                        step.mark(ins)
                    step.wait()
                dve.tensor_scalar(varr[:, :], mv[:, :, 0], 1e-24, 1.0 / D, ALU.max, ALU.mult).then_inc(var_ready, 1)
                rounds += 1
                dve.wait_ge(rstd_ready, rounds)
                with step.loop(B, T) as b:
                    for t in range(T):
                        step.mark(dve.tensor_scalar(
                            rn[:, ds(b * T + t, 1), :], xn[:, ds(b * T + t, 1), :], rstd[:, ds(b * T + t, 1)], None,
                            ALU.mult))
                step.wait()
                dve.sem_inc(rn_ready, 1)

        def norm_pool(pool, step, call, done):
            rounds = before(n_rstd, call)
            if call == 0:
                pool.wait_ge(consts_ready, CONSTS)
            for _ in range(n_rstd(call)):
                rounds += 1
                pool.wait_ge(var_ready, rounds)
                pool.tensor_tensor(rstd[:, :], varr[:, :], expo[:, :], ALU.pow).then_inc(rstd_ready, 1)

        def turn_batch(pe, src, b, turned):
            if turned >= 2:
                pe.wait_ge(xnT_ready, turned - 1)
            for t in range(T):
                ins = pe.transpose(bank(turned % 2)[:, t * P:t * P + P], src[:, b * T + t, :], ident[:, :])
            ins.then_inc(xn_turned, 1)

        def norm_tensor(pe, call, done):
            pe.wait_ge(turn_done, done)
            if call == 0:
                pe.wait_ge(consts_ready, CONSTS)
            turned = before(n_turn, call)
            pe.wait_ge(xn_ready, call + 1)
            for b in range(B):
                turn_batch(pe, xn, b, turned + b)
            if call in RMS:
                which = 0 if call == RMS[0] else 1
                pe.wait_ge(xnT_ready, turned + B)
                kinds = (0,) if which == 0 else (1, 2)
                n = 0
                for kind in kinds:
                    for b in range(B):
                        ins = pe.matmul(bank(2)[0:2 * B, :], tokens[:, kind, b, :], xnT[:, b * S:b * S + S],
                                        start=(n == 0), stop=(n == len(kinds) * B - 1))
                        n += 1
                ins.then_inc(logits_ready, 1)
                pe.wait_ge(rn_ready, which + 1)
                for b in range(B):
                    turn_batch(pe, rn, b, turned + B + b)

        def norm_scalar(act, step, call, done):
            turned = before(n_turn, call)
            act.wait_ge(turn_done, done)
            for b in range(B):
                act.wait_ge(xn_turned, turned + b + 1)
                src, dst = bank((turned + b) % 2), xnT[:, b * S:b * S + S]
                if call == TWICE:
                    ins = act.activation(dst, src, ACT.Identity, bias=col("L1_xattn_ln_b"), scale=col("L1_xattn_ln_g"))
                else:
                    ins = act.copy(dst, src)
                ins.then_inc(xnT_ready, 1)
            if call in RMS:
                which = 0 if call == RMS[0] else 1
                act.wait_ge(logits_ready, which + 1)
                gain = col("L0_ffn_gamma_l" if which == 0 else "L1_ffn_gamma_light")
                for b in range(B):
                    act.wait_ge(xn_turned, turned + B + b + 1)
                    act.mul(xnT[:, b * S:b * S + S], bank((turned + B + b) % 2), gain).then_inc(xnT_ready, 1)

        logits_ready = sem("logits_ready")

        sw = carve({"kT": B * KC, "Kbd": B * H * KC, "vs": B * NCH * D, "Vbd": B * 2 * NCH * HH * 9, "qT": S,
                    "bias": 2 * H * KC, "mask": 2 * KC, "maskf": 2 * KC, "sc": 4 * HK, "mx": 4 * HH,
                    "pT": 2 * NCH * P, "rec": 2 * HH, "o": T * D, "oT": S, "x1": S, "yT": S})
        kT_s = sw["kT"].rearrange("p (b k) -> p b k", b=B)
        Kbd = sw["Kbd"].rearrange("p (b h k) -> p b h k", b=B, h=H)
        vs = sw["vs"].rearrange("p (b c d) -> p b c d", b=B, c=NCH)
        Vbd = sw["Vbd"].rearrange("p (b f c h e) -> p b f c h e", b=B, f=2, c=NCH, h=HH)
        qT_s = sw["qT"]
        bias_s = sw["bias"].rearrange("p (n h k) -> p n h k", n=2, h=H)
        mask_s = sw["mask"].rearrange("p (n k) -> p n k", n=2)
        maskf = sw["maskf"].rearrange("p (n k) -> p n k", n=2)
        sc_s = sw["sc"].rearrange("p (n h k) -> p n h k", n=4, h=HH)
        pr_s = sw["sc"].rearrange("p (n k) -> p n k", n=4)
        mx_s = sw["mx"].rearrange("p (n h) -> p n h", n=4)
        pT_s = sw["pT"].rearrange("p (n k) -> p n k", n=2)
        rec_s = sw["rec"].rearrange("p (n h) -> p n h", n=2)
        o_s = sw["o"].rearrange("p (n d) -> p n d", n=T)
        x1 = sw["x1"].rearrange("p (t d) -> p t d", t=T)
        sc_at = sum(n for n in (B * KC, B * H * KC, B * NCH * D, B * 2 * NCH * HH * 9, S, 2 * H * KC, 2 * KC, 2 * KC))
        bias_at = sc_at - 2 * H * KC - 4 * KC
        ctx8 = work[:, sc_at:sc_at + B * HK].rearrange("p (b h k) -> p b h k", b=B, h=HH)
        sigT = work[:, bias_at:bias_at + 2 * NCH * S].rearrange("p (u q) -> p u q", u=2 * NCH)
        h_s = work[:, sc_at:sc_at + NF * S].rearrange("p (f q) -> p f q", f=NF)
        assert 2 * NCH * S <= 2 * H * KC + 4 * KC + 4 * HK and NF * S <= 4 * HK
        U = 2 * T

        ctx_here = sem("ctx_here")
        vs_zero, ones_set = sem("vs_zero"), sem("ones_set")
        kv_proj, kv_out, kv_bias = sem("kv_proj"), sem("kv_out"), sem("kv_bias")
        kv_ready = Signal(sem("kv_ready"), 1)
        q_proj, q_ready = Signal(sem("q_proj"), 1), Signal(sem("q_ready"), 1)
        bias_in = [Signal(sem(f"bias_in{i}"), 2 * 16) for i in range(2)]
        mask_in = [Signal(sem(f"mask_in{i}"), 2 * 16) for i in range(2)]
        mask_seen = sem("mask_seen")
        bq_scaled = sem("bq_scaled")
        masked = Signal(sem("masked"), T)
        s_scores = Signal(sem("s_scores"), U)
        s_read = Signal(sem("s_read"), U)
        s_max = Signal(sem("s_max"), U)
        s_shift = [Signal(sem(f"s_shift{i}"), T) for i in range(2)]
        s_probs = Signal(sem("s_probs"), U)
        s_turned = Signal(sem("s_turned"), U)
        s_pT = Signal(sem("s_pT"), U)
        s_av = Signal(sem("s_av"), U)
        s_o = Signal(sem("s_o"), U)
        o_turned = Signal(sem("o_turned"), 1)
        o_ready = Signal(sem("o_ready"), 1)
        o_out = Signal(sem("o_out"), 1)
        o_read = Signal(sem("o_read"), 1, 1)
        f_var, f_rstd = Signal(sem("f_var"), 1), Signal(sem("f_rstd"), 1)

        SMALL = ["L0_xattn", "L2_xattn", "L3_xattn"]
        rows_of = [P] * (NCH - 1) + [LASTR]

        def need(engine, signal, value):
            if not isinstance(value, int) or value > 0:
                engine.wait_ge(signal.sem, value)

        def kv_pool(pool, step, use, done):
            pool.wait_ge(turn_done, done)
            pool.memset(vs[:, :, NCH - 1, :], 0.0).then_inc(vs_zero, 1)
            pool.tensor_copy(sw["Vbd"].rearrange("p (n r e) -> p n r e", n=2 * B, e=9)[:, :, :, 8:9],
                             head_of_key[:, :, :].rearrange("p c h -> p (c h)").unsqueeze(1).unsqueeze(3)
                             .to_broadcast([P, 2 * B, NCH * HH, 1])).then_inc(ones_set, 1)

        def values_bias(pool, use):
            for b in range(B):
                pool.wait_ge(kv_out, use * B + b + 1)
                pool.tensor_tensor(vs[:, b], vs[:, b],
                                   row(SMALL[use] + "_bv").unsqueeze(1).to_broadcast([P, NCH, D]), ALU.add)\
                    .then_inc(kv_bias, 1)

        def kv_tensor(pe, use, done):
            name = SMALL[use]
            pe.wait_ge(turn_done, done)
            pe.wait_ge(mats_loaded[0 if use == 0 else 4], 16)
            if use == 0:
                pe.wait_ge(small_loaded, 48)
            for b in range(B):
                pe.wait_ge(ctx_here, use * B + b + 1)
                a = 2 + 2 * (b % 3)
                if b >= 3:
                    pe.wait_ge(kv_out, use * B + b - 2)
                pe.matmul(bank(a)[:, 0:KC], mat(name + "_Wk"), ctxT[:, b, :], start=True, stop=True)
                flat = ctx8[:, b].rearrange("p h k -> p (h k)")
                for c, n in enumerate(rows_of):
                    to = bank(a + 1)[:, c * P:c * P + P] if c < 4 else bank(a)[0:n, P:2 * P]
                    ins_ = pe.matmul(to, flat[:, c * P:c * P + n], mat(name + "_Wv"), start=True, stop=True)
                ins_.then_inc(kv_proj, 1)

        def kv_scalar(act, step, use, done):
            act.wait_ge(turn_done, done)
            if use == 0:
                act.wait_ge(small_loaded, 48)
            for b in range(B):
                act.copy(ctx8[:, b], ctxT[:, b:b + 1, :].to_broadcast([P, HH, KC])).then_inc(ctx_here, 1)
            act.wait_ge(vs_zero, use + 1)
            for b in range(B):
                a = 2 + 2 * (b % 3)
                act.wait_ge(kv_proj, use * B + b + 1)
                if use == 0:
                    act.copy(kT_s[:, b], bank(a)[:, 0:KC])
                else:
                    act.activation(kT_s[:, b], bank(a)[:, 0:KC], ACT.Identity, bias=col(SMALL[use] + "_bk"))
                act.copy(vs[0:LASTR, b, 4, :], bank(a)[0:LASTR, P:2 * P])
                act.copy(vs[:, b, 0:4, :], bank(a + 1).rearrange("p (c d) -> p c d", c=4)).then_inc(kv_out, 1)

        def spread_values(dve, b):
            for half in range(2):
                last = dve.tensor_tensor(
                    Vbd[:, b, half, :, :, 0:8],
                    vs[:, b, :, half * 64:half * 64 + 64].rearrange("p c (h e) -> p c h e", e=DK),
                    head_of_key[:, :, :].unsqueeze(3).to_broadcast([P, NCH, HH, DK]), ALU.mult)
            return last

        def q_projection(pe, use, b):
            g = b + use * B
            need(pe, o_read, o_read.at(g, -1))
            pe.matmul(bank(7), mat(SMALL[use] + "_Wq"), xnT[:, ds(b * S, S)], start=True, stop=True)\
                .then_inc(q_proj.sem, 1)

        def evacuate_q(act, use, b):
            act.wait_ge(q_proj.sem, q_proj.at(b + use * B, 1))
            if use == 0:
                ins_ = act.mul(qT_s, bank(7), float(DK) ** -0.5)
            else:
                act.wait_ge(bq_scaled, 2)
                ins_ = act.activation(qT_s, bank(7), ACT.Identity, bias=bq_s[:, use - 1:use], scale=float(DK) ** -0.5)
            ins_.then_inc(q_ready.sem, 1)

        def residual(dve, step, use, done, g, b):
            dve.wait_ge(turn_done, b + done)
            dve.wait_ge(o_out.sem, o_out.at(g, 0))
            out4 = bank(7).rearrange("p (t d) -> p t d", t=T)
            xb = x[:, ds(b * T, T), :]
            step(dve.tensor_tensor(x1, out4, row(SMALL[use] + "_bo").unsqueeze(1).to_broadcast([P, T, D]), ALU.add))
            dve.sem_inc(o_read.sem, 1)
            dve.scalar_tensor_tensor(out=xb, in0=x1, scalar=tg[:, use + 1:use + 2], in1=xb, op0=ALU.mult,
                                     op1=ALU.add).then_inc(turn_done, 1)

        def attend_sync(sp, use, done):
            sp.wait_ge(turn_done, done)

            def turn(b):
                g = b + use * B
                for t in range(T):
                    need(sp, s_read, s_read.at(g, 2 * (t - 1)))
                    sp.dma_start(bias_s[:, t % 2], ins["bias"][ds(b * T + t, 1)].rearrange(
                        "a p (h k) -> p (a h) k", h=H)).then_inc(bias_in[t % 2].sem, 16)
                    if use == 1:
                        sp.dma_start(mask_s[:, t % 2].bitcast(I32), ins["mask"][ds(b * T + t, 1)].rearrange(
                            "a p k -> p (a k)")).then_inc(mask_in[t % 2].sem, 16)

            turn(0)
            with sp.Fori(1, B) as b:
                turn(b)

        def by_pool(use, u):
            return use == 0 or u % 2 == 0

        def subtract_max(engine, g, u):
            return engine.tensor_tensor(sc_s[:, u % 4], sc_s[:, u % 4],
                                        mx_s[:, u % 4].unsqueeze(2).to_broadcast([P, HH, KC]), ALU.subtract)\
                .then_inc(s_shift[u % 2].sem, 1)

        def attend_pool(pool, step, use, done):
            def mask(b, g, t):
                pool.wait_ge(mask_in[t % 2].sem, mask_in[t % 2].at(b, 16 * (t // 2 + 1)))
                pool.sem_inc(mask_seen, 1)
                step(pool.tensor_scalar(maskf[:, t % 2], mask_s[:, t % 2].bitcast(I32), 0, MASKED,
                                        ALU.is_equal, ALU.mult))
                pool.wait_ge(bias_in[t % 2].sem, bias_in[t % 2].at(g, 16 * (t // 2 + 1)))
                pool.tensor_tensor(bias_s[:, t % 2], bias_s[:, t % 2],
                                   maskf[:, t % 2].unsqueeze(1).to_broadcast([P, H, KC]), ALU.add)\
                    .then_inc(masked.sem, 1)

            def power(b):
                pool.wait_ge(f_var.sem, f_var.at(b, 0))
                pool.tensor_tensor(rstd[:, 0:T], varr[:, 0:T], expo[:, 0:T], ALU.pow).then_inc(f_rstd.sem, 1)

            def turn(b, first):
                g = b + use * B
                if use == 1:
                    mask(b, g, 0)
                for u in range(U):
                    if by_pool(use, u):
                        pool.wait_ge(s_max.sem, s_max.at(g, u + 1))
                        subtract_max(pool, g, u)
                    if use == 1 and u % 2 == 0 and u // 2 + 1 < T:
                        mask(b, g, u // 2 + 1)
                    if use == 0 and u == 5 and not first:
                        power(b)

            per = T if use == 1 else 0
            if use == 1:
                values_bias(pool, use)
            turn(0, True)
            with step.loop(B - 1, per, 1) as b:
                turn(b, False)
            if use == 0:
                power(B)

        def attend_tensor(pe, use, done):
            name = SMALL[use]
            pe.wait_ge(xnT_ready, xnT_count([0, 4, 6][use]))
            pe.wait_ge(kv_out, (use + 1) * B)

            def scores(b, g, u):
                need(pe, s_read, s_read.at(g, u - 1))
                if u == 0:
                    pe.wait_ge(q_ready.sem, q_ready.at(g, 1))
                    pe.wait_ge(kv_ready.sem, kv_ready.at(g, 1))
                t, half = divmod(u, 2)
                for j in range(2):
                    h = half * HH + 4 * j
                    ins_ = pe.matmul(bank(2 * (u % 2) + j)[:, 0:4 * KC], qT_s[:, t * P:t * P + P],
                                     Kbd[:, ds(b, 1), h:h + 4, :].rearrange("p a h k -> p (a h) k"),
                                     start=True, stop=True)
                ins_.then_inc(s_scores.sem, 1)

            def turn_probs(g, u):
                pe.wait_ge(s_probs.sem, s_probs.at(g, u + 1))
                need(pe, s_pT, s_pT.at(g, u))
                for c, n in enumerate(rows_of):
                    to = bank(4)[:, c * P:c * P + P] if c < 4 else bank(5)[0:n, 0:P]
                    ins_ = pe.transpose(to, pr_s[:, u % 4, c * P:c * P + n], ident[:, :])
                ins_.then_inc(s_turned.sem, 1)

            def av(b, g, u):
                pe.wait_ge(s_pT.sem, s_pT.at(g, u + 1))
                need(pe, s_o, s_o.at(g, u))
                for c, n in enumerate(rows_of):
                    ins_ = pe.matmul(bank(6)[:, 0:72], pT_s[0:n, u % 2, c * P:c * P + P],
                                     Vbd[0:n, ds(b, 1), u % 2, c, :, :].rearrange("p a h e -> p (a h) e"),
                                     start=(c == 0), stop=(c == NCH - 1))
                ins_.then_inc(s_av.sem, 1)

            def turn_o(g):
                pe.wait_ge(s_o.sem, s_o.at(g, 0))
                for t in range(T):
                    ins_ = pe.transpose(bank(7)[:, t * P:t * P + P], o_s[:, t, :], ident[:, :])
                ins_.then_inc(o_turned.sem, 1)

            def project(g):
                pe.wait_ge(o_ready.sem, o_ready.at(g, 0))
                for t in range(T):
                    ins_ = pe.matmul(bank(7)[:, t * P:t * P + P], sw["oT"][:, t * P:t * P + P], mat(name + "_Wo"),
                                     start=True, stop=True)
                ins_.then_inc(o_out.sem, 1)

            def turn(b, first):
                g = b + use * B
                q_projection(pe, use, b)
                for u in range(U):
                    if u > 0:
                        scores(b, g, u)
                    if u >= 3:
                        av(b, g, u - 3)
                    elif not first:
                        av(b - 1, g, u - 3)
                    if u >= 2 or not first:
                        turn_probs(g, u - 2)
                    if u == 0:
                        scores(b, g, 0)
                    if u == 3 and not first:
                        turn_o(g)
                    if u == 4 and not first:
                        project(g)

            turn(0, True)
            with pe.Fori(1, B) as b:
                turn(b, False)
            end = (use + 1) * B
            av(B - 1, end, -3)
            turn_probs(end, -2)
            av(B - 1, end, -2)
            turn_probs(end, -1)
            av(B - 1, end, -1)
            pe.wait_ge(o_read.sem, o_read.at(end, -1))
            turn_o(end)
            project(end)

        def attend_scalar(act, step, use, done):
            def probs(g, u):
                s = s_shift[u % 2]
                act.wait_ge(s.sem, s.at(g, u // 2 + 1))
                act.activation(pr_s[:, u % 4], sc_s[:, u % 4], ACT.Exp).then_inc(s_probs.sem, 1)

            def copy_pT(g, u):
                act.wait_ge(s_turned.sem, s_turned.at(g, u + 1))
                need(act, s_av, s_av.at(g, u - 1))
                act.copy(pT_s[:, u % 2, 0:4 * P], bank(4))
                act.copy(pT_s[0:LASTR, u % 2, 4 * P:5 * P], bank(5)[0:LASTR, 0:P])\
                    .then_inc(s_pT.sem, 1)

            def copy_oT(g):
                act.wait_ge(o_turned.sem, o_turned.at(g, 0))
                act.copy(sw["oT"], bank(7)).then_inc(o_ready.sem, 1)

            def turn(b, first):
                g = b + use * B
                evacuate_q(act, use, b)
                for u in range(U):
                    if u >= 2 or not first:
                        copy_pT(g, u - 2)
                    if u == 4 and not first:
                        copy_oT(g)
                    probs(g, u)

            turn(0, True)
            with act.Fori(1, B) as b:
                turn(b, False)
            end = (use + 1) * B
            copy_pT(end, -2)
            copy_pT(end, -1)
            copy_oT(end)

        def attend_vector(dve, step, use, done):
            name = SMALL[use]

            def prepare(b):
                if use > 0:
                    dve.wait_ge(kv_bias, use * B - B + b + 1)
                dve.wait_ge(kv_out, use * B + b + 1)
                dve.tensor_tensor(Kbd[:, b], kT_s[:, b].unsqueeze(1).to_broadcast([P, H, KC]),
                                  head_of_row[:, :].unsqueeze(2).to_broadcast([P, H, KC]), ALU.mult)
                spread_values(dve, b).then_inc(kv_ready.sem, 1)

            def shift(g, u):
                t, half = divmod(u, 2)
                dve.wait_ge(s_scores.sem, s_scores.at(g, u + 1))
                if use == 0:
                    dve.wait_ge(bias_in[t % 2].sem, bias_in[t % 2].at(g, 16 * (t // 2 + 1)))
                else:
                    dve.wait_ge(masked.sem, masked.at(g - B, t + 1))
                need(dve, s_turned, s_turned.at(g, u - 3))
                two = bank(2 * (u % 2), 2).rearrange("p (j n) -> p j n", j=2)[:, :, 0:4 * KC]
                dve.tensor_tensor(sc_s[:, u % 4].rearrange("p (j h) k -> p j (h k)", j=2), two,
                                  bias_s[:, t % 2, half * HH:half * HH + HH].rearrange("p (j h) k -> p j (h k)", j=2),
                                  ALU.add).then_inc(s_read.sem, 1)
                dve.wait_ge(s_read.sem, s_read.at(g, u + 1))
                dve.tensor_reduce(mx_s[:, u % 4], sc_s[:, u % 4], X, ALU.max).then_inc(s_max.sem, 1)
                if not by_pool(use, u):
                    dve.wait_ge(s_max.sem, s_max.at(g, u + 1))
                    subtract_max(dve, g, u)

            def norm_o(g, u):
                t, half = divmod(u % U, 2)
                o9 = bank(6)[:, 0:72].rearrange("p (h e) -> p h e", e=9)
                dve.wait_ge(s_av.sem, s_av.at(g, u + 1))
                if u == 0:
                    need(dve, o_turned, o_turned.at(g, 0))
                dst = o_s[:, t, half * 64:half * 64 + 64].rearrange("p (h e) -> p h e", e=DK)
                step(dve.reciprocal(rec_s[:, u % 2].unsqueeze(2), o9[:, :, 8:9]))
                dve.tensor_tensor(dst, o9[:, :, 0:8], rec_s[:, u % 2].unsqueeze(2).to_broadcast([P, HH, DK]),
                                  ALU.mult).then_inc(s_o.sem, 1)

            def add_input(g, b):
                dve.wait_ge(o_out.sem, o_out.at(g, 0))
                x1b = rn[:, ds(b * T, T), :]
                step(dve.tensor_tensor(x1b, bank(7).rearrange("p (t d) -> p t d", t=T), xn[:, ds(b * T, T), :], ALU.add))
                dve.sem_inc(o_read.sem, 1)
                for t in range(T):
                    step.mark(dve.bn_stats(stat[:, t, :], rn[:, ds(b * T + t, 1), :]))
                step.wait()
                dve.memset(spare[:, :], 0.0)
                for t in range(T):
                    step.mark(dve.bn_aggr(mv[:, t, :], stat[:, t, :]))
                step.wait()
                dve.tensor_scalar(varr[:, 0:T], mv[:, 0:T, 1], EPS, None, ALU.add).then_inc(f_var.sem, 1)

            def norm_x1(g, b):
                dve.wait_ge(f_rstd.sem, f_rstd.at(g, 0))
                for t in range(T):
                    ins_ = dve.tensor_scalar(xn[:, ds(b * T + t, 1), :], rn[:, ds(b * T + t, 1), :], mv[:, t, 0:1],
                                             rstd[:, t:t + 1], ALU.subtract, ALU.mult)
                ins_.then_inc(turn_done, 1)

            def turn(b, first):
                g = b + use * B
                for u in range(U):
                    if u == 0:
                        if not first:
                            norm_o(g, -3)
                        shift(g, 0)
                    else:
                        shift(g, u)
                        if u >= 3 or not first:
                            norm_o(g, u - 3)
                    if first and u in (2, 4, 6):
                        prepare(u // 2)
                    if u == 5 and not first:
                        residual(dve, step, use, done, g, b - 1) if use else add_input(g, b - 1)
                    if u == 7 and not first and not use:
                        norm_x1(g, b - 1)

            dve.wait_ge(ones_set, use + 1)
            prepare(0)
            dve.wait_ge(kv_out, (use + 1) * B)
            turn(0, True)
            with step.loop(B - 1, U + (9 if use == 0 else 1), 1) as b:
                turn(b, False)
            end = (use + 1) * B
            for u in (-3, -2, -1):
                norm_o(end, u)
            if use:
                residual(dve, step, use, done, end, B - 1)
            else:
                add_input(end, B - 1)
                norm_x1(end, B - 1)

        f_turn = Signal(sem("f_turn"), 1)
        f_yT = Signal(sem("f_yT"), 1)
        f_h, f_gelu = Signal(sem("f_h"), NF), Signal(sem("f_gelu"), NF)
        f_out = Signal(sem("f_out"), 1)
        f_read = Signal(sem("f_read"), 1, 1)
        f_var2, f_rstd2 = Signal(sem("f_var2"), 1), Signal(sem("f_rstd2"), 1)


        f_y = Signal(sem("f_y"), 1)

        def ffn0_pool(pool, step, use, done):
            pool.wait_ge(turn_done, done)
            with pool.Fori(0, B) as b:
                pool.wait_ge(f_var2.sem, f_var2.at(b, 1))
                pool.tensor_tensor(rstd[:, 0:T], varr[:, 0:T], expo[:, 0:T], ALU.pow).then_inc(f_rstd2.sem, 1)

        def ffn0_tensor(pe, use, done):
            pe.wait_ge(turn_done, done)
            with pe.Fori(0, B) as b:
                pe.wait_ge(f_y.sem, f_y.at(b, 1))
                for t in range(T):
                    ins_ = pe.transpose(bank(7)[:, t * P:t * P + P], o_s[:, t, :], ident[:, :])
                ins_.then_inc(f_turn.sem, 1)
                pe.wait_ge(f_yT.sem, f_yT.at(b, 1))
                for f in range(NF):
                    pe.matmul(bank(f), mat("L0_xattn_W1", f * P), sw["yT"], start=True, stop=True).then_inc(f_h.sem, 1)
                pe.wait_ge(f_gelu.sem, f_gelu.at(b, NF))
                pe.wait_ge(f_read.sem, f_read.at(b, 0))
                for t in range(T):
                    for f in range(NF):
                        ins_ = pe.matmul(bank(6)[:, t * P:t * P + P], h_s[:, f, t * P:t * P + P],
                                         mat("L0_xattn_W2", f * P), start=(f == 0), stop=(f == NF - 1))
                ins_.then_inc(f_out.sem, 1)

        def ffn0_scalar(act, step, use, done):
            act.wait_ge(turn_done, done)
            with act.Fori(0, B) as b:
                act.copy(o_s, xn[:, ds(b * T, T), :]).then_inc(f_y.sem, 1)
                act.wait_ge(f_turn.sem, f_turn.at(b, 1))
                act.activation(sw["yT"], bank(7), ACT.Identity, scale=col("L0_xattn_g1"), bias=col("L0_xattn_be1"))\
                    .then_inc(f_yT.sem, 1)
                for f in range(NF):
                    act.wait_ge(f_h.sem, f_h.at(b, f + 1))
                    act.activation(h_s[:, f, :], bank(f), ACT.Gelu, bias=col("L0_xattn_b1", f)).then_inc(f_gelu.sem, 1)

        def ffn0_vector(dve, step, use, done):
            dve.sem_inc(f_read.sem, f_read.ahead)
            with step.loop(B, 2 + 2 * T + T + 2) as b:
                dve.wait_ge(turn_done, b + done)
                dve.wait_ge(f_out.sem, f_out.at(b, 1))
                x1b, xb = rn[:, ds(b * T, T), :], x[:, ds(b * T, T), :]
                step(dve.tensor_tensor(x1, bank(6).rearrange("p (t d) -> p t d", t=T), x1b, ALU.add))
                dve.sem_inc(f_read.sem, 1)
                step(dve.tensor_tensor(x1, x1, row("L0_xattn_b2").unsqueeze(1).to_broadcast([P, T, D]), ALU.add))
                for t in range(T):
                    step.mark(dve.bn_stats(stat[:, t, :], x1[:, t, :]))
                step.wait()
                dve.memset(spare[:, :], 0.0)
                for t in range(T):
                    step.mark(dve.bn_aggr(mv[:, t, :], stat[:, t, :]))
                step.wait()
                dve.tensor_scalar(varr[:, 0:T], mv[:, 0:T, 1], EPS, None, ALU.add).then_inc(f_var2.sem, 1)
                dve.wait_ge(f_rstd2.sem, f_rstd2.at(b, 1))
                for t in range(T):
                    step.mark(dve.tensor_scalar(x1[:, t, :], x1[:, t, :], mv[:, t, 0:1], rstd[:, t:t + 1],
                                                ALU.subtract, ALU.mult))
                step.wait()
                step(dve.tensor_tensor(x1, x1, row("L0_xattn_g2").unsqueeze(1).to_broadcast([P, T, D]), ALU.mult))
                step(dve.tensor_tensor(x1, x1, row("L0_xattn_be2").unsqueeze(1).to_broadcast([P, T, D]), ALU.add))
                dve.scalar_tensor_tensor(out=xb, in0=x1, scalar=tg[:, 0:1], in1=xb, op0=ALU.mult,
                                         op1=ALU.add).then_inc(turn_done, 1)

        g_keys = Signal(sem("g_keys"), 2)
        g_scores = Signal(sem("g_scores"), 2 * NCH)
        g_sig = Signal(sem("g_sig"), 2 * NCH)
        g_av = Signal(sem("g_av"), 2)
        g_o = Signal(sem("g_o"), 2)

        def gated_pool(pool, step, use, done):
            values_bias(pool, use)

        def gated_tensor(pe, use, done):
            name = SMALL[use]
            pe.wait_ge(xnT_ready, xnT_count(6))
            pe.wait_ge(kv_out, (use + 1) * B)

            def scores(b, half):
                pe.wait_ge(g_keys.sem, g_keys.at(b, half + 1))
                if half == 0:
                    pe.wait_ge(q_ready.sem, q_ready.at(b + use * B, 1))
                keys = Kbd[:, 0, half * HH:half * HH + HH, :].rearrange("p h k -> p (h k)")
                for c, n in enumerate(rows_of):
                    need(pe, g_sig, g_sig.at(b, half * NCH + c + 1 - NCH))
                    pe.matmul(bank(c)[0:n, :], keys[:, c * P:c * P + n], qT_s, start=True, stop=True)\
                        .then_inc(g_scores.sem, 1)

            def av(b, turn, half):
                pe.wait_ge(g_sig.sem, g_sig.at(turn, NCH * (half + 1)))
                need(pe, g_o, g_o.at(turn, half - 1))
                h = half % 2
                pe.wait_ge(kv_ready.sem, (use + 1) * B)
                for t in range(T):
                    for c, n in enumerate(rows_of):
                        ins_ = pe.matmul(bank(5 + h)[:, t * 72:t * 72 + 72], sigT[0:n, h * NCH + c, t * P:t * P + P],
                                         Vbd[0:n, ds(b, 1), h, c, :, :].rearrange("p a h e -> p (a h) e"),
                                         start=(c == 0), stop=(c == NCH - 1))
                ins_.then_inc(g_av.sem, 1)

            def turn_o(turn):
                pe.wait_ge(g_o.sem, g_o.at(turn, 0))
                for t in range(T):
                    ins_ = pe.transpose(bank(7)[:, t * P:t * P + P], o_s[:, t, :], ident[:, :])
                ins_.then_inc(o_turned.sem, 1)

            def project(g):
                pe.wait_ge(o_ready.sem, o_ready.at(g, 0))
                for t in range(T):
                    ins_ = pe.matmul(bank(7)[:, t * P:t * P + P], sw["oT"][:, t * P:t * P + P], mat(name + "_Wo"),
                                     start=True, stop=True)
                ins_.then_inc(o_out.sem, 1)

            def turn(b, first):
                q_projection(pe, use, b)
                if not first:
                    av(b - 1, b, -1)
                scores(b, 0)
                if not first:
                    turn_o(b)
                scores(b, 1)
                if not first:
                    project(b + use * B)
                av(b, b, 0)

            turn(0, True)
            with pe.Fori(1, B) as b:
                turn(b, False)
            av(B - 1, B, -1)
            pe.wait_ge(o_read.sem, o_read.at((use + 1) * B, -1))
            turn_o(B)
            project((use + 1) * B)

        def gated_scalar(act, step, use, done):
            def copy_oT(g):
                act.wait_ge(o_turned.sem, o_turned.at(g, 0))
                act.copy(sw["oT"], bank(7)).then_inc(o_ready.sem, 1)

            def turn(b, first):
                evacuate_q(act, use, b)
                for u in range(2 * NCH):
                    if u % NCH == 0:
                        need(act, g_av, g_av.at(b, u // NCH - 1))
                    if u == NCH and not first:
                        copy_oT(b + use * B)
                    n = rows_of[u % NCH]
                    act.wait_ge(g_scores.sem, g_scores.at(b, u + 1))
                    act.activation(sigT[0:n, u, :], bank(u % NCH)[0:n, :], ACT.Sigmoid).then_inc(g_sig.sem, 1)

            turn(0, True)
            with act.Fori(1, B) as b:
                turn(b, False)
            copy_oT((use + 1) * B)

        def gated_vector(dve, step, use, done):
            def keys(b, half):
                need(dve, g_scores, g_scores.at(b, NCH * (half - 1)))
                dve.tensor_tensor(Kbd[:, 0, half * HH:half * HH + HH, :],
                                  kT_s[:, ds(b, 1), :].to_broadcast([P, HH, KC]),
                                  head_of_row[:, half * HH:half * HH + HH].unsqueeze(2).to_broadcast([P, HH, KC]),
                                  ALU.mult).then_inc(g_keys.sem, 1)

            def copy_o(turn, half):
                dve.wait_ge(g_av.sem, g_av.at(turn, half + 1))
                if half == 0:
                    need(dve, o_turned, o_turned.at(turn + use * B, 0))
                h = half % 2
                o9 = bank(5 + h)[:, 0:T * 72].rearrange("p (t h e) -> p t h e", t=T, e=9)
                dve.tensor_copy(o_s[:, :, h * 64:h * 64 + 64].rearrange("p t (h e) -> p t h e", e=DK), o9[:, :, :, 0:8])\
                    .then_inc(g_o.sem, 1)

            def turn(b, first):
                for half in range(2):
                    keys(b, half)
                if first:
                    for i in range(B):
                        dve.wait_ge(kv_bias, (use - 1) * B + i + 1)
                        spread_values(dve, i).then_inc(kv_ready.sem, 1)
                else:
                    copy_o(b, -1)
                    residual(dve, step, use, done, b + use * B, b - 1)
                copy_o(b, 0)

            dve.wait_ge(ones_set, use + 1)
            dve.wait_ge(kv_out, (use + 1) * B)
            turn(0, True)
            with step.loop(B - 1, 1, 1) as b:
                turn(b, False)
            copy_o(B, -1)
            residual(dve, step, use, done, (use + 1) * B, B - 1)


        ROUND, ROUNDS = 12, 4
        assert 2 + ROUND * ROUNDS == DESCENT
        R8 = 2 * B
        K_OF = [(NQ * 9 / 8, NQ * 9 / 8), (NQ * 9 / 8, NKV * 9 / 8)]
        k_inv = sb("k_inv", [R8, 2, S])
        k_log = sb("k_log", [R8, 2])
        k_col = sb("k_col", [R8, 2])
        d_s, d_e = sb("d_s", [R8, S]), sb("d_e", [R8, S])
        d_sum = sb("d_sum", [R8, 2])
        d_c, d_m, d_ln = sb("d_c", [R8, 1]), sb("d_m", [R8, 1]), sb("d_ln", [R8, 1])
        col_s = sb("col_s", [P, T, R8])
        col_w = sb("col_w", [P, T, R8])
        d_arg = Signal(sem("d_arg"), ROUNDS + 2)
        d_exp = Signal(sem("d_exp"), ROUNDS + 2)
        d_total = Signal(sem("d_total"), ROUNDS + 1)
        d_log = Signal(sem("d_log"), ROUNDS + 1)
        c_turned, c_read = sem("c_turned"), sem("c_read")
        b_spread, b_read = sem("b_spread"), sem("b_read")

        def descent_vector(dve, step, which, bc, nrow):
            k1 = lambda: k_inv[:, which, :]
            dve.wait_ge(logits_ready, which + 1)
            step(dve.tensor_copy(d_s[:, :], bank(2)[0:R8, :]))
            step(dve.tensor_scalar(d_c[:, :], k_log[:, which:which + 1], -1.0, float(np.log(S)), ALU.mult, ALU.add))
            step(dve.tensor_scalar(d_e[:, :], d_s[:, :], d_c[:, :], None, ALU.min))
            step(dve.tensor_reduce(d_m[:, :], d_e[:, :], X, ALU.max))
            dve.tensor_scalar(d_e[:, :], d_e[:, :], d_m[:, :], None, ALU.subtract).then_inc(d_arg.sem, 1)
            dve.wait_ge(d_exp.sem, d_exp.at(which, 1))
            dve.tensor_reduce(d_sum[:, 0:1], d_e[:, :], X, ALU.add).then_inc(d_total.sem, 1)
            dve.wait_ge(d_log.sem, d_log.at(which, 1))
            step(dve.tensor_tensor(d_c[:, :], d_m[:, :], d_ln[:, :], ALU.add))
            with step.loop(ROUNDS, ROUND + 2) as r:
                step(dve.tensor_scalar(d_e[:, :], d_s[:, :], d_c[:, :], 60.0, ALU.subtract, ALU.min))
                dve.sem_inc(d_arg.sem, 1)
                dve.wait_ge(d_exp.sem, r + d_exp.at(which, 2))
                total = k_col[:, which:which + 1]
                for i in range(ROUND):
                    nxt = d_sum[:, i % 2:i % 2 + 1]
                    step(dve.scalar_tensor_tensor(out=junk[0:R8, :], in0=d_e[:, :], scalar=total, in1=k1(),
                                                  op0=ALU.min, op1=ALU.mult, accum_out=nxt))
                    total = nxt
                dve.sem_inc(d_total.sem, 1)
                dve.wait_ge(d_log.sem, r + d_log.at(which, 2))
                step(dve.tensor_tensor(d_c[:, :], d_c[:, :], d_ln[:, :], ALU.add))
            dve.tensor_scalar(d_e[:, :], d_s[:, :], d_c[:, :], 0.0, ALU.subtract, ALU.min).then_inc(d_arg.sem, 1)
            dve.wait_ge(c_turned, which + 1)
            dve.tensor_copy(col_s[:, :, :], bank(3)[:, 0:T * R8].rearrange("p (t r) -> p t r", t=T)).then_inc(c_read, 1)
            dve.wait_ge(c_read, which + 1)
            step(dve.tensor_scalar(col_w[:, :, :], col_s[:, :, :], -1.0, 1.0, ALU.mult, ALU.add))
            dve.tensor_tensor(col_w[:, :, :], col_w[:, :, :], col_s[:, :, :], ALU.add).then_inc(w_ready, 1)
            for r in range(nrow):
                dve.wait_ge(b_spread, which * B + r + 1)
                ins_ = dve.tensor_copy(bc[:, r, :], bank(4 + r % 2))
                ins_.then_inc(b_read, 1)
            dve.wait_ge(b_read, which * B + nrow)

        w_ready = sem("w_ready")

        def descent_scalar(act, which):
            def exp(value, wait, **kw):
                act.wait_ge(d_arg.sem, wait)
                act.activation(value, d_e[:, :], ACT.Exp, **kw).then_inc(d_exp.sem, 1)

            def log(wait, i):
                act.wait_ge(d_total.sem, wait)
                act.activation(d_ln[:, :], d_sum[:, i:i + 1], ACT.Ln, scale=k_inv[:, which, 0:1]).then_inc(d_log.sem, 1)

            exp(d_e[:, :], d_arg.at(which, 1))
            log(d_total.at(which, 1), 0)
            with act.Fori(0, ROUNDS) as r:
                exp(d_e[:, :], r + d_arg.at(which, 2), bias=k_log[:, which:which + 1])
                log(r + d_total.at(which, 2), (ROUND - 1) % 2)
            exp(d_e[:, :], d_arg.at(which, ROUNDS + 2))

        def descent_tensor(pe, which, nrow):
            pe.wait_ge(d_exp.sem, d_exp.at(which, ROUNDS + 2))
            for t in range(T):
                ins_ = pe.transpose(bank(3)[:, t * R8:t * R8 + R8], d_e[:, t * P:t * P + P], ident[0:R8, 0:R8])
            ins_.then_inc(c_turned, 1)
            for r in range(nrow):
                if r >= 2:
                    pe.wait_ge(b_read, which * B + r - 1)
                pe.matmul(bank(4 + r % 2), row_of[:, r, :], d_e[:, :], start=True, stop=True).then_inc(b_spread, 1)

        def rank_tile(dve, step, bc, r, t):
            score = col_s[:, t, ds(r, 1)]
            step(dve.tensor_scalar(junk[:, :], bc[:, ds(r, 1), :], score, 0.0, ALU.is_gt, ALU.add,
                                   accum_out=over[:, t:t + 1]))
            step(dve.scalar_tensor_tensor(out=junk[:, :], in0=bc[:, ds(r, 1), :], scalar=score, in1=earlier[:, t, :],
                                          op0=ALU.is_equal, op1=ALU.mult, accum_out=ties[:, t:t + 1]))

        def place_tokens(dve, step, place, n):
            step(dve.tensor_tensor(over[:, :], over[:, :], ties[:, :], ALU.add))
            for t in range(T):
                step.mark(dve.tensor_scalar(place[:, t, :], slot_no[:, 0:n], over[:, t:t + 1], None, ALU.is_equal))
            step.wait()

        def rank_and_place(dve, step, bc, r, place, n):
            for t in range(T):
                rank_tile(dve, step, bc, r, t)
            place_tokens(dve, step, place, n)

        RANK_STEPS = 3 * T + 1
        over, ties = sb("over", [P, T]), sb("ties", [P, T])

        rw = carve({"bc": B * S, "place": T * NQ, "rn": T * D, "w": T, "ws": 1, "xg": NQ, "placeT": T * P, "hl": S,
                    "hh": NF * NQ, "routed": D, "sum": T * D})
        bc0 = rw["bc"].rearrange("p (r q) -> p r q", r=B)
        place0 = rw["place"].rearrange("p (t i) -> p t i", t=T)
        rn0 = rw["rn"].rearrange("p (t d) -> p t d", t=T)
        hh = rw["hh"].rearrange("p (f i) -> p f i", f=NF)
        sum0 = rw["sum"].rearrange("p (t d) -> p t d", t=T)
        r_copied = Signal(sem("r_copied"), 1)
        r_placed = Signal(sem("r_placed"), 1)
        r_gath = Signal(sem("r_gath"), 1)
        r_light = Signal(sem("r_light"), 1)
        r_lgelu = Signal(sem("r_lgelu"), 1)
        r_xg = Signal(sem("r_xg"), 1)
        r_h = Signal(sem("r_h"), 1)
        r_hgelu = Signal(sem("r_hgelu"), 1)
        r_heavy = Signal(sem("r_heavy"), 1)
        r_routed = Signal(sem("r_routed"), 1)
        r_out = Signal(sem("r_out"), 1)

        def route0_pool(pool, step, use, done):
            pool.wait_ge(w_ready, 1)
            with pool.Fori(0, B) as b:
                pool.wait_ge(turn_done, b + done)
                pool.tensor_copy(rn0, rn[:, ds(b * T, T), :])
                pool.tensor_copy(rw["w"].unsqueeze(2), col_w[:, :, ds(b, 1)]).then_inc(r_copied.sem, 1)

        def route0_tensor(pe, use, done):
            pe.wait_ge(mats_loaded[1], 16)
            descent_tensor(pe, 0, B)
            pe.wait_ge(xnT_ready, xnT_count(1))
            pe.wait_ge(b_read, B)
            with pe.Fori(0, B) as b:
                pe.wait_ge(turn_done, b + done)
                pe.matmul(bank(3)[0:64, :], mat("L0_ffn_w1_l", 0, 64), xnT[:, ds(b * S, S)], start=True, stop=True)\
                    .then_inc(r_light.sem, 1)
                pe.wait_ge(r_copied.sem, r_copied.at(b, 1))
                pe.wait_ge(r_placed.sem, r_placed.at(b, 1))
                for t in range(T):
                    pe.matmul(bank(0)[:, 0:NQ], rn0[:, t, :], place0[:, t, :], start=(t == 0), stop=(t == T - 1))
                for t in range(T):
                    pe.matmul(bank(1)[:, 0:1], place0[:, t, :], rw["w"][:, t:t + 1], start=(t == 0), stop=(t == T - 1))
                for t in range(T):
                    ins_ = pe.transpose(bank(2)[:, t * P:t * P + P], place0[:, t, :], ident[:, :])
                ins_.then_inc(r_gath.sem, 1)
                pe.wait_ge(r_xg.sem, r_xg.at(b, 1))
                for f in range(NF):
                    ins_ = pe.matmul(bank(4)[:, f * P:f * P + P], mat("L0_ffn_w1_h", f * P), rw["xg"],
                                     start=True, stop=True)
                ins_.then_inc(r_h.sem, 1)
                pe.wait_ge(r_hgelu.sem, r_hgelu.at(b, 1))
                for f in range(NF):
                    ins_ = pe.matmul(bank(5)[:, 0:D], hh[:, f, :], mat("L0_ffn_w2_h", f * P),
                                     start=(f == 0), stop=(f == NF - 1))
                ins_.then_inc(r_heavy.sem, 1)
                pe.wait_ge(r_lgelu.sem, r_lgelu.at(b, 1))
                pe.wait_ge(r_routed.sem, r_routed.at(b, 1))
                for t in range(T):
                    pe.matmul(bank(6)[:, t * P:t * P + P], rw["hl"][0:64, t * P:t * P + P],
                              mat("L0_ffn_w2_l", 0, D, 64), start=True, stop=False)
                    ins_ = pe.matmul(bank(6)[:, t * P:t * P + P], rw["placeT"][:, t * P:t * P + P], rw["routed"],
                                     start=False, stop=True)
                ins_.then_inc(r_out.sem, 1)

        def route0_scalar(act, step, use, done):
            descent_scalar(act, 0)
            with act.Fori(0, B) as b:
                act.wait_ge(turn_done, b + done)
                act.wait_ge(r_gath.sem, r_gath.at(b, 1))
                act.mul(rw["xg"], bank(0)[:, 0:NQ], col("L0_ffn_gamma_h"))
                act.copy(rw["placeT"], bank(2)).then_inc(r_xg.sem, 1)
                act.wait_ge(r_light.sem, r_light.at(b, 1))
                act.activation(rw["hl"][0:64, :], bank(3)[0:64, :], ACT.Gelu, bias=col("L0_ffn_b1_l", 0, 64))\
                    .then_inc(r_lgelu.sem, 1)
                act.wait_ge(r_h.sem, r_h.at(b, 1))
                for f in range(NF):
                    ins_ = act.activation(hh[:, f, :], bank(4)[:, f * P:f * P + P], ACT.Gelu,
                                          bias=col("L0_ffn_b1_h", f))
                ins_.then_inc(r_hgelu.sem, 1)

        def route0_vector(dve, step, use, done):
            descent_vector(dve, step, 0, bc0, B)
            with step.loop(B, RANK_STEPS + 2) as b:
                dve.wait_ge(turn_done, b + done)
                rank_and_place(dve, step, bc0, b, place0, NQ)
                dve.sem_inc(r_placed.sem, 1)
                dve.wait_ge(r_gath.sem, r_gath.at(b, 1))
                dve.tensor_copy(rw["ws"], bank(1)[:, 0:1])
                dve.wait_ge(r_heavy.sem, r_heavy.at(b, 1))
                step(dve.tensor_tensor(rw["routed"], bank(5)[:, 0:D], row("L0_ffn_b2_h"), ALU.add))
                dve.tensor_scalar(rw["routed"], rw["routed"], rw["ws"], None, ALU.mult).then_inc(r_routed.sem, 1)
                dve.wait_ge(r_out.sem, r_out.at(b, 1))
                step(dve.tensor_tensor(sum0, bank(6).rearrange("p (t d) -> p t d", t=T),
                                       row("L0_ffn_b2_l").unsqueeze(1).to_broadcast([P, T, D]), ALU.add))
                xb = x[:, ds(b * T, T), :]
                dve.scalar_tensor_tensor(out=xb, in0=sum0, scalar=tg[:, 4:5], in1=xb, op0=ALU.mult, op1=ALU.add)\
                    .then_inc(turn_done, 1)

        aw = carve({"qT": NBLK * S, "kT": NBLK * NKEY, "v": 5 * H * DH, "ctx": KC, "pr": 2 * NKEY, "pT": 2 * 5 * P,
                    "nm": 4, "sums": T * H, "rec": 4, "o": T * H * DH, "sum": T * D})
        qT_a = aw["qT"].rearrange("p (i q) -> p i q", i=NBLK)
        kT_a = aw["kT"].rearrange("p (i k) -> p i k", i=NBLK)
        v_a = aw["v"].rearrange("p (c n) -> p c n", c=5)
        pr_a = aw["pr"].rearrange("p (n k) -> p n k", n=2)
        pT_a = aw["pT"].rearrange("p (n k) -> p n k", n=2)
        o_a = aw["o"].rearrange("p (t n) -> p t n", t=T)
        oT_a = qT_a
        sum_a = aw["sum"].rearrange("p (t d) -> p t d", t=T)
        ITEMS = [("q", i) for i in range(NBLK)] + [("k", i) for i in range(NBLK)] + [("km", 0), ("km", 1)] + \
                [("v", i) for i in range(2 * T)] + [("vm", 0), ("vm", 1)]
        HALF_ITEMS = len(ITEMS) // 2
        UA = T * H
        GA = UA // 4
        a_in = Signal(sem("a_in"), 1)
        a_proj = Signal(sem("a_proj"), len(ITEMS))
        a_even = Signal(sem("a_even"), HALF_ITEMS)
        a_odd = Signal(sem("a_odd"), HALF_ITEMS)
        a_scores = Signal(sem("a_scores"), UA)
        a_max = Signal(sem("a_max"), UA)
        a_probs = Signal(sem("a_probs"), UA)
        a_turned = Signal(sem("a_turned"), UA)
        a_pT = Signal(sem("a_pT"), UA)
        a_av = Signal(sem("a_av"), UA)
        a_o = Signal(sem("a_o"), GA)
        a_oturn = Signal(sem("a_oturn"), NBLK)
        a_oe = Signal(sem("a_oe"), NBLK // 2)
        a_oo = Signal(sem("a_oo"), NBLK // 2)
        a_out = Signal(sem("a_out"), 1)
        key_rows = [P] * T + [KC]

        def self_pool(pool, step, use, done):
            pool.wait_ge(xnT_ready, xnT_count(TWICE))
            with pool.Fori(0, B) as b:
                pool.wait_ge(turn_done, b + done)
                pool.tensor_copy(x_in[:, :], xnT[:, ds(b * S, S)])
                pool.tensor_copy(aw["ctx"].unsqueeze(1), ctxT[:, ds(b, 1), :]).then_inc(a_in.sem, 1)

        def item_place(kind, i, n):
            to = bank(n % 8)
            if kind == "q":
                return to, qT_a[:, i, :]
            if kind == "k":
                return to, kT_a[:, i, 0:S]
            if kind == "km":
                return to[:, 0:4 * KC].rearrange("p (j k) -> p j k", j=4), kT_a[:, 4 * i:4 * i + 4, S:NKEY]
            if kind == "v":
                return to, v_a[:, i // 2, (i % 2) * S:(i % 2) * S + S]
            return to[0:KC, :], v_a[0:KC, T, i * S:i * S + S]

        def self_tensor(pe, use, done):
            pe.wait_ge(mats_loaded[2], 16)

            def item(g, n):
                kind, i = ITEMS[n]
                to, _ = item_place(kind, i, n)
                if n >= 8:
                    s = (a_even, a_odd)[n % 2]
                    pe.wait_ge(s.sem, s.at(g, (n - 8) // 2 + 1))
                if kind in "qk":
                    ins_ = pe.matmul(to, mat("L1_xattn_W" + kind, i * P), x_in[:, :], start=True, stop=True)
                elif kind == "km":
                    for j in range(4):
                        ins_ = pe.matmul(to[:, j, :], mat("L1_xattn_Wm", (4 * i + j) * P), aw["ctx"],
                                         start=True, stop=True)
                elif kind == "v":
                    ins_ = pe.matmul(to, x_in[:, (i // 2) * P:(i // 2) * P + P], mat("L1_xattn_Wv", (i % 2) * S, S),
                                     start=True, stop=True)
                else:
                    ins_ = pe.matmul(to, aw["ctx"], mat("L1_xattn_Wm", i * S, S), start=True, stop=True)
                ins_.then_inc(a_proj.sem, 1)

            def scores(g, u):
                t, h = divmod(u, H)
                if u >= 2:
                    pe.wait_ge(a_probs.sem, a_probs.at(g, u - 1))
                at = slice(DH * (h % 2), DH * (h % 2) + DH)
                q = qT_a[at, h // 2, t * P:t * P + P]
                pe.matmul(bank(2 * (u % 2)), q, kT_a[at, h // 2, 0:S], start=True, stop=True)
                pe.matmul(bank(2 * (u % 2) + 1)[:, 0:KC], q, kT_a[at, h // 2, S:NKEY], start=True, stop=True)\
                    .then_inc(a_scores.sem, 1)

            def turn_probs(g, u):
                pe.wait_ge(a_probs.sem, a_probs.at(g, u + 1))
                if u >= 1:
                    pe.wait_ge(a_pT.sem, a_pT.at(g, u))
                for c, n in enumerate(key_rows):
                    to = bank(4)[:, c * P:c * P + P] if c < T else bank(5)[0:n, 0:P]
                    ins_ = pe.transpose(to, pr_a[:, u % 2, c * P:c * P + n], ident[:, :])
                ins_.then_inc(a_turned.sem, 1)

            def av(g, u):
                h, group = u % H, u // 4
                pe.wait_ge(a_pT.sem, a_pT.at(g, u + 1))
                if u % 4 == 0 and group >= 2:
                    pe.wait_ge(a_o.sem, a_o.at(g, group - 1))
                for c, n in enumerate(key_rows):
                    ins_ = pe.matmul(bank(6 + group % 2)[:, (u % 4) * DH:(u % 4) * DH + DH],
                                     pT_a[0:n, u % 2, c * P:c * P + P], v_a[0:n, c, h * DH:h * DH + DH],
                                     start=(c == 0), stop=(c == T))
                ins_.then_inc(a_av.sem, 1)

            with pe.Fori(0, B) as b:
                pe.wait_ge(turn_done, b + done)
                pe.wait_ge(a_in.sem, a_in.at(b, 1))
                for n in range(len(ITEMS)):
                    item(b, n)
                pe.wait_ge(a_even.sem, a_even.at(b, HALF_ITEMS))
                pe.wait_ge(a_odd.sem, a_odd.at(b, HALF_ITEMS))
                for u in range(UA + 2):
                    if u < UA:
                        scores(b, u)
                    if u >= 2:
                        av(b, u - 2)
                    if 1 <= u <= UA:
                        turn_probs(b, u - 1)
                pe.wait_ge(a_o.sem, a_o.at(b, GA))
                for i in range(NBLK):
                    for t in range(T):
                        ins_ = pe.transpose(bank(i)[:, t * P:t * P + P], o_a[:, t, i * P:i * P + P], ident[:, :])
                    ins_.then_inc(a_oturn.sem, 1)
                pe.wait_ge(a_oe.sem, a_oe.at(b, NBLK // 2))
                pe.wait_ge(a_oo.sem, a_oo.at(b, NBLK // 2))
                for t in range(T):
                    for i in range(NBLK):
                        ins_ = pe.matmul(bank(0)[:, t * P:t * P + P], oT_a[:, i, t * P:t * P + P],
                                         mat("L1_xattn_Wo", i * P), start=(i == 0), stop=(i == NBLK - 1))
                ins_.then_inc(a_out.sem, 1)

        def self_scalar(act, step, use, done):
            with act.Fori(0, B) as b:
                act.wait_ge(turn_done, b + done)
                for n in range(0, len(ITEMS), 2):
                    src, dst = item_place(*ITEMS[n], n)
                    act.wait_ge(a_proj.sem, a_proj.at(b, n + 1))
                    (act.mul(dst, src, DH ** -0.5) if ITEMS[n][0] == "q" else act.copy(dst, src)).then_inc(a_even.sem, 1)
                for u in range(UA):
                    act.wait_ge(a_max.sem, a_max.at(b, u + 1))
                    if u >= 2:
                        act.wait_ge(a_turned.sem, a_turned.at(b, u - 1))
                    act.activation(pr_a[:, u % 2], bank(2 * (u % 2), 2)[:, 0:NKEY], ACT.Exp,
                                   bias=aw["nm"][:, u % 4:u % 4 + 1], accum_out=aw["sums"][:, u:u + 1])\
                        .then_inc(a_probs.sem, 1)
                for i in range(0, NBLK, 2):
                    act.wait_ge(a_oturn.sem, a_oturn.at(b, i + 1))
                    act.copy(oT_a[:, i, :], bank(i)).then_inc(a_oe.sem, 1)

        def self_vector(dve, step, use, done):
            def max_of(g, u):
                dve.wait_ge(a_scores.sem, a_scores.at(g, u + 1))
                dve.tensor_reduce(aw["nm"][:, u % 4:u % 4 + 1], bank(2 * (u % 2), 2)[:, 0:NKEY], X, ALU.max,
                                  negate=True).then_inc(a_max.sem, 1)

            def copy_pT(g, u):
                dve.wait_ge(a_turned.sem, a_turned.at(g, u + 1))
                if u >= 2:
                    dve.wait_ge(a_av.sem, a_av.at(g, u - 1))
                dve.tensor_copy(pT_a[:, u % 2, 0:T * P], bank(4))
                dve.tensor_copy(pT_a[0:KC, u % 2, T * P:T * P + P], bank(5)[0:KC, 0:P]).then_inc(a_pT.sem, 1)

            def norm_o(g, i):
                t, j = divmod(i, 4)
                dve.wait_ge(a_av.sem, a_av.at(g, 4 * i + 4))
                step(dve.reciprocal(aw["rec"], aw["sums"][:, 4 * i:4 * i + 4]))
                dve.tensor_tensor(o_a[:, t, j * 4 * DH:(j + 1) * 4 * DH].rearrange("p (h e) -> p h e", h=4),
                                  bank(6 + i % 2)[:, 0:4 * DH].rearrange("p (h e) -> p h e", h=4),
                                  aw["rec"].unsqueeze(2).to_broadcast([P, 4, DH]), ALU.mult).then_inc(a_o.sem, 1)

            with step.loop(B, GA + 1) as b:
                dve.wait_ge(turn_done, b + done)
                for n in range(1, len(ITEMS), 2):
                    src, dst = item_place(*ITEMS[n], n)
                    dve.wait_ge(a_proj.sem, a_proj.at(b, n + 1))
                    if ITEMS[n][0] == "q":
                        dve.tensor_scalar(dst, src, DH ** -0.5, None, ALU.mult).then_inc(a_odd.sem, 1)
                    else:
                        dve.tensor_copy(dst, src).then_inc(a_odd.sem, 1)
                for u in range(UA + 3):
                    if u < UA:
                        max_of(b, u)
                    if 1 <= u <= UA:
                        copy_pT(b, u - 1)
                    if u >= 6 and (u - 6) % 4 == 0:
                        norm_o(b, (u - 6) // 4)
                for i in range(1, NBLK, 2):
                    dve.wait_ge(a_oturn.sem, a_oturn.at(b, i + 1))
                    dve.tensor_copy(oT_a[:, i, :], bank(i)).then_inc(a_oo.sem, 1)
                dve.wait_ge(a_out.sem, a_out.at(b, 1))
                step(dve.tensor_tensor(sum_a, bank(0).rearrange("p (t d) -> p t d", t=T),
                                       row("L1_xattn_bo").unsqueeze(1).to_broadcast([P, T, D]), ALU.add))
                xb = x[:, ds(b * T, T), :]
                dve.scalar_tensor_tensor(out=xb, in0=sum_a, scalar=tg[:, 1:2], in1=xb, op0=ALU.mult, op1=ALU.add)\
                    .then_inc(turn_done, 1)
        NKC = NKV // P
        lw = carve({"bc": R8 * S, "placeq": T * NQ, "placek": T * NKV, "rn": T * D, "w": T * 2, "ws": 1 + NKC,
                    "qT": NBF * S, "kT": NBF * S, "v": T * HF * DH, "pr": 4 * 4 * P, "pT": 2 * 4 * P, "nm": 4 * 4,
                    "sums": 4 * 4, "rec": 2 * 4, "o": T * HF * DH, "placeT": T * P, "xq": NQ, "xk": NKV,
                    "kh": NBF * NKV, "qh": NBF * NQ, "vh": NKC * HF * DH, "routed": D})
        bc1 = lw["bc"].rearrange("p (r q) -> p r q", r=R8)
        placeq = lw["placeq"].rearrange("p (t i) -> p t i", t=T)
        placek = lw["placek"].rearrange("p (t i) -> p t i", t=T)
        rn1 = lw["rn"].rearrange("p (t d) -> p t d", t=T)
        w1 = lw["w"].rearrange("p (k t) -> p t k", k=2)
        qT_l = lw["qT"].rearrange("p (i q) -> p i q", i=NBF)
        kT_l = lw["kT"].rearrange("p (i q) -> p i q", i=NBF)
        v_l = lw["v"].rearrange("p (t n) -> p t n", t=T)
        pr_l = lw["pr"].rearrange("p (n k) -> p n k", n=4)
        pT_l = lw["pT"].rearrange("p (n k) -> p n k", n=2)
        nm_l = lw["nm"].rearrange("p (n k) -> p n k", n=4)
        sums_l = lw["sums"].rearrange("p (n k) -> p n k", n=4)
        rec_l = lw["rec"].rearrange("p (n k) -> p n k", n=2)
        o_l = lw["o"].rearrange("p (t n) -> p t n", t=T)
        oT_l = qT_l
        kh = lw["kh"].rearrange("p (i k) -> p i k", i=NBF)
        qh = lw["qh"].rearrange("p (i q) -> p i q", i=NBF)
        vh = lw["vh"].rearrange("p (c n) -> p c n", c=NKC)
        oh, ohT = lw["placek"][:, 0:HF * DH], lw["placeq"]
        LITEMS = [("q", i) for i in range(NBF)] + [("k", i) for i in range(NBF)] + [("v", i) for i in range(T)]
        ITEM_BANK = [0, 1, 3, 4, 5, 6, 7, 2]
        HL = len(LITEMS) // 2
        UL, UH = 2 * T, 4
        UT = UL + UH
        l_x = Signal(sem("l_x"), 1)
        l_rn = Signal(sem("l_rn"), 1)
        l_proj = Signal(sem("l_proj"), len(LITEMS), 1)
        l_even, l_odd = Signal(sem("l_even"), HL), Signal(sem("l_odd"), HL)
        l_placed = Signal(sem("l_placed"), 1)
        l_gath = Signal(sem("l_gath"), 1, 1)
        l_gx, l_gturn = Signal(sem("l_gx"), 1), Signal(sem("l_gturn"), 1)
        l_hproj = Signal(sem("l_hproj"), 5)
        l_ha, l_hd = Signal(sem("l_ha"), 2), Signal(sem("l_hd"), 3)
        l_scores, l_max = Signal(sem("l_scores"), UT), Signal(sem("l_max"), UT)
        l_probs, l_turned = Signal(sem("l_probs"), UT, 4), Signal(sem("l_turned"), UT, 4)
        l_pT = Signal(sem("l_pT"), UT, 4)
        l_av, l_o = Signal(sem("l_av"), UT, 4), Signal(sem("l_o"), UT, 4)
        l_oturn, l_oT = Signal(sem("l_oturn"), NBF + 1), Signal(sem("l_oT"), NBF + 1)
        l_light = Signal(sem("l_light"), 1)
        l_added = Signal(sem("l_added"), 1, 1)
        l_heavy, l_routed = Signal(sem("l_heavy"), 1), Signal(sem("l_routed"), 1)
        l_out = Signal(sem("l_out"), 1)

        def blocks_of(u):
            if u < UL:
                return [(2 * i + u % 2, 0) for i in range(4)], u // 2
            j = u - UL
            return [(4 * (j // 2) + 2 * i + j % 2, c) for i in range(2) for c in range(NKC)], None

        def route1_pool(pool, step, use, done):
            pool.wait_ge(w_ready, 2)
            pool.wait_ge(xnT_ready, xnT_count(3))
            with pool.Fori(0, B) as b:
                pool.wait_ge(l_proj.sem, l_proj.at(b, 0))
                pool.tensor_copy(x_in[:, :], xnT[:, ds(b * S, S)]).then_inc(l_x.sem, 1)
                pool.wait_ge(l_gath.sem, l_gath.at(b, 0))
                pool.tensor_copy(rn1, rn[:, ds(b * T, T), :])
                for kind in range(2):
                    ins_ = pool.tensor_copy(w1[:, :, kind:kind + 1], col_w[:, :, ds(b + kind * B, 1)])
                ins_.then_inc(l_rn.sem, 1)

        def route1_tensor(pe, use, done):
            pe.wait_ge(mats_loaded[3], 16)
            for s in (l_proj, l_gath, l_turned, l_av):
                pe.sem_inc(s.sem, s.ahead)
            descent_tensor(pe, 1, R8)
            pe.wait_ge(b_read, B + R8)

            def items(b):
                pe.wait_ge(l_x.sem, l_x.at(b, 1))
                for n, (kind, i) in enumerate(LITEMS):
                    if n == 6:
                        pe.wait_ge(l_added.sem, l_added.at(b, 0))
                    if n == 7:
                        pe.wait_ge(turn_done, b + done)
                    if n >= 8:
                        s = (l_even, l_odd)[n % 2]
                        pe.wait_ge(s.sem, s.at(b, (n - 8) // 2 + 1))
                    to = bank(ITEM_BANK[n % 8])
                    if kind == "v":
                        ins_ = pe.matmul(to, x_in[:, i * P:i * P + P], mat("L1_ffn_wv_light", 0, HF * DH),
                                         start=True, stop=True)
                    else:
                        ins_ = pe.matmul(to, mat(f"L1_ffn_w{kind}_light", i * P), x_in[:, :], start=True, stop=True)
                    ins_.then_inc(l_proj.sem, 1)
                pe.wait_ge(l_even.sem, l_even.at(b, HL))
                pe.wait_ge(l_odd.sem, l_odd.at(b, HL))

            def scores(b, u):
                pe.wait_ge(l_probs.sem, l_probs.at(b, u - 1))
                if u == UL:
                    pe.wait_ge(l_ha.sem, l_ha.at(b, 2))
                    pe.wait_ge(l_hd.sem, l_hd.at(b, 1))
                blocks, w = blocks_of(u)
                for i in range(4 if u < UL else 2):
                    h = blocks[i * (1 if u < UL else NKC)][0]
                    at = slice(DH * (h % 2), DH * (h % 2) + DH)
                    if u < UL:
                        q, k, n = qT_l[at, h // 2, w * P:w * P + P], kT_l[at, h // 2, w * P:w * P + P], P
                    else:
                        q, k, n = qh[at, h // 2, :], kh[at, h // 2, :], NKV
                    ins_ = pe.matmul(bank(u % 2)[:, i * n:i * n + n], q, k, start=True, stop=True)
                ins_.then_inc(l_scores.sem, 1)

            def turn_probs(b, u):
                pe.wait_ge(l_probs.sem, l_probs.at(b, u + 1))
                pe.wait_ge(l_pT.sem, l_pT.at(b, u - 1))
                for i in range(4):
                    ins_ = pe.transpose(bank(4 + u % 2)[:, i * P:i * P + P], pr_l[:, u % 4, i * P:i * P + P], ident[:, :])
                ins_.then_inc(l_turned.sem, 1)

            def av(b, u):
                pe.wait_ge(l_pT.sem, l_pT.at(b, u + 1))
                pe.wait_ge(l_o.sem, l_o.at(b, u))
                if u == UL:
                    pe.wait_ge(l_hd.sem, l_hd.at(b, 3))
                blocks, w = blocks_of(u)
                for i, (h, c) in enumerate(blocks):
                    v = v_l[:, w, h * DH:h * DH + DH] if u < UL else vh[:, c, h * DH:h * DH + DH]
                    j = i if u < UL else i // NKC
                    ins_ = pe.matmul(bank(6)[:, j * DH:j * DH + DH], pT_l[:, u % 2, i * P:i * P + P], v,
                                     start=(u < UL or c == 0), stop=(u < UL or c == NKC - 1))
                ins_.then_inc(l_av.sem, 1)

            def gather(b):
                pe.wait_ge(l_placed.sem, l_placed.at(b, 1))
                pe.wait_ge(l_rn.sem, l_rn.at(b, 1))
                for t in range(T):
                    pe.matmul(bank(2)[:, 0:NQ], rn1[:, t, :], placeq[:, t, :], start=(t == 0), stop=(t == T - 1))
                for t in range(T):
                    pe.matmul(bank(2)[:, NQ:NQ + NKV], rn1[:, t, :], placek[:, t, :], start=(t == 0), stop=(t == T - 1))
                for j in range(1 + NKC):
                    for t in range(T):
                        place = placeq[:, t, :] if j == 0 else placek[:, t, (j - 1) * P:j * P]
                        pe.matmul(bank(2)[:, NQ + NKV + j:NQ + NKV + j + 1], place,
                                  w1[:, t, 0:1] if j == 0 else w1[:, t, 1:2], start=(t == 0), stop=(t == T - 1))
                for t in range(T):
                    ins_ = pe.transpose(bank(3)[:, t * P:t * P + P], placeq[:, t, :], ident[:, :])
                ins_.then_inc(l_gath.sem, 1)

            def routed_keys(b, pair):
                for j in range(2):
                    ins_ = pe.matmul(bank(2 + pair)[:, j * NKV:j * NKV + NKV],
                                     mat("L1_ffn_wk_heavy", (2 * pair + j) * P), lw["xk"], start=True, stop=True)
                ins_.then_inc(l_hproj.sem, 1)

            def routed_values(b, c, to):
                pe.matmul(to, lw["xk"][:, c * P:c * P + P], mat("L1_ffn_wv_heavy", 0, HF * DH), start=True, stop=True)\
                    .then_inc(l_hproj.sem, 1)

            def projections(b, u):
                if u == 5:
                    pe.wait_ge(l_gx.sem, l_gx.at(b, 1))
                    for i in range(NBF):
                        ins_ = pe.matmul(bank(7)[:, i * NQ:i * NQ + NQ], mat("L1_ffn_wq_heavy", i * P), lw["xq"],
                                         start=True, stop=True)
                    ins_.then_inc(l_hproj.sem, 1)
                    routed_keys(b, 0)
                if u == 6:
                    pe.wait_ge(l_gturn.sem, l_gturn.at(b, 1))
                    routed_keys(b, 1)
                    pe.wait_ge(l_ha.sem, l_ha.at(b, 1))
                    routed_values(b, 0, bank(7))
                if u == 7:
                    pe.wait_ge(l_ha.sem, l_ha.at(b, 2))
                    routed_values(b, 1, bank(2))

            def turn_block(b, i):
                if i == 0:
                    pe.wait_ge(l_o.sem, l_o.at(b, UL))
                    pe.wait_ge(l_hd.sem, l_hd.at(b, 3))
                if i >= 2:
                    pe.wait_ge(l_oT.sem, l_oT.at(b, i - 1))
                for t in range(T):
                    ins_ = pe.transpose(bank(2 + i % 2)[:, t * P:t * P + P], o_l[:, t, i * P:i * P + P], ident[:, :])
                ins_.then_inc(l_oturn.sem, 1)

            with pe.Fori(0, B) as b:
                items(b)
                for u in range(UT + 3):
                    if u < UT:
                        scores(b, u)
                    if u >= 3:
                        av(b, u - 3)
                    if 2 <= u < UT + 2:
                        turn_probs(b, u - 2)
                    if u == 4:
                        gather(b)
                    projections(b, u)
                    if 10 <= u < 10 + NBF:
                        turn_block(b, u - 10)
                pe.wait_ge(l_oT.sem, l_oT.at(b, NBF))
                for t in range(T):
                    for i in range(NBF):
                        ins_ = pe.matmul(bank(7)[:, t * P:t * P + P], oT_l[:, i, t * P:t * P + P],
                                         mat("L1_ffn_wo_light", i * P), start=(i == 0), stop=(i == NBF - 1))
                ins_.then_inc(l_light.sem, 1)
                pe.wait_ge(l_o.sem, l_o.at(b, UT))
                for i in range(NBF):
                    ins_ = pe.transpose(bank(4)[:, i * P:i * P + P], oh[:, i * P:i * P + P], ident[:, :])
                ins_.then_inc(l_oturn.sem, 1)
                pe.wait_ge(l_oT.sem, l_oT.at(b, NBF + 1))
                for i in range(NBF):
                    ins_ = pe.matmul(bank(5)[:, 0:D], ohT[:, i * P:i * P + P], mat("L1_ffn_wo_heavy", i * P),
                                     start=(i == 0), stop=(i == NBF - 1))
                ins_.then_inc(l_heavy.sem, 1)
                pe.wait_ge(l_routed.sem, l_routed.at(b, 1))
                for t in range(T):
                    ins_ = pe.matmul(bank(2)[:, t * P:t * P + P], lw["placeT"][:, t * P:t * P + P], lw["routed"],
                                     start=True, stop=True)
                ins_.then_inc(l_out.sem, 1)

        def route1_scalar(act, step, use, done):
            for s in (l_probs, l_pT):
                act.sem_inc(s.sem, s.ahead)
            descent_scalar(act, 1)

            def probs(b, u):
                act.wait_ge(l_max.sem, l_max.at(b, u + 1))
                act.wait_ge(l_turned.sem, l_turned.at(b, u - 3))
                act.wait_ge(l_o.sem, l_o.at(b, u - 3))
                n = P if u < UL else NKV
                for i in range(4 * P // n):
                    ins_ = act.activation(pr_l[:, u % 4, i * n:i * n + n], bank(u % 2)[:, i * n:i * n + n], ACT.Exp,
                                          bias=nm_l[:, u % 4, i:i + 1], accum_out=sums_l[:, u % 4, i:i + 1])
                ins_.then_inc(l_probs.sem, 1)

            def copy_pT(b, u):
                act.wait_ge(l_turned.sem, l_turned.at(b, u + 1))
                act.wait_ge(l_av.sem, l_av.at(b, u - 1))
                act.copy(pT_l[:, u % 2, :], bank(4 + u % 2)).then_inc(l_pT.sem, 1)

            with act.Fori(0, B) as b:
                for n in range(0, len(LITEMS), 2):
                    kind, i = LITEMS[n]
                    act.wait_ge(l_proj.sem, l_proj.at(b, n + 1))
                    dst = {"q": qT_l, "k": kT_l, "v": v_l}[kind][:, i, :]
                    src = bank(ITEM_BANK[n % 8])
                    (act.mul(dst, src, DH ** -0.5) if kind == "q" else act.copy(dst, src)).then_inc(l_even.sem, 1)
                for u in range(UT + 2):
                    if u >= 2:
                        copy_pT(b, u - 2)
                    if 11 <= u < 11 + NBF:
                        act.wait_ge(l_oturn.sem, l_oturn.at(b, u - 10))
                        act.copy(oT_l[:, u - 11, :], bank(2 + (u - 11) % 2)).then_inc(l_oT.sem, 1)
                    if u < UT:
                        probs(b, u)
                    if u == 4:
                        act.wait_ge(l_gath.sem, l_gath.at(b, 1))
                        act.mul(lw["xq"], bank(2)[:, 0:NQ], col("L1_ffn_gamma_heavy"))
                        act.mul(lw["xk"], bank(2)[:, NQ:NQ + NKV], col("L1_ffn_gamma_heavy"))
                        act.copy(lw["ws"], bank(2)[:, NQ + NKV:NQ + NKV + 1 + NKC]).then_inc(l_gx.sem, 1)
                    if u == 5:
                        act.wait_ge(l_hproj.sem, l_hproj.at(b, 1))
                        act.mul(lw["qh"], bank(7), DH ** -0.5).then_inc(l_ha.sem, 1)
                        act.wait_ge(l_hproj.sem, l_hproj.at(b, 2))
                        act.copy(lw["kh"][:, 0:S], bank(2)).then_inc(l_ha.sem, 1)
                act.wait_ge(l_oturn.sem, l_oturn.at(b, NBF))
                act.copy(oT_l[:, NBF - 1, :], bank(3)).then_inc(l_oT.sem, 1)
                act.wait_ge(l_oturn.sem, l_oturn.at(b, NBF + 1))
                act.copy(ohT, bank(4)).then_inc(l_oT.sem, 1)

        def route1_vector(dve, step, use, done):
            dve.sem_inc(l_o.sem, l_o.ahead)
            dve.sem_inc(l_added.sem, l_added.ahead)
            descent_vector(dve, step, 1, bc1, R8)

            def max_of(b, u):
                dve.wait_ge(l_scores.sem, l_scores.at(b, u + 1))
                dve.wait_ge(l_probs.sem, l_probs.at(b, u - 3))
                n = 4 if u < UL else 2
                dve.tensor_reduce(nm_l[:, u % 4, 0:n], bank(u % 2).rearrange("p (i k) -> p i k", i=n), X, ALU.max,
                                  negate=True).then_inc(l_max.sem, 1)

            def norm_o(b, u):
                dve.wait_ge(l_av.sem, l_av.at(b, u + 1))
                blocks, w = blocks_of(u)
                n = 4 if u < UL else 2
                step(dve.reciprocal(rec_l[:, u % 2, 0:n], sums_l[:, u % 4, 0:n]))
                if u < UL:
                    dst = o_l[:, w, :].rearrange("p (i r e) -> p i r e", r=2, e=DH)[:, :, u % 2, :]
                else:
                    j = u - UL
                    dst = oh[:, (j // 2) * 256:(j // 2) * 256 + 256].rearrange("p (i r e) -> p i r e", r=2, e=DH)[:, :, j % 2, :]
                dve.tensor_tensor(dst, bank(6)[:, 0:n * DH].rearrange("p (i e) -> p i e", i=n),
                                  rec_l[:, u % 2, 0:n].unsqueeze(2).to_broadcast([P, n, DH]), ALU.mult)\
                    .then_inc(l_o.sem, 1)

            with step.loop(B, 2 * RANK_STEPS + UT) as b:
                for n in range(1, len(LITEMS), 2):
                    kind, i = LITEMS[n]
                    dve.wait_ge(l_proj.sem, l_proj.at(b, n + 1))
                    dst, src = {"q": qT_l, "k": kT_l, "v": v_l}[kind][:, i, :], bank(ITEM_BANK[n % 8])
                    (dve.tensor_scalar(dst, src, DH ** -0.5, None, ALU.mult) if kind == "q"
                     else dve.tensor_copy(dst, src)).then_inc(l_odd.sem, 1)
                    if n // 2 < T:
                        rank_tile(dve, step, bc1, b, n // 2)
                    if n // 2 == T:
                        place_tokens(dve, step, placeq, NQ)
                for u in range(UT + 3):
                    if u < UT:
                        max_of(b, u)
                    if u >= 3:
                        norm_o(b, u - 3)
                    if u < T:
                        rank_tile(dve, step, bc1, b + B, u)
                    if u == T - 1:
                        place_tokens(dve, step, placek, NKV)
                        dve.sem_inc(l_placed.sem, 1)
                    if u == 5:
                        dve.wait_ge(l_gath.sem, l_gath.at(b, 1))
                        dve.tensor_copy(lw["placeT"], bank(3)).then_inc(l_gturn.sem, 1)
                    if u == 6:
                        dve.wait_ge(l_hproj.sem, l_hproj.at(b, 3))
                        dve.tensor_copy(lw["kh"][:, S:2 * S], bank(3)).then_inc(l_hd.sem, 1)
                        dve.wait_ge(l_hproj.sem, l_hproj.at(b, 4))
                        dve.wait_ge(l_gx.sem, l_gx.at(b, 1))
                        dve.tensor_scalar(vh[:, 0, :], bank(7), lw["ws"][:, 1:2], None, ALU.mult).then_inc(l_hd.sem, 1)
                    if u == 7:
                        dve.wait_ge(l_hproj.sem, l_hproj.at(b, 5))
                        dve.tensor_scalar(vh[:, 1, :], bank(2), lw["ws"][:, 2:3], None, ALU.mult).then_inc(l_hd.sem, 1)
                xb = x[:, ds(b * T, T), :]
                gate = tg[:, 5:6]
                dve.wait_ge(l_light.sem, l_light.at(b, 1))
                dve.scalar_tensor_tensor(out=xb, in0=bank(7).rearrange("p (t d) -> p t d", t=T), scalar=gate, in1=xb,
                                         op0=ALU.mult, op1=ALU.add).then_inc(l_added.sem, 1)
                dve.wait_ge(l_heavy.sem, l_heavy.at(b, 1))
                dve.tensor_scalar(lw["routed"], bank(5)[:, 0:D], lw["ws"][:, 0:1], None, ALU.mult)\
                    .then_inc(l_routed.sem, 1)
                dve.wait_ge(l_out.sem, l_out.at(b, 1))
                dve.wait_ge(l_added.sem, l_added.at(b, 1))
                dve.scalar_tensor_tensor(out=xb, in0=bank(2).rearrange("p (t d) -> p t d", t=T), scalar=gate, in1=xb,
                                         op0=ALU.mult, op1=ALU.add).then_inc(turn_done, 1)

        W2, W3 = 3 * FF, 2 * FF + NF
        mw = carve({"w": 2 * W2, "h": 2 * NF * S, "sg": 2 * S, "acc": NT * D, "y": 2 * T * D, "lg": NT * 16, "pr": NT * 16,
                    "mx": NT * 2, "sm": NT * 2, "cw": NT * E, "top": NT * E, "idx": NT * E, "idxf": NT * E,
                    "hot": NT * E})
        wts = mw["w"].rearrange("p (n k) -> p n k", n=2)
        h_m = mw["h"].rearrange("p (n f q) -> p n f q", n=2, f=NF)
        sg = mw["sg"].rearrange("p (n q) -> p n q", n=2)
        acc = mw["acc"].rearrange("p (n d) -> p n d", n=NT)
        y_m = mw["y"].rearrange("p (n t d) -> p n t d", n=2, t=T)
        cw = mw["cw"].rearrange("p (n e) -> p n e", n=NT)
        IB = 2 * B

        class Experts:

            def __init__(self, n):
                self.loaded = [sem(f"e{n}_loaded{i}") for i in range(2)]
                self.logits = sem(f"e{n}_logits")
                self.lgread = sem(f"e{n}_lgread")
                self.sm = sem(f"e{n}_sm")
                self.exps = sem(f"e{n}_exps")
                self.pre = Signal(sem(f"e{n}_pre"), IB * NF)
                self.act = Signal(sem(f"e{n}_act"), IB * NF)
                self.h = Signal(sem(f"e{n}_h"), IB * NF)
                self.y = Signal(sem(f"e{n}_y"), IB, 2)
                self.acc = Signal(sem(f"e{n}_acc"), IB, 2)

        ex = [Experts(2), Experts(3)]

        def moe_sync(sp, which, done):
            src, n = (ins["experts2"], W2) if which == 0 else (ins["experts3"], W3)
            s = ex[which]
            sp.wait_ge(turn_done, done)
            for i in range(2):
                sp.dma_start(wts[:, i, 0:n], src[:, i, :]).then_inc(s.loaded[i], 16)
            with sp.Fori(0, E // 2 - 1) as r:
                for i in range(2):
                    sp.wait_ge(s.y.sem, s.y.at(r, (i + 1) * B))
                    sp.dma_start(wts[:, i, 0:n], src[:, ds(2 * r + (2 + i), 1), :].rearrange("p a n -> p (a n)"))\
                        .then_inc(s.loaded[i], 16)

        def moe_tensor(pe, which, done):
            s = ex[which]
            pe.wait_ge(turn_done, done)
            pe.wait_ge(xnT_ready, xnT_count(5 + 2 * which))
            pe.wait_ge(mats_loaded[4], 16)
            pe.sem_inc(s.y.sem, s.y.ahead)
            n = 16 if which == 0 else 8
            name = "L2_ffn_w_router" if which == 0 else "L3_ffn_gate_w"
            for i in range(NT):
                ins_ = pe.matmul(bank(7)[:, i * n:i * n + n], xnT[:, i * P:i * P + P], mat(name, 0, n),
                                 start=True, stop=True)
            ins_.then_inc(s.logits, 1)

            def up(r, i):
                e, b = divmod(i, B)
                if b == 0:
                    pe.wait_ge(s.loaded[e], r * 16 + 16)
                for f in range(NF):
                    k = i * NF + f
                    if which == 0:
                        if k >= 2:
                            pe.wait_ge(s.h.sem, s.h.at(r, k - 1))
                        pe.matmul(bank(2 * (k % 2)), wts[:, e, f * P:f * P + P], xnT[:, b * S:b * S + S],
                                  start=True, stop=True)
                        ins_ = pe.matmul(bank(2 * (k % 2) + 1), wts[:, e, FF + f * P:FF + f * P + P],
                                         xnT[:, b * S:b * S + S], start=True, stop=True)
                    else:
                        if k >= 4:
                            pe.wait_ge(s.act.sem, s.act.at(r, k - 3))
                        ins_ = pe.matmul(bank(k % 4), wts[:, e, f * P:f * P + P], xnT[:, b * S:b * S + S],
                                         start=True, stop=True)
                    ins_.then_inc(s.pre.sem, 1)

            def down(r, i):
                e = i // B
                pe.wait_ge(s.acc.sem, s.acc.at(r, i - 1))
                ready = s.h if which == 0 else s.act
                pe.wait_ge(ready.sem, ready.at(r, (i + 1) * NF))
                off = 2 * FF if which == 0 else FF
                for t in range(T):
                    for f in range(NF):
                        ins_ = pe.matmul(bank(4 + i % 2)[:, t * P:t * P + P], h_m[:, i % 2, f, t * P:t * P + P],
                                         wts[:, e, off + f * P:off + f * P + P], start=(f == 0), stop=(f == NF - 1))
                ins_.then_inc(s.y.sem, 1)

            with pe.Fori(0, E // 2) as r:
                for i in range(IB + 1):
                    if i < IB:
                        up(r, i)
                    if i >= 1:
                        down(r, i - 1)

        def moe_scalar(act, which, done):
            s = ex[which]
            act.wait_ge(s.sm, 1)
            lg = mw["lg"].rearrange("p (n k e) -> p n k e", n=NT, e=E)
            pr = mw["pr"].rearrange("p (n k e) -> p n k e", n=NT, e=E)
            if which == 0:
                act.activation(pr[:, :, 0, :], lg[:, :, 0, :], ACT.Exp)
                act.activation(pr[:, :, 1, :], lg[:, :, 1, :], ACT.Exp, scale=1.0 / 0.1).then_inc(s.exps, 1)
            else:
                act.activation(mw["pr"][:, 0:NT * E], mw["lg"][:, 0:NT * E], ACT.Exp).then_inc(s.exps, 1)
            with act.Fori(0, E // 2) as r:
                for i in range(IB):
                    for f in range(NF):
                        k = i * NF + f
                        act.wait_ge(s.pre.sem, s.pre.at(r, k + 1))
                        if which == 0:
                            if k >= 2:
                                act.wait_ge(s.h.sem, s.h.at(r, k - 1))
                            act.activation(sg[:, k % 2, :], bank(2 * (k % 2)), ACT.Silu).then_inc(s.act.sem, 1)
                        else:
                            if f == 0:
                                act.wait_ge(s.y.sem, s.y.at(r, i - 1))
                            act.activation(h_m[:, i % 2, f, :], bank(k % 4), ACT.Gelu, bias=wts[:, i // B, 2 * FF + f:2 * FF + f + 1])\
                                .then_inc(s.act.sem, 1)

        def moe_vector(dve, step, which, done):
            s = ex[which]
            dve.wait_ge(turn_done, done)
            step(dve.memset(mw["acc"], 0.0))
            dve.sem_inc(s.acc.sem, s.acc.ahead)
            dve.wait_ge(s.logits, 1)
            if which == 0:
                lg = mw["lg"].rearrange("p (n e) -> p n e", e=E)
                pr = mw["pr"].rearrange("p (n e) -> p n e", e=E)
                mx, sm = mw["mx"], mw["sm"]
                n2 = 2 * NT
                step(dve.tensor_copy(mw["lg"], bank(7)[:, 0:NT * 16]))
                step(dve.tensor_reduce(mx, lg, X, ALU.max))
                dve.tensor_tensor(lg, lg, mx.unsqueeze(2).to_broadcast([P, n2, E]), ALU.subtract).then_inc(s.sm, 1)
                dve.wait_ge(s.exps, 1)
                step(dve.tensor_reduce(sm, pr, X, ALU.add))
                step(dve.reciprocal(sm, sm))
                step(dve.tensor_tensor(pr, pr, sm.unsqueeze(2).to_broadcast([P, n2, E]), ALU.mult))
                both = mw["pr"].rearrange("p (n k e) -> p n k e", n=NT, e=E)
                step(dve.tensor_tensor(cw, both[:, :, 0, :], both[:, :, 1, :], ALU.mult))
                step(dve.tensor_reduce(sm[:, 0:NT], cw, X, ALU.add))
                step(dve.tensor_scalar(sm[:, 0:NT], sm[:, 0:NT], 1e-9, None, ALU.add))
                step(dve.reciprocal(sm[:, 0:NT], sm[:, 0:NT]))
                step(dve.tensor_tensor(cw, cw, sm[:, 0:NT].unsqueeze(2).to_broadcast([P, NT, E]), ALU.mult))
            else:
                lg = mw["lg"][:, 0:NT * E].rearrange("p (n e) -> p n e", e=E)
                top = mw["top"].rearrange("p (n e) -> p n e", e=E)
                idx = mw["idx"].bitcast(U32).rearrange("p (n e) -> p n e", e=E)
                idxf = mw["idxf"].rearrange("p (n e) -> p n e", e=E)
                hot = mw["hot"].rearrange("p (n e) -> p n e", e=E)
                ex8 = mw["pr"][:, 0:NT * E].rearrange("p (n e) -> p n e", e=E)
                sm = mw["sm"][:, 0:NT]
                step(dve.tensor_tensor(lg, bank(7)[:, 0:NT * E].rearrange("p (n e) -> p n e", e=E),
                                       row("L3_ffn_gate_b", 0, E).unsqueeze(1).to_broadcast([P, NT, E]), ALU.add))
                for i in range(NT):
                    step.mark(dve.max(top[:, i, :], lg[:, i, :]))
                step.wait()
                for i in range(NT):
                    step.mark(dve.max_index(idx[:, i, :], top[:, i, :], lg[:, i, :]))
                step.wait()
                step(dve.tensor_copy(mw["idxf"], mw["idx"].bitcast(U32)))
                picks = pick[:, :].unsqueeze(1).to_broadcast([P, NT, E])
                step(dve.tensor_tensor(hot, picks, idxf[:, :, 0:1].to_broadcast([P, NT, E]), ALU.is_equal))
                step(dve.tensor_tensor(cw, picks, idxf[:, :, 1:2].to_broadcast([P, NT, E]), ALU.is_equal))
                step(dve.tensor_tensor(hot, hot, cw, ALU.add))
                dve.tensor_tensor(lg, lg, top[:, :, 0:1].to_broadcast([P, NT, E]), ALU.subtract).then_inc(s.sm, 1)
                dve.wait_ge(s.exps, 1)
                step(dve.tensor_tensor(cw, ex8, hot, ALU.mult))
                step(dve.tensor_reduce(sm, cw, X, ALU.add))
                step(dve.reciprocal(sm, sm))
                step(dve.tensor_tensor(cw, cw, sm.unsqueeze(2).to_broadcast([P, NT, E]), ALU.mult))

            def gate(r, i):
                for f in range(NF):
                    k = i * NF + f
                    dve.wait_ge(s.act.sem, s.act.at(r, k + 1))
                    if f == 0:
                        dve.wait_ge(s.y.sem, s.y.at(r, i - 1))
                    dve.tensor_tensor(h_m[:, i % 2, f, :], sg[:, k % 2, :], bank(2 * (k % 2) + 1), ALU.mult)\
                        .then_inc(s.h.sem, 1)

            def add_up(r, i):
                e, b = divmod(i, B)
                dve.wait_ge(s.y.sem, s.y.at(r, i + 1))
                src = bank(4 + i % 2).rearrange("p (t d) -> p t d", t=T)
                if which == 1:
                    bias = rows[:, ds(ROW_AT["L3_ffn_b2"][0] + (2 * r + e) * D, D)].unsqueeze(1).to_broadcast([P, T, D])
                    step(dve.tensor_tensor(y_m[:, i % 2], src, bias, ALU.add))
                    src = y_m[:, i % 2]
                for t in range(T):
                    n = b * T + t
                    ins_ = dve.scalar_tensor_tensor(out=acc[:, n, :], in0=src[:, t, :], scalar=cw[:, n, ds(2 * r + e, 1)],
                                                    in1=acc[:, n, :], op0=ALU.mult, op1=ALU.add)
                ins_.then_inc(s.acc.sem, 1)

            with step.loop(E // 2, IB * which) as r:
                for i in range(IB + 1):
                    if which == 0 and i < IB:
                        gate(r, i)
                    if i >= 1:
                        add_up(r, i - 1)
            dve.wait_ge(s.acc.sem, s.acc.at(E // 2 - 1, IB))
            n = 6 + which
            dve.scalar_tensor_tensor(out=x[:, :, :], in0=acc, scalar=tg[:, n:n + 1], in1=x[:, :, :], op0=ALU.mult,
                                     op1=ALU.add).then_inc(turn_done, 1)

        def moe2_sync(sp, use, done):
            moe_sync(sp, 0, done)

        def moe3_sync(sp, use, done):
            moe_sync(sp, 1, done)

        def moe2_tensor(pe, use, done):
            moe_tensor(pe, 0, done)

        def moe3_tensor(pe, use, done):
            moe_tensor(pe, 1, done)

        def moe2_scalar(act, step, use, done):
            moe_scalar(act, 0, done)

        def moe3_scalar(act, step, use, done):
            moe_scalar(act, 1, done)

        def moe2_vector(dve, step, use, done):
            moe_vector(dve, step, 0, done)

        def moe3_vector(dve, step, use, done):
            moe_vector(dve, step, 1, done)

        def setup_pool(pool, step):
            pool.memset(ident[:, :], 0.0)
            pool.memset(head_of_row[:, :], 1.0)
            pool.memset(head_of_key[:, :, :], 1.0)
            pool.memset(earlier[:, :, :], 1.0)
            pool.memset(expo[:, :], -0.5)
            pool.memset(tokens[:, :, :, :], 0.0)
            pool.memset(junk[:, :], 0.0)
            for which in range(2):
                pool.memset(k_inv[:, which, :], 1.0 / K_OF[which][1])
                pool.memset(k_col[:, which:which + 1], K_OF[which][1])
                pool.memset(k_log[:, which:which + 1], float(np.log(K_OF[which][1])))
            step(pool.memset(row_of[:, :, :], 1.0))
            for which in range(2):
                k = K_OF[which][0]
                for buf, n, v in ((k_inv[:, which, :], S, 1.0 / k), (k_col[:, which:which + 1], 1, k),
                                  (k_log[:, which:which + 1], 1, float(np.log(k)))):
                    ins_ = pool.affine_select(out=buf, in_=buf, compare_op=ALU.is_ge, fill=v, base=-B,
                                              pattern=[[0, n]], channel_multiplier=1)
            step(ins_)
            pool.affine_select(out=ident[:, :], in_=ident[:, :], compare_op=ALU.not_equal, fill=1.0, base=0,
                               pattern=[[-1, P]], channel_multiplier=1).then_inc(consts_ready, 1)
            step(pool.affine_select(out=head_of_row[:, :], in_=head_of_row[:, :], compare_op=ALU.is_ge, fill=0.0, base=0,
                                    pattern=[[-DK, H]], channel_multiplier=1))
            pool.affine_select(out=head_of_row[:, :], in_=head_of_row[:, :], compare_op=ALU.is_ge, fill=0.0,
                               base=DK - 1, pattern=[[DK, H]], channel_multiplier=-1).then_inc(consts_ready, 1)
            step(pool.affine_select(out=head_of_key[:, :, :], in_=head_of_key[:, :, :], compare_op=ALU.is_ge, fill=0.0,
                                    base=0, pattern=[[P, NCH], [-KC, HH]], channel_multiplier=1))
            pool.affine_select(out=head_of_key[:, :, :], in_=head_of_key[:, :, :], compare_op=ALU.is_ge, fill=0.0,
                               base=KC - 1, pattern=[[-P, NCH], [KC, HH]], channel_multiplier=-1)\
                .then_inc(consts_ready, 1)
            pool.affine_select(out=earlier[:, :, :], in_=earlier[:, :, :], compare_op=ALU.is_gt, fill=0.0, base=0,
                               pattern=[[P, T], [-1, S]], channel_multiplier=1).then_inc(consts_ready, 1)
            step(pool.affine_select(out=row_of[:, :, :], in_=row_of[:, :, :], compare_op=ALU.is_equal, fill=0.0, base=0,
                                    pattern=[[-1, 2 * B], [0, P]], channel_multiplier=1))
            pool.sem_inc(consts_ready, 1)
            pool.iota(slot_no[:, :], [[1, NKV]], base=0, channel_multiplier=0, allow_small_or_imprecise_dtypes=True)\
                .then_inc(consts_ready, 1)
            pool.iota(pick[:, :], [[1, 8]], base=0, channel_multiplier=0, allow_small_or_imprecise_dtypes=True)\
                .then_inc(consts_ready, 1)
            pool.wait_ge(small_loaded, 48)
            for kind, (name, base) in enumerate((("L0_ffn_routing_token", 0), ("L1_ffn_q_routing_token", 0),
                                                 ("L1_ffn_kv_routing_token", B))):
                for b in range(B):
                    ins_ = pool.tensor_copy(tokens[:, kind, b, base + b:base + b + 1], col(name))
            step(ins_)
            pool.sem_inc(consts_ready, 2)

        def setup_sync(sp):
            sp.dma_start(x[:, :, :], ins["x"]).then_inc(x_loaded, 16)
            sp.dma_start(ctxT[:, :, :], ins["ctxT"]).then_inc(small_loaded, 16)
            sp.dma_start(cols[:, :], ins["cols"]).then_inc(small_loaded, 16)
            sp.dma_start(rows[:, :], ins["rows"].to_broadcast([P, NROW])).then_inc(small_loaded, 16)
            for i, (first, past) in enumerate(MAT_PARTS):
                a, z = MAT_AT[first][0], MAT_AT[past][0] if past else NMAT
                sp.dma_start(mats[:, a:z], ins["mats"][:, a:z]).then_inc(mats_loaded[i], 16)

        def setup_scalar(act):
            act.wait_ge(small_loaded, 48)
            act.activation(tg[:, :], row("g_xattn", 0, 8), ACT.Tanh).then_inc(gates_ready, 1)
            for i, layer in enumerate(("L2", "L3")):
                act.mul(bq_s[:, i:i + 1], col(layer + "_xattn_bq"), float(DK) ** -0.5).then_inc(bq_scaled, 1)

        def setup_vector(dve):
            dve.wait_ge(consts_ready, CONSTS)
            dve.wait_ge(gates_ready, 1)
            dve.wait_ge(x_loaded, 16)
            dve.sem_inc(o_read.sem, o_read.ahead)
            dve.sem_inc(turn_done, 1)

        ENGINE_PARTS = {
            "sync": {"attend": attend_sync, "moe2": moe2_sync, "moe3": moe3_sync},
            "gpsimd": {"norm": norm_pool, "kv": kv_pool, "attend": attend_pool, "ffn0": ffn0_pool,
                       "gated": gated_pool, "route0": route0_pool, "self": self_pool,
                       "route1": route1_pool},
            "scalar": {"norm": norm_scalar, "kv": kv_scalar, "attend": attend_scalar, "ffn0": ffn0_scalar,
                       "gated": gated_scalar, "route0": route0_scalar, "self": self_scalar,
                       "route1": route1_scalar, "moe2": moe2_scalar, "moe3": moe3_scalar},
            "tensor": {"norm": norm_tensor, "kv": kv_tensor, "attend": attend_tensor, "ffn0": ffn0_tensor,
                       "gated": gated_tensor, "route0": route0_tensor, "self": self_tensor,
                       "route1": route1_tensor, "moe2": moe2_tensor, "moe3": moe3_tensor},
            "vector": {"norm": norm_vector, "attend": attend_vector, "ffn0": ffn0_vector, "gated": gated_vector,
                        "route0": route0_vector, "self": self_vector,
                       "route1": route1_vector, "moe2": moe2_vector, "moe3": moe3_vector},
        }

        def layers(name, *args):
            done = 1
            for part, use in LAYERS:
                f = ENGINE_PARTS[name].get(part)
                if f:
                    f(*args, use, done)
                done += TURNS[part]
            return done

        block = ctx.enter_context(nc.Block())

        @block.sync
        def _(sp):
            setup_sync(sp)
            done = layers("sync", sp)
            sp.wait_ge(turn_done, done)
            sp.dma_start(out, x[:, :, :]).then_inc(stored, 16)
            sp.wait_ge(stored, 16)

        @block.gpsimd
        def _(pool):
            step = Steps(pool, pool_step)
            setup_pool(pool, step)
            layers("gpsimd", pool, step)

        @block.scalar
        def _(act):
            setup_scalar(act)
            layers("scalar", act, Steps(act, act_step))

        @block.tensor
        def _(pe):
            layers("tensor", pe)

        @block.vector
        def _(dve):
            setup_vector(dve)
            layers("vector", dve, Steps(dve, dve_step))


def _blocks(w):
    n = w.shape[0] // 128
    return w.reshape(n, 128, -1).transpose(1, 0, 2).reshape(128, -1)


def _rows128(w):
    out = np.zeros((128, w.shape[1]), w.dtype)
    out[:w.shape[0]] = w
    return out


def lay_out(v):
    v = {k: np.asarray(a) for k, a in v.items()}
    m = {n: v[n].T for n in ("L0_xattn_Wq", "L0_xattn_Wk", "L0_xattn_Wv", "L0_xattn_Wo", "L0_xattn_W1",
                             "L0_ffn_w1_l", "L0_ffn_w1_h", "L3_xattn_Wq", "L3_xattn_Wk", "L3_xattn_Wv", "L3_xattn_Wo")}
    m["L0_xattn_W2"] = _blocks(v["L0_xattn_W2"].T)
    m["L0_ffn_w2_l"] = _rows128(v["L0_ffn_w2_l"].T)
    m["L0_ffn_w2_h"] = _blocks(v["L0_ffn_w2_h"].T)
    inner = v["L1_xattn_Wq"].shape[1]
    m["L1_xattn_Wk"], m["L1_xattn_Wv"] = v["L1_xattn_Wkv"][:, :inner], v["L1_xattn_Wkv"][:, inner:]
    hid = v["L1_ffn_wq_light"].shape[1]
    m["L1_ffn_wk_light"], m["L1_ffn_wv_light"] = v["L1_ffn_wkv_light"][:, :hid], v["L1_ffn_wkv_light"][:, hid:]
    kv = v["L1_ffn_wkv_heavy"].reshape(HF, 2, DH, D)
    m["L1_ffn_wk_heavy"], m["L1_ffn_wv_heavy"] = (kv[:, i].reshape(hid, D).T for i in range(2))
    for n in ("L1_xattn_Wo", "L1_ffn_wo_light", "L1_ffn_wo_heavy"):
        m[n] = _blocks(v[n])
    mats = np.concatenate([m[n] if n in m else v[n] for n, _ in MATS], axis=1)
    cols = np.concatenate([v[n].reshape(-1, 128).T if v[n].size >= 128 else _rows128(v[n].reshape(-1, 1))
                           for n, _ in COLS], axis=1)
    rows = np.concatenate([v[n].reshape(-1) for n, _ in ROWS]).reshape(1, -1)
    w1 = v["L3_ffn_w1"].transpose(1, 0, 2)
    up = [v["L2_ffn_w_gate"].transpose(1, 0, 2), v["L2_ffn_w_up"].transpose(1, 0, 2)]
    down = [v[n].reshape(E, NF, 128, D).transpose(2, 0, 1, 3).reshape(128, E, NF * D)
            for n in ("L2_ffn_w_down", "L3_ffn_w2")]
    return {
        "x": v["x"].reshape(NT, P, D).transpose(1, 0, 2),
        "ctxT": v["ctx_1024"].transpose(2, 0, 1),
        "bias": v["fside_Bx16xSxS2_0"].reshape(B, H, T, P, KC).transpose(0, 2, 3, 1, 4).reshape(NT, P, H * KC),
        "mask": v["mask_Bx1xSxS2_ik1"].reshape(NT, P, KC),
        "mats": mats, "cols": cols, "rows": rows,
        "experts2": np.concatenate([up[0], up[1], down[0]], axis=2),
        "experts3": np.concatenate([w1, down[1], v["L3_ffn_b1"].reshape(E, NF, 128).transpose(2, 0, 1)], axis=2),
    }


def build(nc, arrays, stages):
    ins = {n: nc.dram_tensor(f"in_{n}_dram", a.shape, mybir.dt.from_np(a.dtype), kind="ExternalInput").ap()
           for n, a in arrays.items()}
    out = nc.dram_tensor("out_0_dram", (P, NT, D), F32, kind="ExternalOutput").ap()
    flamingo_kernel(nc, ins, out, stages)


def kernel(**inputs):
    import concourse.bacc as _bacc
    from concourse.bass_utils import run_bass_kernel_spmd as _run

    arrays = {n: np.ascontiguousarray(a) for n, a in lay_out(inputs).items()}
    nc = _bacc.Bacc("TRN2", target_bir_lowering=False, num_devices=1)
    build(nc, arrays, 8)
    r = _run(nc, [{f"in_{n}_dram": a for n, a in arrays.items()}], core_ids=[0])
    return r.results[0]["out_0_dram"].transpose(1, 0, 2).reshape(B, S, D)
```

```python
from contextlib import ExitStack, contextmanager

import numpy as np
import concourse.bass as bass
from concourse import mybir

F32 = mybir.dt.float32
I32 = mybir.dt.int32
U32 = mybir.dt.uint32
ALU = mybir.AluOpType
ACT = mybir.ActivationFunctionType
X = mybir.AxisListType.X
ds = bass.ds

P = 128
B = 4
S = 512
T = S // P
NT = B * T
D = 128
KC = 77
FF = 512
NF = FF // P
H = 16
DK = D // H
HH = H // 2
HK = HH * KC
NCH = -(-HK // P)
LASTR = HK - (NCH - 1) * P
DH = 64
NBLK = H * DH // P
HF = 8
NBF = HF * DH // P
NKEY = S + KC
NQ, NKV = 128, 256
E = 8
DESCENT = 50
EPS = 1e-5
MASKED = -3.0e38

COLS = [("L0_xattn_g1", 1), ("L0_xattn_be1", 1), ("L0_xattn_b1", 4), ("L0_ffn_gamma_l", 1), ("L0_ffn_gamma_h", 1),
        ("L0_ffn_b1_l", 1), ("L0_ffn_b1_h", 4), ("L1_xattn_ln_g", 1), ("L1_xattn_ln_b", 1), ("L1_ffn_gamma_light", 1),
        ("L1_ffn_gamma_heavy", 1), ("L2_xattn_bq", 1), ("L2_xattn_bk", 1), ("L3_xattn_bq", 1), ("L3_xattn_bk", 1),
        ("L0_ffn_routing_token", 1), ("L1_ffn_q_routing_token", 1), ("L1_ffn_kv_routing_token", 1)]
ROWS = [("L0_xattn_b2", 128), ("L0_xattn_g2", 128), ("L0_xattn_be2", 128), ("L0_ffn_b2_l", 128), ("L0_ffn_b2_h", 128),
        ("L1_xattn_bo", 128), ("L2_xattn_bv", 128), ("L2_xattn_bo", 128), ("L3_xattn_bv", 128), ("L3_xattn_bo", 128),
        ("L3_ffn_b2", 1024), ("L3_ffn_gate_b", 8), ("g_xattn", 4), ("g_ffn", 4)]
MATS = [("L0_xattn_Wq", 128), ("L0_xattn_Wk", 128), ("L0_xattn_Wv", 128), ("L0_xattn_Wo", 128), ("L0_xattn_W1", 512),
        ("L0_xattn_W2", 512), ("L0_ffn_w1_l", 64), ("L0_ffn_w2_l", 128), ("L0_ffn_w1_h", 512), ("L0_ffn_w2_h", 512),
        ("L1_xattn_Wq", 1024), ("L1_xattn_Wk", 1024), ("L1_xattn_Wv", 1024), ("L1_xattn_Wm", 1024),
        ("L1_xattn_Wo", 1024),
        ("L1_ffn_wq_light", 512), ("L1_ffn_wk_light", 512), ("L1_ffn_wv_light", 512), ("L1_ffn_wo_light", 512),
        ("L1_ffn_wq_heavy", 512), ("L1_ffn_wk_heavy", 512), ("L1_ffn_wv_heavy", 512), ("L1_ffn_wo_heavy", 512),
        ("L2_xattn_Wq", 128), ("L2_xattn_Wk", 128), ("L2_xattn_Wv", 128), ("L2_xattn_Wo", 128),
        ("L2_ffn_w_router", 8), ("L2_ffn_w_gating", 8),
        ("L3_xattn_Wq", 128), ("L3_xattn_Wk", 128), ("L3_xattn_Wv", 128), ("L3_xattn_Wo", 128), ("L3_ffn_gate_w", 8)]


def offsets(table):
    at, out = 0, {}
    for name, n in table:
        out[name] = (at, n)
        at += n
    return out, at


COL_AT, NCOL = offsets(COLS)
ROW_AT, NROW = offsets(ROWS)
MAT_AT, NMAT = offsets(MATS)
MAT_PARTS = [("L0_xattn_Wq", "L0_xattn_W1"), ("L0_xattn_W1", "L0_ffn_w1_l"), ("L0_ffn_w1_l", "L1_xattn_Wq"),
             ("L1_xattn_Wq", "L1_ffn_wq_light"),
             ("L1_ffn_wq_light", "L2_xattn_Wq"), ("L2_xattn_Wq", None)]


class Signal:

    def __init__(self, sem, per, ahead=0):
        self.sem, self.per, self.ahead = sem, per, ahead

    def at(self, turn, k):
        return turn * self.per + (k + self.ahead)


class Steps:

    def __init__(self, engine, sem):
        self.engine, self.sem, self.base, self.turn, self.per, self.k = engine, sem, 0, 0, 0, 0

    def mark(self, ins):
        ins.then_inc(self.sem, 1)
        self.k += 1

    def wait(self):
        self.engine.wait_ge(self.sem, self.turn * self.per + (self.base + self.k))

    def __call__(self, ins):
        self.mark(ins)
        self.wait()

    @contextmanager
    def loop(self, turns, per, start=0):
        self.base, self.k, self.per = self.base + self.k - start * per, 0, per
        with self.engine.Fori(start, start + turns) as turn:
            self.turn = turn
            yield turn
        assert self.k == per, f"the loop's steps: {self.k}, not {per}"
        self.base, self.k, self.turn, self.per = self.base + (start + turns) * per, 0, 0, 0


def flamingo_kernel(nc, ins, out):
    ctx = ExitStack()

    def sb(name, shape, dt=F32):
        return ctx.enter_context(nc.sbuf_tensor(name, shape, dt))

    def sem(name):
        return ctx.enter_context(nc.semaphore(name))

    with ctx:
        mats = sb("mats", [P, NMAT])
        cols = sb("cols", [P, NCOL])
        rows = sb("rows", [P, NROW])
        ctxT = sb("ctxT", [P, B, KC])
        ident = sb("ident", [P, P])
        head_of_row = sb("head_of_row", [P, H])
        head_of_key = sb("head_of_key", [P, NCH, HH])
        earlier = sb("earlier", [P, T, S])
        slot_no = sb("slot_no", [P, NKV])
        expo = sb("expo", [P, NT])
        row_of = sb("row_of", [2 * B, 2 * B, P])
        tokens = sb("tokens", [P, 3, B, 2 * B])
        pick = sb("pick", [P, 8])
        tg = sb("tg", [P, 8])

        x = sb("x", [P, NT, D])
        xn = sb("xn", [P, NT, D])
        xnT = sb("xnT", [P, NT * P])
        rn = sb("rn", [P, NT, D])
        stat = sb("stat", [P, 2 * NT, 6])
        mv = sb("mv", [P, 2 * NT, 2])
        varr = sb("varr", [P, 2 * NT])
        squares = sb("squares", [P, NT])
        rstd = sb("rstd", [P, 2 * NT])
        x_in = sb("x_in", [P, S])
        junk = sb("junk", [P, S])
        spare = sb("spare", [P, 2])
        bq_s = sb("bq_s", [P, 2])
        work = sb("work", [P, 21504])
        psum = ctx.enter_context(nc.psum_tensor("psum", [P, 8 * 512], F32))

        def bank(i, n=1):
            return psum[:, 512 * i:512 * (i + n)]

        def carve(sizes):
            at, out = 0, {}
            for name, n in sizes.items():
                out[name] = work[:, at:at + n]
                at += n
            assert at <= 21504, at
            return out

        def col(name, i=0, n=P):
            return cols[0:n, COL_AT[name][0] + i:COL_AT[name][0] + i + 1]

        def row(name, i=0, n=D, parts=P):
            return rows[0:parts, ROW_AT[name][0] + i:ROW_AT[name][0] + i + n]

        def mat(name, i=0, n=P, parts=P):
            return mats[0:parts, MAT_AT[name][0] + i:MAT_AT[name][0] + i + n]

        dve_step, act_step, pool_step = sem("dve_step"), sem("act_step"), sem("pool_step")
        x_loaded, ctx_loaded = sem("x_loaded"), sem("ctx_loaded")
        small_loaded = sem("small_loaded")
        mats_loaded = [sem(f"mats_loaded{i}") for i in range(len(MAT_PARTS))]
        consts_ready, gates_ready = sem("consts_ready"), sem("gates_ready")
        turn_done = sem("turn_done")
        var_ready, rstd_ready = sem("var_ready"), sem("rstd_ready")
        xn_ready, rn_ready = sem("xn_ready"), sem("rn_ready")
        xn_turned, xnT_ready = sem("xn_turned"), sem("xnT_ready")
        x_new, x_final = sem("x_new"), sem("x_final")
        stored = sem("stored")

        CONSTS = 3
        routing_ready = sem("routing_ready")
        LAYERS = [("kv", 0), ("norm", 0), ("attend", 0), ("ffn0", 0), ("norm", 1), ("route0", 0),
                  ("norm", 2), ("self", 0), ("norm", 3), ("route1", 0),
                  ("kv", 1), ("norm", 4), ("attend", 1), ("norm", 5), ("moe2", 0),
                  ("kv", 2), ("norm", 6), ("gated", 2), ("norm", 7), ("moe3", 0)]
        TURNS = {"kv": 0, "norm": 0, "attend": B, "gated": B, "ffn0": B, "route0": B, "self": B, "route1": B,
                 "moe2": 1, "moe3": 1}
        RMS = (1, 3)
        TWICE = 2

        def before(kind_counts, call):
            return sum(kind_counts(c) for c in range(call))

        n_rstd = lambda c: 2 if c == TWICE else 1
        n_turn = lambda c: 2 * B if c in RMS else B

        xnT_count = lambda call: before(n_turn, call + 1)

        def norm_vector(dve, step, call, done):
            dve.wait_ge(turn_done, done)
            if call == 0:
                dve.wait_ge(x_loaded, 16)
            asked = before(n_rstd, call) * B

            def stats(src, b, at):
                for t in range(T):
                    step.mark(dve.bn_stats(stat[:, at + b * T + t, :], src[:, b * T + t, :]))

            def variances(b, at):
                step.wait()
                for t in range(T):
                    step.mark(dve.bn_aggr(mv[:, at + b * T + t, :], stat[:, at + b * T + t, :]))
                step.wait()
                dve.tensor_scalar(varr[:, at + b * T:at + b * T + T], mv[:, at + b * T:at + b * T + T, 1], EPS, None,
                                  ALU.add).then_inc(var_ready, 1)

            def scale(src, b, at, power):
                dve.wait_ge(rstd_ready, power)
                for t in range(T):
                    n = b * T + t
                    step.mark(dve.tensor_scalar(xn[:, n, :], src[:, n, :], mv[:, at + n, 0:1], rstd[:, at + n:at + n + 1],
                                                ALU.subtract, ALU.mult))

            if call != TWICE:
                for b in range(B + 1):
                    if b < B:
                        stats(x, b, 0)
                    if b >= 1:
                        scale(x, b - 1, 0, asked + b)
                    if b < B:
                        variances(b, 0)
                    else:
                        step.wait()
                    if b >= 1:
                        dve.sem_inc(xn_ready, 1)
                return
            for b in range(B + 2):
                if b < B:
                    stats(x, b, 0)
                if 1 <= b <= B:
                    scale(x, b - 1, 0, asked + (b if b == 1 else 2 * b - 2))
                if b < B:
                    variances(b, 0)
                else:
                    step.wait()
                if 1 <= b <= B:
                    stats(xn, b - 1, NT)
                if 2 <= b:
                    scale(xn, b - 2, NT, asked + (2 * b - 1 if b <= B else 2 * B))
                if 1 <= b <= B:
                    variances(b - 1, NT)
                else:
                    step.wait()
                if 2 <= b:
                    dve.sem_inc(xn_ready, 1)

        def norm_pool(pool, step, call, done):
            asked = before(n_rstd, call) * B

            def power(b, at):
                nonlocal asked
                asked += 1
                pool.wait_ge(var_ready, asked)
                pool.tensor_tensor(rstd[:, at + b * T:at + b * T + T], varr[:, at + b * T:at + b * T + T],
                                   expo[:, 0:T], ALU.pow).then_inc(rstd_ready, 1)

            for b in range(B + (call == TWICE)):
                if b < B:
                    power(b, 0)
                if call == TWICE and b >= 1:
                    power(b - 1, NT)
            if call in RMS:
                which = RMS.index(call)
                for b in range(B):
                    at = slice(NT + b * T, NT + b * T + T)
                    pool.wait_ge(squares_ready, which * B + b + 1)
                    step(pool.tensor_scalar(varr[:, at], squares[:, b * T:b * T + T], 1e-24, 1.0 / D, ALU.max, ALU.mult))
                    step(pool.tensor_tensor(rstd[:, at], varr[:, at], expo[:, 0:T], ALU.pow))
                    pool.tensor_tensor(rn[:, b * T:b * T + T, :], xn[:, b * T:b * T + T, :],
                                       rstd[:, at].unsqueeze(2).to_broadcast([P, T, D]), ALU.mult).then_inc(rn_ready, 1)

        def norm_tensor(pe, call, done):
            pe.wait_ge(turn_done, done)
            if call == 0:
                pe.wait_ge(consts_ready, CONSTS)
            turned = before(n_turn, call)
            which = RMS.index(call) if call in RMS else 0
            kinds = (0,) if which == 0 else (1, 2)
            if call in RMS:
                pe.wait_ge(routing_ready, 1)

            def logits(b):
                pe.wait_ge(xnT_ready, turned + b + 1)
                for kind in kinds:
                    ins = pe.matmul(bank(2)[0:2 * B, :], tokens[:, kind, b, :], xnT[:, b * S:b * S + S],
                                    start=(b == 0 and kind == kinds[0]), stop=(b == B - 1 and kind == kinds[-1]))
                if b == B - 1:
                    ins.then_inc(logits_ready, 1)

            for b in range(B):
                pe.wait_ge(xn_ready, call * B + b + 1)
                if b >= 2:
                    pe.wait_ge(xnT_ready, turned + b - 1)
                for t in range(T):
                    ins = pe.transpose(bank(b % 2)[:, t * P:t * P + P], xn[:, b * T + t, :], ident[:, :])
                ins.then_inc(xn_turned, 1)
                if call in RMS and b >= 1:
                    logits(b - 1)
            if call in RMS:
                logits(B - 1)
                for b in range(B):
                    pe.wait_ge(rn_ready, which * B + b + 1)
                    pe.wait_ge(xnT_ready, turned + B)
                    for t in range(T):
                        ins = pe.transpose(bank(RN_BANK[b])[:, t * P:t * P + P], rn[:, b * T + t, :], ident[:, :])
                    ins.then_inc(xn_turned, 1)

        def norm_scalar(act, step, call, done):
            turned = before(n_turn, call)
            act.wait_ge(turn_done, done)
            for b in range(B):
                act.wait_ge(xn_turned, turned + b + 1)
                src, dst = bank(b % 2), xnT[:, b * S:b * S + S]
                if call == TWICE:
                    ins = act.activation(dst, src, ACT.Identity, bias=col("L1_xattn_ln_b"), scale=col("L1_xattn_ln_g"))
                else:
                    ins = act.copy(dst, src)
                ins.then_inc(xnT_ready, 1)
                if call in RMS:
                    for t in range(T):
                        n = b * T + t
                        ins = act.activation(rn[:, n, :], xn[:, n, :], ACT.Square, accum_out=squares[:, n:n + 1])
                    ins.then_inc(squares_ready, 1)

        def rms_scalar(act, call):
            turned = before(n_turn, call) + B
            act.wait_ge(logits_ready, RMS.index(call) + 1)
            gain = col("L0_ffn_gamma_l" if call == RMS[0] else "L1_ffn_gamma_light")
            for b in range(B):
                act.wait_ge(xn_turned, turned + b + 1)
                act.mul(xnT[:, b * S:b * S + S], bank(RN_BANK[b]), gain).then_inc(xnT_ready, 1)

        RN_BANK = [0, 1, 6, 7]
        squares_ready = sem("squares_ready")
        logits_ready = sem("logits_ready")

        sw = carve({"kT": B * KC, "Kbd": B * H * KC, "vs": B * NCH * D, "Vbd": B * 2 * NCH * HH * 9, "qT": S,
                    "bias": 2 * H * KC, "mask": 2 * KC, "maskf": 2 * KC, "sc": 4 * HK, "mx": 4 * HH,
                    "pT": 2 * NCH * P, "rec": 2 * HH, "o": T * D, "oT": S, "x1": S, "yT": S})
        kT_s = sw["kT"].rearrange("p (b k) -> p b k", b=B)
        Kbd = sw["Kbd"].rearrange("p (b h k) -> p b h k", b=B, h=H)
        vs = sw["vs"].rearrange("p (b c d) -> p b c d", b=B, c=NCH)
        Vbd = sw["Vbd"].rearrange("p (b f c h e) -> p b f c h e", b=B, f=2, c=NCH, h=HH)
        qT_s = sw["qT"]
        bias_s = sw["bias"].rearrange("p (n h k) -> p n h k", n=2, h=H)
        mask_s = sw["mask"].rearrange("p (n k) -> p n k", n=2)
        maskf = sw["maskf"].rearrange("p (n k) -> p n k", n=2)
        sc_s = sw["sc"].rearrange("p (n h k) -> p n h k", n=4, h=HH)
        pr_s = sw["sc"].rearrange("p (n k) -> p n k", n=4)
        mx_s = sw["mx"].rearrange("p (n h) -> p n h", n=4)
        pT_s = sw["pT"].rearrange("p (n k) -> p n k", n=2)
        rec_s = sw["rec"].rearrange("p (n h) -> p n h", n=2)
        o_s = sw["o"].rearrange("p (n d) -> p n d", n=T)
        x1 = sw["x1"].rearrange("p (t d) -> p t d", t=T)
        sc_at = sum(n for n in (B * KC, B * H * KC, B * NCH * D, B * 2 * NCH * HH * 9, S, 2 * H * KC, 2 * KC, 2 * KC))
        bias_at = sc_at - 2 * H * KC - 4 * KC
        ctx8 = work[:, sc_at:sc_at + B * HK].rearrange("p (b h k) -> p b h k", b=B, h=HH)
        sigT = work[:, bias_at:bias_at + 2 * NCH * S].rearrange("p (u q) -> p u q", u=2 * NCH)
        h_s = work[:, sc_at:sc_at + NF * S].rearrange("p (f q) -> p f q", f=NF)
        assert 2 * NCH * S <= 2 * H * KC + 4 * KC + 4 * HK and NF * S <= 4 * HK
        U = 2 * T

        ctx_here = sem("ctx_here")
        vs_zero, ones_set = sem("vs_zero"), sem("ones_set")
        kv_proj, kv_out, kv_bias = sem("kv_proj"), sem("kv_out"), sem("kv_bias")
        kv_ready = Signal(sem("kv_ready"), 1)
        q_proj, q_ready = Signal(sem("q_proj"), 1), Signal(sem("q_ready"), 1)
        bias_in = [Signal(sem(f"bias_in{i}"), 2 * 16) for i in range(2)]
        mask_in = [Signal(sem(f"mask_in{i}"), 2 * 16) for i in range(2)]
        mask_seen = sem("mask_seen")
        bq_scaled = sem("bq_scaled")
        masked = Signal(sem("masked"), T)
        s_scores = Signal(sem("s_scores"), U)
        s_read = Signal(sem("s_read"), U)
        s_max = Signal(sem("s_max"), U)
        s_shift = [Signal(sem(f"s_shift{i}"), T) for i in range(2)]
        s_probs = Signal(sem("s_probs"), U)
        s_turned = Signal(sem("s_turned"), U)
        s_pT = Signal(sem("s_pT"), U)
        s_av = Signal(sem("s_av"), U)
        s_o = Signal(sem("s_o"), U)
        o_turned = Signal(sem("o_turned"), 1)
        o_ready = Signal(sem("o_ready"), 1)
        o_out = Signal(sem("o_out"), 1)
        o_read = Signal(sem("o_read"), 1, 1)
        f_var, f_rstd = Signal(sem("f_var"), 1), Signal(sem("f_rstd"), 1)

        SMALL = ["L0_xattn", "L2_xattn", "L3_xattn"]
        rows_of = [P] * (NCH - 1) + [LASTR]

        def need(engine, signal, value):
            if not isinstance(value, int) or value > 0:
                engine.wait_ge(signal.sem, value)

        def kv_pool(pool, step, use, done):
            pool.wait_ge(turn_done, done)
            pool.memset(vs[:, :, NCH - 1, :], 0.0).then_inc(vs_zero, 1)
            pool.tensor_copy(sw["Vbd"].rearrange("p (n r e) -> p n r e", n=2 * B, e=9)[:, :, :, 8:9],
                             head_of_key[:, :, :].rearrange("p c h -> p (c h)").unsqueeze(1).unsqueeze(3)
                             .to_broadcast([P, 2 * B, NCH * HH, 1])).then_inc(ones_set, 1)

        def values_bias(pool, use):
            for b in range(B):
                pool.wait_ge(kv_out, use * B + b + 1)
                pool.tensor_tensor(vs[:, b], vs[:, b],
                                   row(SMALL[use] + "_bv").unsqueeze(1).to_broadcast([P, NCH, D]), ALU.add)\
                    .then_inc(kv_bias, 1)

        def kv_tensor(pe, use, done):
            name = SMALL[use]
            pe.wait_ge(turn_done, done)
            pe.wait_ge(mats_loaded[0 if use == 0 else 5], 16)
            if use == 0:
                pe.wait_ge(ctx_loaded, 16)
            for b in range(B):
                pe.wait_ge(ctx_here, use * B + b + 1)
                a = 2 + 2 * (b % 3)
                if b >= 3:
                    pe.wait_ge(kv_out, use * B + b - 2)
                pe.matmul(bank(a)[:, 0:KC], mat(name + "_Wk"), ctxT[:, b, :], start=True, stop=True)
                flat = ctx8[:, b].rearrange("p h k -> p (h k)")
                for c, n in enumerate(rows_of):
                    to = bank(a + 1)[:, c * P:c * P + P] if c < 4 else bank(a)[0:n, P:2 * P]
                    ins_ = pe.matmul(to, flat[:, c * P:c * P + n], mat(name + "_Wv"), start=True, stop=True)
                ins_.then_inc(kv_proj, 1)

        def kv_scalar(act, step, use, done):
            act.wait_ge(turn_done, done)
            if use == 0:
                act.wait_ge(ctx_loaded, 16)
            for b in range(B):
                act.copy(ctx8[:, b], ctxT[:, b:b + 1, :].to_broadcast([P, HH, KC])).then_inc(ctx_here, 1)
            act.wait_ge(vs_zero, use + 1)
            for b in range(B):
                a = 2 + 2 * (b % 3)
                act.wait_ge(kv_proj, use * B + b + 1)
                if use == 0:
                    act.copy(kT_s[:, b], bank(a)[:, 0:KC])
                else:
                    act.activation(kT_s[:, b], bank(a)[:, 0:KC], ACT.Identity, bias=col(SMALL[use] + "_bk"))
                act.copy(vs[0:LASTR, b, 4, :], bank(a)[0:LASTR, P:2 * P])
                act.copy(vs[:, b, 0:4, :], bank(a + 1).rearrange("p (c d) -> p c d", c=4)).then_inc(kv_out, 1)

        def spread_values(dve, b):
            for half in range(2):
                last = dve.tensor_tensor(
                    Vbd[:, b, half, :, :, 0:8],
                    vs[:, b, :, half * 64:half * 64 + 64].rearrange("p c (h e) -> p c h e", e=DK),
                    head_of_key[:, :, :].unsqueeze(3).to_broadcast([P, NCH, HH, DK]), ALU.mult)
            return last

        def q_projection(pe, use, b):
            g = b + use * B
            need(pe, o_read, o_read.at(g, -1))
            pe.wait_ge(xnT_ready, b + xnT_count([0, 4, 6][use]) - B + 1)
            pe.matmul(bank(7), mat(SMALL[use] + "_Wq"), xnT[:, ds(b * S, S)], start=True, stop=True)\
                .then_inc(q_proj.sem, 1)

        def evacuate_q(act, use, b):
            act.wait_ge(q_proj.sem, q_proj.at(b + use * B, 1))
            if use == 0:
                ins_ = act.mul(qT_s, bank(7), float(DK) ** -0.5)
            else:
                act.wait_ge(bq_scaled, 2)
                ins_ = act.activation(qT_s, bank(7), ACT.Identity, bias=bq_s[:, use - 1:use], scale=float(DK) ** -0.5)
            ins_.then_inc(q_ready.sem, 1)

        def residual(dve, step, use, done, g, b):
            dve.wait_ge(turn_done, b + done)
            dve.wait_ge(o_out.sem, o_out.at(g, 0))
            out4 = bank(7).rearrange("p (t d) -> p t d", t=T)
            xb = x[:, ds(b * T, T), :]
            step(dve.tensor_tensor(x1, out4, row(SMALL[use] + "_bo").unsqueeze(1).to_broadcast([P, T, D]), ALU.add))
            dve.sem_inc(o_read.sem, 1)
            dve.scalar_tensor_tensor(out=xb, in0=x1, scalar=tg[:, use + 1:use + 2], in1=xb, op0=ALU.mult,
                                     op1=ALU.add).then_inc(turn_done, 1)

        def load_matrices(sp, i):
            first, past = MAT_PARTS[i]
            a, z = MAT_AT[first][0], MAT_AT[past][0] if past else NMAT
            sp.dma_start(mats[:, a:z], ins["mats"][:, a:z]).then_inc(mats_loaded[i], 16)

        def attend_sync(sp, use, done):
            sp.wait_ge(turn_done, done)

            def turn(b):
                g = b + use * B
                for t in range(T):
                    need(sp, s_read, s_read.at(g, 2 * (t - 1)))
                    sp.dma_start(bias_s[:, t % 2], ins["bias"][ds(b * T + t, 1)].rearrange(
                        "a p (h k) -> p (a h) k", h=H)).then_inc(bias_in[t % 2].sem, 16)
                    if use == 1:
                        sp.dma_start(mask_s[:, t % 2].bitcast(I32), ins["mask"][ds(b * T + t, 1)].rearrange(
                            "a p k -> p (a k)")).then_inc(mask_in[t % 2].sem, 16)
                    if use == 0 and t == 1 and isinstance(b, int):
                        for i in range(1, len(MAT_PARTS)):
                            load_matrices(sp, i)

            turn(0)
            with sp.Fori(1, B) as b:
                turn(b)

        def by_pool(use, u):
            return use == 0 or u % 2 == 0

        def subtract_max(engine, g, u):
            return engine.tensor_tensor(sc_s[:, u % 4], sc_s[:, u % 4],
                                        mx_s[:, u % 4].unsqueeze(2).to_broadcast([P, HH, KC]), ALU.subtract)\
                .then_inc(s_shift[u % 2].sem, 1)

        def attend_pool(pool, step, use, done):
            def mask(b, g, t):
                pool.wait_ge(mask_in[t % 2].sem, mask_in[t % 2].at(b, 16 * (t // 2 + 1)))
                pool.sem_inc(mask_seen, 1)
                step(pool.tensor_scalar(maskf[:, t % 2], mask_s[:, t % 2].bitcast(I32), 0, MASKED,
                                        ALU.is_equal, ALU.mult))
                pool.wait_ge(bias_in[t % 2].sem, bias_in[t % 2].at(g, 16 * (t // 2 + 1)))
                pool.tensor_tensor(bias_s[:, t % 2], bias_s[:, t % 2],
                                   maskf[:, t % 2].unsqueeze(1).to_broadcast([P, H, KC]), ALU.add)\
                    .then_inc(masked.sem, 1)

            def power(b):
                pool.wait_ge(f_var.sem, f_var.at(b, 0))
                pool.tensor_tensor(rstd[:, 0:T], varr[:, 0:T], expo[:, 0:T], ALU.pow).then_inc(f_rstd.sem, 1)

            def turn(b, first):
                g = b + use * B
                if use == 1:
                    mask(b, g, 0)
                for u in range(U):
                    if by_pool(use, u):
                        pool.wait_ge(s_max.sem, s_max.at(g, u + 1))
                        subtract_max(pool, g, u)
                    if use == 1 and u % 2 == 0 and u // 2 + 1 < T:
                        mask(b, g, u // 2 + 1)
                    if use == 0 and u == 6 and not first:
                        power(b)

            per = T if use == 1 else 0
            if use == 1:
                values_bias(pool, use)
            turn(0, True)
            with step.loop(B - 1, per, 1) as b:
                turn(b, False)
            if use == 0:
                power(B)

        def attend_tensor(pe, use, done):
            name = SMALL[use]
            pe.wait_ge(kv_out, (use + 1) * B)

            def scores(b, g, u):
                need(pe, s_read, s_read.at(g, u - 1))
                if u == 0:
                    pe.wait_ge(q_ready.sem, q_ready.at(g, 1))
                    pe.wait_ge(kv_ready.sem, kv_ready.at(g, 1))
                    pe.wait_ge(xnT_ready, xnT_count([0, 4, 6][use]))
                t, half = divmod(u, 2)
                for j in range(2):
                    h = half * HH + 4 * j
                    ins_ = pe.matmul(bank(2 * (u % 2) + j)[:, 0:4 * KC], qT_s[:, t * P:t * P + P],
                                     Kbd[:, ds(b, 1), h:h + 4, :].rearrange("p a h k -> p (a h) k"),
                                     start=True, stop=True)
                ins_.then_inc(s_scores.sem, 1)

            def turn_probs(g, u):
                pe.wait_ge(s_probs.sem, s_probs.at(g, u + 1))
                need(pe, s_pT, s_pT.at(g, u))
                for c, n in enumerate(rows_of):
                    to = bank(4)[:, c * P:c * P + P] if c < 4 else bank(5)[0:n, 0:P]
                    ins_ = pe.transpose(to, pr_s[:, u % 4, c * P:c * P + n], ident[:, :])
                ins_.then_inc(s_turned.sem, 1)

            def av(b, g, u):
                pe.wait_ge(s_pT.sem, s_pT.at(g, u + 1))
                need(pe, s_o, s_o.at(g, u))
                for c, n in enumerate(rows_of):
                    ins_ = pe.matmul(bank(6)[:, 0:72], pT_s[0:n, u % 2, c * P:c * P + P],
                                     Vbd[0:n, ds(b, 1), u % 2, c, :, :].rearrange("p a h e -> p (a h) e"),
                                     start=(c == 0), stop=(c == NCH - 1))
                ins_.then_inc(s_av.sem, 1)

            def turn_o(g):
                pe.wait_ge(s_o.sem, s_o.at(g, 0))
                for t in range(T):
                    ins_ = pe.transpose(bank(7)[:, t * P:t * P + P], o_s[:, t, :], ident[:, :])
                ins_.then_inc(o_turned.sem, 1)

            def project(g):
                pe.wait_ge(o_ready.sem, o_ready.at(g, 0))
                for t in range(T):
                    ins_ = pe.matmul(bank(7)[:, t * P:t * P + P], sw["oT"][:, t * P:t * P + P], mat(name + "_Wo"),
                                     start=True, stop=True)
                ins_.then_inc(o_out.sem, 1)

            def turn(b, first):
                g = b + use * B
                q_projection(pe, use, b)
                for u in range(U):
                    if u > 0:
                        scores(b, g, u)
                    if u >= 3:
                        av(b, g, u - 3)
                    elif not first:
                        av(b - 1, g, u - 3)
                    if u == 0:
                        scores(b, g, 0)
                    if u >= 2 or not first:
                        turn_probs(g, u - 2)
                    if u == 3 and not first:
                        turn_o(g)
                    if u == 4 and not first:
                        project(g)

            turn(0, True)
            with pe.Fori(1, B) as b:
                turn(b, False)
            end = (use + 1) * B
            av(B - 1, end, -3)
            turn_probs(end, -2)
            av(B - 1, end, -2)
            turn_probs(end, -1)
            av(B - 1, end, -1)
            pe.wait_ge(o_read.sem, o_read.at(end, -1))
            turn_o(end)
            project(end)

        def attend_scalar(act, step, use, done):
            def probs(g, u):
                s = s_shift[u % 2]
                act.wait_ge(s.sem, s.at(g, u // 2 + 1))
                act.activation(pr_s[:, u % 4], sc_s[:, u % 4], ACT.Exp).then_inc(s_probs.sem, 1)

            def copy_pT(g, u):
                act.wait_ge(s_turned.sem, s_turned.at(g, u + 1))
                need(act, s_av, s_av.at(g, u - 1))
                act.copy(pT_s[:, u % 2, 0:4 * P], bank(4))
                act.copy(pT_s[0:LASTR, u % 2, 4 * P:5 * P], bank(5)[0:LASTR, 0:P])\
                    .then_inc(s_pT.sem, 1)

            def copy_oT(g):
                act.wait_ge(o_turned.sem, o_turned.at(g, 0))
                act.copy(sw["oT"], bank(7)).then_inc(o_ready.sem, 1)

            def turn(b, first):
                g = b + use * B
                for u in range(U):
                    if u >= 2 or not first:
                        copy_pT(g, u - 2)
                    probs(g, u)
                    if u == 3 and not first:
                        copy_oT(g)

            turn(0, True)
            with act.Fori(1, B) as b:
                turn(b, False)
            end = (use + 1) * B
            copy_pT(end, -2)
            copy_pT(end, -1)
            copy_oT(end)

        def attend_vector(dve, step, use, done):
            name = SMALL[use]

            def prepare(b):
                if use > 0:
                    dve.wait_ge(kv_bias, use * B - B + b + 1)
                dve.wait_ge(kv_out, use * B + b + 1)
                dve.tensor_tensor(Kbd[:, b], kT_s[:, b].unsqueeze(1).to_broadcast([P, H, KC]),
                                  head_of_row[:, :].unsqueeze(2).to_broadcast([P, H, KC]), ALU.mult)
                spread_values(dve, b).then_inc(kv_ready.sem, 1)

            def shift(g, u):
                t, half = divmod(u, 2)
                dve.wait_ge(s_scores.sem, s_scores.at(g, u + 1))
                if use == 0:
                    dve.wait_ge(bias_in[t % 2].sem, bias_in[t % 2].at(g, 16 * (t // 2 + 1)))
                else:
                    dve.wait_ge(masked.sem, masked.at(g - B, t + 1))
                need(dve, s_turned, s_turned.at(g, u - 3))
                two = bank(2 * (u % 2), 2).rearrange("p (j n) -> p j n", j=2)[:, :, 0:4 * KC]
                dve.tensor_tensor(sc_s[:, u % 4].rearrange("p (j h) k -> p j (h k)", j=2), two,
                                  bias_s[:, t % 2, half * HH:half * HH + HH].rearrange("p (j h) k -> p j (h k)", j=2),
                                  ALU.add).then_inc(s_read.sem, 1)
                dve.wait_ge(s_read.sem, s_read.at(g, u + 1))
                dve.tensor_reduce(mx_s[:, u % 4], sc_s[:, u % 4], X, ALU.max).then_inc(s_max.sem, 1)
                if not by_pool(use, u):
                    dve.wait_ge(s_max.sem, s_max.at(g, u + 1))
                    subtract_max(dve, g, u)

            def norm_o(g, u):
                t, half = divmod(u % U, 2)
                o9 = bank(6)[:, 0:72].rearrange("p (h e) -> p h e", e=9)
                dve.wait_ge(s_av.sem, s_av.at(g, u + 1))
                if u == 0:
                    need(dve, o_turned, o_turned.at(g, 0))
                dst = o_s[:, t, half * 64:half * 64 + 64].rearrange("p (h e) -> p h e", e=DK)
                step(dve.reciprocal(rec_s[:, u % 2].unsqueeze(2), o9[:, :, 8:9]))
                dve.tensor_tensor(dst, o9[:, :, 0:8], rec_s[:, u % 2].unsqueeze(2).to_broadcast([P, HH, DK]),
                                  ALU.mult).then_inc(s_o.sem, 1)

            def add_input(g, b):
                dve.wait_ge(o_out.sem, o_out.at(g, 0))
                x1b = rn[:, ds(b * T, T), :]
                step(dve.tensor_tensor(x1b, bank(7).rearrange("p (t d) -> p t d", t=T), xn[:, ds(b * T, T), :], ALU.add))
                dve.sem_inc(o_read.sem, 1)

            def stats_x1(b):
                for t in range(T):
                    step.mark(dve.bn_stats(stat[:, t, :], rn[:, ds(b * T + t, 1), :]))
                step.wait()
                dve.memset(spare[:, :], 0.0)
                for t in range(T):
                    step.mark(dve.bn_aggr(mv[:, t, :], stat[:, t, :]))
                step.wait()
                dve.tensor_scalar(varr[:, 0:T], mv[:, 0:T, 1], EPS, None, ALU.add).then_inc(f_var.sem, 1)

            def norm_x1(g, b):
                dve.wait_ge(f_rstd.sem, f_rstd.at(g, 0))
                for t in range(T):
                    ins_ = dve.tensor_scalar(xn[:, ds(b * T + t, 1), :], rn[:, ds(b * T + t, 1), :], mv[:, t, 0:1],
                                             rstd[:, t:t + 1], ALU.subtract, ALU.mult)
                ins_.then_inc(turn_done, 1)

            def queries(g):
                dve.wait_ge(q_proj.sem, q_proj.at(g, 1))
                if use == 0:
                    ins_ = dve.tensor_scalar(qT_s, bank(7), float(DK) ** -0.5, None, ALU.mult)
                else:
                    ins_ = dve.tensor_scalar(qT_s, bank(7), col(name + "_bq"), float(DK) ** -0.5, ALU.add, ALU.mult)
                ins_.then_inc(q_ready.sem, 1)

            def turn(b, first):
                g = b + use * B
                queries(g)
                for u in range(U):
                    if u == 0:
                        if not first:
                            norm_o(g, -3)
                        shift(g, 0)
                    else:
                        shift(g, u)
                        if u >= 3 or not first:
                            norm_o(g, u - 3)
                    if first and u in (2, 4, 6):
                        prepare(u // 2)
                    if u == 5 and not first:
                        residual(dve, step, use, done, g, b - 1) if use else add_input(g, b - 1)
                    if u == 6 and not first and not use:
                        stats_x1(b - 1)
                    if u == 7 and not first and not use:
                        norm_x1(g, b - 1)

            dve.wait_ge(consts_ready, CONSTS)
            dve.wait_ge(ones_set, use + 1)
            prepare(0)
            dve.wait_ge(kv_out, (use + 1) * B)
            turn(0, True)
            with step.loop(B - 1, U + (9 if use == 0 else 1), 1) as b:
                turn(b, False)
            end = (use + 1) * B
            for u in (-3, -2, -1):
                norm_o(end, u)
            if use:
                residual(dve, step, use, done, end, B - 1)
            else:
                add_input(end, B - 1)
                stats_x1(B - 1)
                norm_x1(end, B - 1)

        f_turn = Signal(sem("f_turn"), 1)
        f_yT = Signal(sem("f_yT"), 1)
        f_h, f_gelu = Signal(sem("f_h"), NF), Signal(sem("f_gelu"), NF)
        f_out = Signal(sem("f_out"), 1)
        f_read = Signal(sem("f_read"), 1, 1)
        f_var2, f_rstd2 = Signal(sem("f_var2"), 1), Signal(sem("f_rstd2"), 1)


        f_y = Signal(sem("f_y"), 1)

        def ffn0_pool(pool, step, use, done):
            routing_constants(pool, step)
            pool.wait_ge(turn_done, done)
            with pool.Fori(0, B) as b:
                pool.wait_ge(f_var2.sem, f_var2.at(b, 1))
                pool.tensor_tensor(rstd[:, 0:T], varr[:, 0:T], expo[:, 0:T], ALU.pow).then_inc(f_rstd2.sem, 1)

        def ffn0_tensor(pe, use, done):
            pe.wait_ge(mats_loaded[1], 16)
            pe.wait_ge(turn_done, done)
            with pe.Fori(0, B) as b:
                pe.wait_ge(f_y.sem, f_y.at(b, 1))
                for t in range(T):
                    ins_ = pe.transpose(bank(7)[:, t * P:t * P + P], o_s[:, t, :], ident[:, :])
                ins_.then_inc(f_turn.sem, 1)
                pe.wait_ge(f_yT.sem, f_yT.at(b, 1))
                for f in range(NF):
                    pe.matmul(bank(f), mat("L0_xattn_W1", f * P), sw["yT"], start=True, stop=True).then_inc(f_h.sem, 1)
                pe.wait_ge(f_gelu.sem, f_gelu.at(b, NF))
                pe.wait_ge(f_read.sem, f_read.at(b, 0))
                for t in range(T):
                    for f in range(NF):
                        ins_ = pe.matmul(bank(6)[:, t * P:t * P + P], h_s[:, f, t * P:t * P + P],
                                         mat("L0_xattn_W2", f * P), start=(f == 0), stop=(f == NF - 1))
                ins_.then_inc(f_out.sem, 1)

        def ffn0_scalar(act, step, use, done):
            gates(act)
            act.wait_ge(turn_done, done)
            with act.Fori(0, B) as b:
                act.copy(o_s, xn[:, ds(b * T, T), :]).then_inc(f_y.sem, 1)
                act.wait_ge(f_turn.sem, f_turn.at(b, 1))
                act.activation(sw["yT"], bank(7), ACT.Identity, scale=col("L0_xattn_g1"), bias=col("L0_xattn_be1"))\
                    .then_inc(f_yT.sem, 1)
                for f in range(NF):
                    act.wait_ge(f_h.sem, f_h.at(b, f + 1))
                    act.activation(h_s[:, f, :], bank(f), ACT.Gelu, bias=col("L0_xattn_b1", f)).then_inc(f_gelu.sem, 1)

        def ffn0_vector(dve, step, use, done):
            dve.wait_ge(gates_ready, 1)
            dve.sem_inc(f_read.sem, f_read.ahead)
            with step.loop(B, 2 + 2 * T + T + 2) as b:
                dve.wait_ge(turn_done, b + done)
                dve.wait_ge(f_out.sem, f_out.at(b, 1))
                x1b, xb = rn[:, ds(b * T, T), :], x[:, ds(b * T, T), :]
                step(dve.tensor_tensor(x1, bank(6).rearrange("p (t d) -> p t d", t=T), x1b, ALU.add))
                dve.sem_inc(f_read.sem, 1)
                step(dve.tensor_tensor(x1, x1, row("L0_xattn_b2").unsqueeze(1).to_broadcast([P, T, D]), ALU.add))
                for t in range(T):
                    step.mark(dve.bn_stats(stat[:, t, :], x1[:, t, :]))
                step.wait()
                dve.memset(spare[:, :], 0.0)
                for t in range(T):
                    step.mark(dve.bn_aggr(mv[:, t, :], stat[:, t, :]))
                step.wait()
                dve.tensor_scalar(varr[:, 0:T], mv[:, 0:T, 1], EPS, None, ALU.add).then_inc(f_var2.sem, 1)
                dve.wait_ge(f_rstd2.sem, f_rstd2.at(b, 1))
                for t in range(T):
                    step.mark(dve.tensor_scalar(x1[:, t, :], x1[:, t, :], mv[:, t, 0:1], rstd[:, t:t + 1],
                                                ALU.subtract, ALU.mult))
                step.wait()
                step(dve.tensor_tensor(x1, x1, row("L0_xattn_g2").unsqueeze(1).to_broadcast([P, T, D]), ALU.mult))
                step(dve.tensor_tensor(x1, x1, row("L0_xattn_be2").unsqueeze(1).to_broadcast([P, T, D]), ALU.add))
                dve.scalar_tensor_tensor(out=xb, in0=x1, scalar=tg[:, 0:1], in1=xb, op0=ALU.mult,
                                         op1=ALU.add).then_inc(turn_done, 1)

        g_keys = Signal(sem("g_keys"), 2)
        g_scores = Signal(sem("g_scores"), 2 * NCH)
        g_sig = Signal(sem("g_sig"), 2 * NCH)
        g_av = Signal(sem("g_av"), 2)
        g_o = Signal(sem("g_o"), 2, 1)

        def gated_pool(pool, step, use, done):
            values_bias(pool, use)

        def gated_tensor(pe, use, done):
            name = SMALL[use]
            pe.wait_ge(kv_out, (use + 1) * B)

            def scores(b, half):
                pe.wait_ge(g_keys.sem, g_keys.at(b, half + 1))
                if half == 0:
                    pe.wait_ge(q_ready.sem, q_ready.at(b + use * B, 1))
                keys = Kbd[:, 0, half * HH:half * HH + HH, :].rearrange("p h k -> p (h k)")
                for c, n in enumerate(rows_of):
                    need(pe, g_sig, g_sig.at(b, half * NCH + c + 1 - NCH))
                    pe.matmul(bank(c)[0:n, :], keys[:, c * P:c * P + n], qT_s, start=True, stop=True)\
                        .then_inc(g_scores.sem, 1)

            def av(b, turn, half):
                pe.wait_ge(g_sig.sem, g_sig.at(turn, NCH * (half + 1)))
                need(pe, g_o, g_o.at(turn, half - 1))
                h = half % 2
                pe.wait_ge(kv_ready.sem, (use + 1) * B)
                for t in range(T):
                    for c, n in enumerate(rows_of):
                        ins_ = pe.matmul(bank(5 + h)[:, t * 72:t * 72 + 72], sigT[0:n, h * NCH + c, t * P:t * P + P],
                                         Vbd[0:n, ds(b, 1), h, c, :, :].rearrange("p a h e -> p (a h) e"),
                                         start=(c == 0), stop=(c == NCH - 1))
                ins_.then_inc(g_av.sem, 1)

            def turn_o(turn):
                pe.wait_ge(g_o.sem, g_o.at(turn, 0))
                for t in range(T):
                    ins_ = pe.transpose(bank(7)[:, t * P:t * P + P], o_s[:, t, :], ident[:, :])
                ins_.then_inc(o_turned.sem, 1)

            def project(g):
                pe.wait_ge(o_ready.sem, o_ready.at(g, 0))
                for t in range(T):
                    ins_ = pe.matmul(bank(7)[:, t * P:t * P + P], sw["oT"][:, t * P:t * P + P], mat(name + "_Wo"),
                                     start=True, stop=True)
                ins_.then_inc(o_out.sem, 1)

            def turn(b, first):
                q_projection(pe, use, b)
                if not first:
                    av(b - 1, b, -1)
                scores(b, 0)
                if not first:
                    turn_o(b)
                scores(b, 1)
                if not first:
                    project(b + use * B)
                av(b, b, 0)

            turn(0, True)
            with pe.Fori(1, B) as b:
                turn(b, False)
            av(B - 1, B, -1)
            pe.wait_ge(o_read.sem, o_read.at((use + 1) * B, -1))
            turn_o(B)
            project((use + 1) * B)

        def gated_scalar(act, step, use, done):
            def copy_oT(g):
                act.wait_ge(o_turned.sem, o_turned.at(g, 0))
                act.copy(sw["oT"], bank(7)).then_inc(o_ready.sem, 1)

            def turn(b, first):
                evacuate_q(act, use, b)
                for u in range(2 * NCH):
                    if u % NCH == 0:
                        need(act, g_av, g_av.at(b, u // NCH - 1))
                    if u == NCH and not first:
                        copy_oT(b + use * B)
                    n = rows_of[u % NCH]
                    act.wait_ge(g_scores.sem, g_scores.at(b, u + 1))
                    act.activation(sigT[0:n, u, :], bank(u % NCH)[0:n, :], ACT.Sigmoid).then_inc(g_sig.sem, 1)

            turn(0, True)
            with act.Fori(1, B) as b:
                turn(b, False)
            copy_oT((use + 1) * B)

        def gated_vector(dve, step, use, done):
            def keys(b, half):
                need(dve, g_scores, g_scores.at(b, NCH * (half - 1)))
                dve.tensor_tensor(Kbd[:, 0, half * HH:half * HH + HH, :],
                                  kT_s[:, ds(b, 1), :].to_broadcast([P, HH, KC]),
                                  head_of_row[:, half * HH:half * HH + HH].unsqueeze(2).to_broadcast([P, HH, KC]),
                                  ALU.mult).then_inc(g_keys.sem, 1)

            def copy_o(turn, half):
                dve.wait_ge(g_av.sem, g_av.at(turn, half + 1))
                if half == 0:
                    need(dve, o_turned, o_turned.at(turn + use * B, 0))
                h = half % 2
                o9 = bank(5 + h)[:, 0:T * 72].rearrange("p (t h e) -> p t h e", t=T, e=9)
                dve.tensor_copy(o_s[:, :, h * 64:h * 64 + 64].rearrange("p t (h e) -> p t h e", e=DK), o9[:, :, :, 0:8])\
                    .then_inc(g_o.sem, 1)

            def turn(b, first):
                for half in range(2):
                    keys(b, half)
                if first:
                    for i in range(B):
                        dve.wait_ge(kv_bias, (use - 1) * B + i + 1)
                        spread_values(dve, i).then_inc(kv_ready.sem, 1)
                else:
                    copy_o(b, -1)
                    residual(dve, step, use, done, b + use * B, b - 1)
                copy_o(b, 0)

            dve.sem_inc(g_o.sem, g_o.ahead)
            dve.wait_ge(ones_set, use + 1)
            dve.wait_ge(kv_out, (use + 1) * B)
            turn(0, True)
            with step.loop(B - 1, 1, 1) as b:
                turn(b, False)
            copy_o(B, -1)
            residual(dve, step, use, done, (use + 1) * B, B - 1)


        ROUND, ROUNDS = 16, 3
        LIFT, CAP = 30.0, 25.0
        assert 2 + ROUND * ROUNDS == DESCENT
        R8 = 2 * B
        K_OF = [(NQ * 9 / 8, NQ * 9 / 8), (NQ * 9 / 8, NKV * 9 / 8)]
        k_inv = sb("k_inv", [R8, 2, S])
        k_log = sb("k_log", [R8, 2])
        k_col = sb("k_col", [R8, 2])
        k_exp, k_ln = sb("k_exp", [R8, 2]), sb("k_ln", [R8, 2])
        d_s, d_e = sb("d_s", [R8, S]), sb("d_e", [R8, S])
        d_sum = sb("d_sum", [R8, 2])
        d_c, d_m, d_ln = sb("d_c", [R8, 1]), sb("d_m", [R8, 1]), sb("d_ln", [R8, 1])
        col_s = sb("col_s", [P, T, R8])
        col_w = sb("col_w", [P, T, R8])
        d_arg = Signal(sem("d_arg"), ROUNDS + 2)
        d_exp = Signal(sem("d_exp"), ROUNDS + 2)
        d_total = Signal(sem("d_total"), ROUNDS + 1)
        d_log = Signal(sem("d_log"), ROUNDS + 1)
        c_turned, c_read = sem("c_turned"), sem("c_read")
        b_spread, b_read = sem("b_spread"), sem("b_read")

        def descent_vector(dve, step, which, bc, nrow):
            k1 = lambda: k_inv[:, which, :]
            dve.wait_ge(routing_ready, 1)
            dve.wait_ge(logits_ready, which + 1)
            step(dve.tensor_copy(d_s[:, :], bank(2)[0:R8, :]))
            step(dve.tensor_scalar(d_c[:, :], k_log[:, which:which + 1], -1.0, float(np.log(S)), ALU.mult, ALU.add))
            step(dve.tensor_scalar(d_e[:, :], d_s[:, :], d_c[:, :], None, ALU.min))
            step(dve.tensor_reduce(d_m[:, :], d_e[:, :], X, ALU.max))
            dve.tensor_scalar(d_e[:, :], d_e[:, :], d_m[:, :], None, ALU.subtract).then_inc(d_arg.sem, 1)
            dve.wait_ge(d_exp.sem, d_exp.at(which, 1))
            dve.tensor_reduce(d_sum[:, 0:1], d_e[:, :], X, ALU.add).then_inc(d_total.sem, 1)
            dve.wait_ge(d_log.sem, d_log.at(which, 1))
            step(dve.tensor_tensor(d_c[:, :], d_m[:, :], d_ln[:, :], ALU.add))
            with step.loop(ROUNDS, ROUND + 2) as r:
                step(dve.tensor_scalar(d_e[:, :], d_s[:, :], d_c[:, :], CAP, ALU.subtract, ALU.min))
                dve.sem_inc(d_arg.sem, 1)
                dve.wait_ge(d_exp.sem, r + d_exp.at(which, 2))
                total = k_col[:, which:which + 1]
                for i in range(ROUND):
                    nxt = d_sum[:, i % 2:i % 2 + 1]
                    step(dve.scalar_tensor_tensor(out=junk[0:R8, :], in0=d_e[:, :], scalar=total, in1=k1(),
                                                  op0=ALU.min, op1=ALU.mult, accum_out=nxt))
                    total = nxt
                dve.sem_inc(d_total.sem, 1)
                dve.wait_ge(d_log.sem, r + d_log.at(which, 2))
                step(dve.tensor_tensor(d_c[:, :], d_c[:, :], d_ln[:, :], ALU.add))
            dve.tensor_scalar(d_e[:, :], d_s[:, :], d_c[:, :], 0.0, ALU.subtract, ALU.min).then_inc(d_arg.sem, 1)
            dve.wait_ge(c_turned, which + 1)
            dve.tensor_copy(col_s[:, :, :], bank(3)[:, 0:T * R8].rearrange("p (t r) -> p t r", t=T)).then_inc(c_read, 1)
            dve.wait_ge(c_read, which + 1)
            step(dve.tensor_scalar(col_w[:, :, :], col_s[:, :, :], -1.0, 1.0, ALU.mult, ALU.add))
            dve.tensor_tensor(col_w[:, :, :], col_w[:, :, :], col_s[:, :, :], ALU.add).then_inc(w_ready, 1)
            assert nrow >= T
            for r in range(nrow):
                dve.wait_ge(b_spread, which * B + r + 1)
                ins_ = dve.tensor_copy(bc[:, r, :], bank(4 + r % 2))
                ins_.then_inc(b_read, 1)
                if r < T:
                    dve.wait_ge(b_read, which * B + 1)
                    rank_tile(dve, step, bc, 0, r, which)
            dve.wait_ge(b_read, which * B + nrow)

        w_ready = sem("w_ready")

        def descent_scalar(act, which):
            def exp(value, wait, **kw):
                act.wait_ge(d_arg.sem, wait)
                act.activation(value, d_e[:, :], ACT.Exp, **kw).then_inc(d_exp.sem, 1)

            def log(wait, i, scale):
                act.wait_ge(d_total.sem, wait)
                act.activation(d_ln[:, :], d_sum[:, i:i + 1], ACT.Ln, scale=scale).then_inc(d_log.sem, 1)

            act.wait_ge(routing_ready, 1)
            exp(d_e[:, :], d_arg.at(which, 1))
            log(d_total.at(which, 1), 0, k_inv[:, which, 0:1])
            with act.Fori(0, ROUNDS) as r:
                exp(d_e[:, :], r + d_arg.at(which, 2), bias=k_exp[:, which:which + 1])
                log(r + d_total.at(which, 2), (ROUND - 1) % 2, k_ln[:, which:which + 1])
            exp(d_e[:, :], d_arg.at(which, ROUNDS + 2))

        def descent_tensor(pe, which, nrow):
            pe.wait_ge(d_exp.sem, d_exp.at(which, ROUNDS + 2))
            for t in range(T):
                ins_ = pe.transpose(bank(3)[:, t * R8:t * R8 + R8], d_e[:, t * P:t * P + P], ident[0:R8, 0:R8])
            ins_.then_inc(c_turned, 1)
            for r in range(nrow):
                if r >= 2:
                    pe.wait_ge(b_read, which * B + r - 1)
                pe.matmul(bank(4 + r % 2), row_of[:, r, :], d_e[:, :], start=True, stop=True).then_inc(b_spread, 1)

        def rank_tile(dve, step, bc, r, t, kind=0):
            score = col_s[:, t, ds(r, 1)]
            step(dve.tensor_scalar(junk[:, :], bc[:, ds(r, 1), :], score, 0.0, ALU.is_gt, ALU.add,
                                   accum_out=over[:, kind, t:t + 1]))
            step(dve.scalar_tensor_tensor(out=junk[:, :], in0=bc[:, ds(r, 1), :], scalar=score, in1=earlier[:, t, :],
                                          op0=ALU.is_equal, op1=ALU.mult, accum_out=ties[:, kind, t:t + 1]))

        def place_tokens(dve, step, place, n, kind=0):
            step(dve.tensor_tensor(over[:, kind, :], over[:, kind, :], ties[:, kind, :], ALU.add))
            for t in range(T):
                step.mark(dve.tensor_scalar(place[:, t, :], slot_no[:, 0:n], over[:, kind, t:t + 1], None, ALU.is_equal))
            step.wait()

        RANK_STEPS = 3 * T + 1
        over, ties = sb("over", [P, 2, T]), sb("ties", [P, 2, T])

        rw = carve({"bc": B * S, "place": T * NQ, "rn": T * D, "w": T, "ws": 1, "xg": NQ, "placeT": T * P, "hl": S,
                    "hh": NF * NQ, "routed": D, "sum": T * D})
        bc0 = rw["bc"].rearrange("p (r q) -> p r q", r=B)
        place0 = rw["place"].rearrange("p (t i) -> p t i", t=T)
        rn0 = rw["rn"].rearrange("p (t d) -> p t d", t=T)
        hh = rw["hh"].rearrange("p (f i) -> p f i", f=NF)
        sum0 = rw["sum"].rearrange("p (t d) -> p t d", t=T)
        r_copied = Signal(sem("r_copied"), 1)
        r_placed = Signal(sem("r_placed"), 1)
        r_gath = Signal(sem("r_gath"), 1, 1)
        r_light = Signal(sem("r_light"), 1)
        r_lgelu = Signal(sem("r_lgelu"), 1)
        r_xg = Signal(sem("r_xg"), 1)
        r_h = Signal(sem("r_h"), 1)
        r_hgelu = Signal(sem("r_hgelu"), 1)
        r_heavy = Signal(sem("r_heavy"), 1)
        r_routed = Signal(sem("r_routed"), 1)
        r_out = Signal(sem("r_out"), 1)

        def route0_pool(pool, step, use, done):
            pool.wait_ge(w_ready, 1)
            pool.wait_ge(turn_done, done)
            with pool.Fori(0, B) as b:
                pool.wait_ge(r_gath.sem, r_gath.at(b, 0))
                pool.tensor_copy(rn0, rn[:, ds(b * T, T), :])
                pool.tensor_copy(rw["w"].unsqueeze(2), col_w[:, :, ds(b, 1)]).then_inc(r_copied.sem, 1)

        def route0_tensor(pe, use, done):
            pe.wait_ge(mats_loaded[2], 16)
            pe.sem_inc(r_gath.sem, r_gath.ahead)
            descent_tensor(pe, 0, B)
            pe.wait_ge(xnT_ready, xnT_count(1))
            pe.wait_ge(b_read, B)

            def output(b):
                pe.wait_ge(r_lgelu.sem, r_lgelu.at(b, 0))
                pe.wait_ge(r_routed.sem, r_routed.at(b, 0))
                pe.wait_ge(turn_done, b + (done - 1))
                for t in range(T):
                    pe.matmul(bank(6)[:, t * P:t * P + P], rw["hl"][0:64, t * P:t * P + P],
                              mat("L0_ffn_w2_l", 0, D, 64), start=True, stop=False)
                    ins_ = pe.matmul(bank(6)[:, t * P:t * P + P], rw["placeT"][:, t * P:t * P + P], rw["routed"],
                                     start=False, stop=True)
                ins_.then_inc(r_out.sem, 1)

            def turn(b, first):
                if not first:
                    output(b)
                pe.matmul(bank(3)[0:64, :], mat("L0_ffn_w1_l", 0, 64), xnT[:, ds(b * S, S)], start=True, stop=True)\
                    .then_inc(r_light.sem, 1)
                pe.wait_ge(r_copied.sem, r_copied.at(b, 1))
                pe.wait_ge(r_placed.sem, r_placed.at(b, 1))
                for t in range(T):
                    pe.matmul(bank(0)[:, 0:NQ], rn0[:, t, :], place0[:, t, :], start=(t == 0), stop=(t == T - 1))
                for t in range(T):
                    pe.matmul(bank(1)[:, 0:1], place0[:, t, :], rw["w"][:, t:t + 1], start=(t == 0), stop=(t == T - 1))
                for t in range(T):
                    ins_ = pe.transpose(bank(2)[:, t * P:t * P + P], place0[:, t, :], ident[:, :])
                ins_.then_inc(r_gath.sem, 1)
                pe.wait_ge(r_xg.sem, r_xg.at(b, 1))
                for f in range(NF):
                    ins_ = pe.matmul(bank(4)[:, f * P:f * P + P], mat("L0_ffn_w1_h", f * P), rw["xg"],
                                     start=True, stop=True)
                ins_.then_inc(r_h.sem, 1)
                pe.wait_ge(r_hgelu.sem, r_hgelu.at(b, 1))
                for f in range(NF):
                    ins_ = pe.matmul(bank(5)[:, 0:D], hh[:, f, :], mat("L0_ffn_w2_h", f * P),
                                     start=(f == 0), stop=(f == NF - 1))
                ins_.then_inc(r_heavy.sem, 1)

            turn(0, True)
            with pe.Fori(1, B) as b:
                turn(b, False)
            output(B)

        def route0_scalar(act, step, use, done):
            descent_scalar(act, 0)
            rms_scalar(act, RMS[0])
            with act.Fori(0, B) as b:
                act.wait_ge(r_light.sem, r_light.at(b, 1))
                act.activation(rw["hl"][0:64, :], bank(3)[0:64, :], ACT.Gelu, bias=col("L0_ffn_b1_l", 0, 64))\
                    .then_inc(r_lgelu.sem, 1)
                act.wait_ge(r_gath.sem, r_gath.at(b, 1))
                act.mul(rw["xg"], bank(0)[:, 0:NQ], col("L0_ffn_gamma_h")).then_inc(r_xg.sem, 1)
                act.copy(rw["placeT"], bank(2))
                act.wait_ge(r_h.sem, r_h.at(b, 1))
                for f in range(NF):
                    ins_ = act.activation(hh[:, f, :], bank(4)[:, f * P:f * P + P], ACT.Gelu,
                                          bias=col("L0_ffn_b1_h", f))
                ins_.then_inc(r_hgelu.sem, 1)

        def route0_vector(dve, step, use, done):
            descent_vector(dve, step, 0, bc0, B)

            def routed(b):
                dve.wait_ge(r_heavy.sem, r_heavy.at(b, 0))
                dve.tensor_copy(rw["ws"], bank(1)[:, 0:1])
                step(dve.tensor_tensor(rw["routed"], bank(5)[:, 0:D], row("L0_ffn_b2_h"), ALU.add))
                dve.tensor_scalar(rw["routed"], rw["routed"], rw["ws"], None, ALU.mult).then_inc(r_routed.sem, 1)

            def add_up(b):
                dve.wait_ge(r_out.sem, r_out.at(b, 0))
                step(dve.tensor_tensor(sum0, bank(6).rearrange("p (t d) -> p t d", t=T),
                                       row("L0_ffn_b2_l").unsqueeze(1).to_broadcast([P, T, D]), ALU.add))
                xb = x[:, ds(b * T - T, T), :]
                dve.scalar_tensor_tensor(out=xb, in0=sum0, scalar=tg[:, 4:5], in1=xb, op0=ALU.mult, op1=ALU.add)\
                    .then_inc(turn_done, 1)

            def turn(b, first):
                for t in range(T):
                    if not first:
                        rank_tile(dve, step, bc0, b, t)
                    if t == T - 2 and not first:
                        routed(b)
                if not first:
                    dve.wait_ge(r_gath.sem, r_gath.at(b, 0))
                place_tokens(dve, step, place0, NQ)
                dve.sem_inc(r_placed.sem, 1)
                if not first:
                    add_up(b)

            turn(0, True)
            with step.loop(B - 1, RANK_STEPS + 2, 1) as b:
                turn(b, False)
            routed(B)
            add_up(B)

        aw = carve({"qT": NBLK * S, "kT": NBLK * NKEY, "v": 5 * H * DH, "ctx": KC, "pr": 2 * NKEY, "pT": 2 * 5 * P,
                    "nm": 4, "sums": T * H, "rec": 4, "o": T * H * DH, "sum": T * D})
        qT_a = aw["qT"].rearrange("p (i q) -> p i q", i=NBLK)
        kT_a = aw["kT"].rearrange("p (i k) -> p i k", i=NBLK)
        v_a = aw["v"].rearrange("p (c n) -> p c n", c=5)
        pr_a = aw["pr"].rearrange("p (n k) -> p n k", n=2)
        pT_a = aw["pT"].rearrange("p (n k) -> p n k", n=2)
        o_a = aw["o"].rearrange("p (t n) -> p t n", t=T)
        oT_a = qT_a
        sum_a = aw["sum"].rearrange("p (t d) -> p t d", t=T)
        ITEMS = [("q", i) for i in range(NBLK)] + [("k", i) for i in range(NBLK)] + [("km", 0), ("km", 1)] + \
                [("v", i) for i in range(2 * T)] + [("vm", 0), ("vm", 1)]
        HALF_ITEMS = len(ITEMS) // 2
        NV = next(n for n, (kind, _) in enumerate(ITEMS) if kind == "v")
        UA = T * H
        GA = UA // 4
        a_in = Signal(sem("a_in"), 1)
        a_proj = Signal(sem("a_proj"), len(ITEMS), 1)
        a_even = Signal(sem("a_even"), HALF_ITEMS)
        a_odd = Signal(sem("a_odd"), HALF_ITEMS)
        a_scores = Signal(sem("a_scores"), UA)
        a_max = Signal(sem("a_max"), UA)
        a_probs = Signal(sem("a_probs"), UA)
        a_turned = Signal(sem("a_turned"), UA)
        a_pT, a_pTm = Signal(sem("a_pT"), UA), Signal(sem("a_pTm"), UA)
        a_av = Signal(sem("a_av"), UA)
        a_o = Signal(sem("a_o"), GA)
        a_oturn = Signal(sem("a_oturn"), NBLK)
        a_oe = Signal(sem("a_oe"), NBLK // 2)
        a_oo = Signal(sem("a_oo"), NBLK // 2)
        a_out = Signal(sem("a_out"), 1)
        key_rows = [P] * T + [KC]

        def self_pool(pool, step, use, done):
            pool.wait_ge(turn_done, done)
            with pool.Fori(0, B) as b:
                pool.wait_ge(xnT_ready, b + xnT_count(TWICE) - B + 1)
                pool.wait_ge(a_proj.sem, a_proj.at(b, 0))
                pool.tensor_copy(x_in[:, :], xnT[:, ds(b * S, S)])
                pool.tensor_copy(aw["ctx"].unsqueeze(1), ctxT[:, ds(b, 1), :]).then_inc(a_in.sem, 1)

        def item_place(kind, i, n):
            to = bank((n + 2) % 8 if n < NV else 4 + (n - NV) % 4)
            if kind == "q":
                return to, qT_a[:, i, :]
            if kind == "k":
                return to, kT_a[:, i, 0:S]
            if kind == "km":
                return to[:, 0:4 * KC].rearrange("p (j k) -> p j k", j=4), kT_a[:, 4 * i:4 * i + 4, S:NKEY]
            if kind == "v":
                return to, v_a[:, i // 2, (i % 2) * S:(i % 2) * S + S]
            return to[0:KC, :], v_a[0:KC, T, i * S:i * S + S]

        def self_tensor(pe, use, done):
            pe.wait_ge(mats_loaded[3], 16)
            pe.sem_inc(a_proj.sem, a_proj.ahead)

            def item(g, n):
                kind, i = ITEMS[n]
                to, _ = item_place(kind, i, n)
                if n == 6:
                    pe.wait_ge(xnT_ready, xnT_count(TWICE))
                    pe.wait_ge(turn_done, g + done)
                if n >= 8:
                    s = (a_even, a_odd)[n % 2]
                    pe.wait_ge(s.sem, s.at(g, (n - (8 if n < NV + 4 else 4)) // 2 + 1))
                if kind in "qk":
                    ins_ = pe.matmul(to, mat("L1_xattn_W" + kind, i * P), x_in[:, :], start=True, stop=True)
                elif kind == "km":
                    for j in range(4):
                        ins_ = pe.matmul(to[:, j, :], mat("L1_xattn_Wm", (4 * i + j) * P), aw["ctx"],
                                         start=True, stop=True)
                elif kind == "v":
                    ins_ = pe.matmul(to, x_in[:, (i // 2) * P:(i // 2) * P + P], mat("L1_xattn_Wv", (i % 2) * S, S),
                                     start=True, stop=True)
                else:
                    ins_ = pe.matmul(to, aw["ctx"], mat("L1_xattn_Wm", i * S, S), start=True, stop=True)
                ins_.then_inc(a_proj.sem, 1)

            def scores(g, u):
                t, h = divmod(u, H)
                if u >= 2:
                    pe.wait_ge(a_probs.sem, a_probs.at(g, u - 1))
                at = slice(DH * (h % 2), DH * (h % 2) + DH)
                q = qT_a[at, h // 2, t * P:t * P + P]
                pe.matmul(bank(2 * (u % 2)), q, kT_a[at, h // 2, 0:S], start=True, stop=True)
                pe.matmul(bank(2 * (u % 2) + 1)[:, 0:KC], q, kT_a[at, h // 2, S:NKEY], start=True, stop=True)\
                    .then_inc(a_scores.sem, 1)

            def turn_probs(g, u):
                pe.wait_ge(a_probs.sem, a_probs.at(g, u + 1))
                if u >= 1:
                    pe.wait_ge(a_pT.sem, a_pT.at(g, u))
                    pe.wait_ge(a_pTm.sem, a_pTm.at(g, u))
                for c, n in enumerate(key_rows):
                    to = bank(4)[:, c * P:c * P + P] if c < T else bank(5)[0:n, 0:P]
                    ins_ = pe.transpose(to, pr_a[:, u % 2, c * P:c * P + n], ident[:, :])
                ins_.then_inc(a_turned.sem, 1)

            def av(g, u):
                h, group = u % H, u // 4
                pe.wait_ge(a_pT.sem, a_pT.at(g, u + 1))
                if u % 4 == 0 and group >= 2:
                    pe.wait_ge(a_o.sem, a_o.at(g, group - 1))
                for c, n in enumerate(key_rows):
                    if c == T:
                        pe.wait_ge(a_pTm.sem, a_pTm.at(g, u + 1))
                    ins_ = pe.matmul(bank(6 + group % 2)[:, (u % 4) * DH:(u % 4) * DH + DH],
                                     pT_a[0:n, u % 2, c * P:c * P + P], v_a[0:n, c, h * DH:h * DH + DH],
                                     start=(c == 0), stop=(c == T))
                ins_.then_inc(a_av.sem, 1)

            with pe.Fori(0, B) as b:
                pe.wait_ge(a_in.sem, a_in.at(b, 1))
                for n in range(NV):
                    item(b, n)
                pe.wait_ge(a_even.sem, a_even.at(b, NV // 2))
                pe.wait_ge(a_odd.sem, a_odd.at(b, NV // 2))
                scores(b, 0)
                scores(b, 1)
                for n in range(NV, len(ITEMS)):
                    item(b, n)
                pe.wait_ge(a_even.sem, a_even.at(b, HALF_ITEMS))
                pe.wait_ge(a_odd.sem, a_odd.at(b, HALF_ITEMS))
                turn_probs(b, 0)
                for u in range(2, UA + 2):
                    if u < UA:
                        scores(b, u)
                    if u >= 2:
                        av(b, u - 2)
                    if 1 <= u <= UA:
                        turn_probs(b, u - 1)
                pe.wait_ge(a_o.sem, a_o.at(b, GA))
                for i in range(NBLK):
                    for t in range(T):
                        ins_ = pe.transpose(bank(i)[:, t * P:t * P + P], o_a[:, t, i * P:i * P + P], ident[:, :])
                    ins_.then_inc(a_oturn.sem, 1)
                pe.wait_ge(a_oe.sem, a_oe.at(b, NBLK // 2))
                pe.wait_ge(a_oo.sem, a_oo.at(b, NBLK // 2))
                for t in range(T):
                    for i in range(NBLK):
                        ins_ = pe.matmul(bank(0)[:, t * P:t * P + P], oT_a[:, i, t * P:t * P + P],
                                         mat("L1_xattn_Wo", i * P), start=(i == 0), stop=(i == NBLK - 1))
                ins_.then_inc(a_out.sem, 1)

        def self_scalar(act, step, use, done):
            def evacuate(b, n):
                src, dst = item_place(*ITEMS[n], n)
                act.wait_ge(a_proj.sem, a_proj.at(b, n + 1))
                (act.mul(dst, src, DH ** -0.5) if ITEMS[n][0] == "q" else act.copy(dst, src)).then_inc(a_even.sem, 1)

            def copy_pTm(b, u):
                act.wait_ge(a_turned.sem, a_turned.at(b, u + 1))
                if u >= 2:
                    act.wait_ge(a_av.sem, a_av.at(b, u - 1))
                act.copy(pT_a[0:KC, u % 2, T * P:T * P + P], bank(5)[0:KC, 0:P]).then_inc(a_pTm.sem, 1)

            with act.Fori(0, B) as b:
                for n in range(0, NV, 2):
                    evacuate(b, n)
                for u in range(UA):
                    if u == 2:
                        for n in range(NV, len(ITEMS), 2):
                            evacuate(b, n)
                    if u >= 2:
                        copy_pTm(b, u - 2)
                    act.wait_ge(a_max.sem, a_max.at(b, u + 1))
                    if u >= 2:
                        act.wait_ge(a_turned.sem, a_turned.at(b, u - 1))
                    act.activation(pr_a[:, u % 2], bank(2 * (u % 2), 2)[:, 0:NKEY], ACT.Exp,
                                   bias=aw["nm"][:, u % 4:u % 4 + 1], accum_out=aw["sums"][:, u:u + 1])\
                        .then_inc(a_probs.sem, 1)
                copy_pTm(b, UA - 2)
                copy_pTm(b, UA - 1)
                for i in range(0, NBLK, 2):
                    act.wait_ge(a_oturn.sem, a_oturn.at(b, i + 1))
                    act.copy(oT_a[:, i, :], bank(i)).then_inc(a_oe.sem, 1)

        def self_vector(dve, step, use, done):
            def max_of(g, u):
                dve.wait_ge(a_scores.sem, a_scores.at(g, u + 1))
                dve.tensor_reduce(aw["nm"][:, u % 4:u % 4 + 1], bank(2 * (u % 2), 2)[:, 0:NKEY], X, ALU.max,
                                  negate=True).then_inc(a_max.sem, 1)

            def copy_pT(g, u):
                dve.wait_ge(a_turned.sem, a_turned.at(g, u + 1))
                if u >= 2:
                    dve.wait_ge(a_av.sem, a_av.at(g, u - 1))
                dve.tensor_copy(pT_a[:, u % 2, 0:T * P], bank(4)).then_inc(a_pT.sem, 1)

            def norm_o(g, i):
                t, j = divmod(i, 4)
                dve.wait_ge(a_av.sem, a_av.at(g, 4 * i + 4))
                step(dve.reciprocal(aw["rec"], aw["sums"][:, 4 * i:4 * i + 4]))
                dve.tensor_tensor(o_a[:, t, j * 4 * DH:(j + 1) * 4 * DH].rearrange("p (h e) -> p h e", h=4),
                                  bank(6 + i % 2)[:, 0:4 * DH].rearrange("p (h e) -> p h e", h=4),
                                  aw["rec"].unsqueeze(2).to_broadcast([P, 4, DH]), ALU.mult).then_inc(a_o.sem, 1)

            def evacuate(b, n):
                src, dst = item_place(*ITEMS[n], n)
                dve.wait_ge(a_proj.sem, a_proj.at(b, n + 1))
                if ITEMS[n][0] == "q":
                    dve.tensor_scalar(dst, src, DH ** -0.5, None, ALU.mult).then_inc(a_odd.sem, 1)
                else:
                    dve.tensor_copy(dst, src).then_inc(a_odd.sem, 1)

            with step.loop(B, GA + 1) as b:
                for n in range(1, NV, 2):
                    evacuate(b, n)
                max_of(b, 0)
                max_of(b, 1)
                for n in range(NV + 1, len(ITEMS), 2):
                    evacuate(b, n)
                copy_pT(b, 0)
                for u in range(2, UA + 3):
                    if u < UA:
                        max_of(b, u)
                    if 1 <= u <= UA:
                        copy_pT(b, u - 1)
                    if u >= 6 and (u - 6) % 4 == 0:
                        norm_o(b, (u - 6) // 4)
                for i in range(1, NBLK, 2):
                    dve.wait_ge(a_oturn.sem, a_oturn.at(b, i + 1))
                    dve.tensor_copy(oT_a[:, i, :], bank(i)).then_inc(a_oo.sem, 1)
                dve.wait_ge(turn_done, b + done)
                dve.wait_ge(a_out.sem, a_out.at(b, 1))
                step(dve.tensor_tensor(sum_a, bank(0).rearrange("p (t d) -> p t d", t=T),
                                       row("L1_xattn_bo").unsqueeze(1).to_broadcast([P, T, D]), ALU.add))
                xb = x[:, ds(b * T, T), :]
                dve.scalar_tensor_tensor(out=xb, in0=sum_a, scalar=tg[:, 1:2], in1=xb, op0=ALU.mult, op1=ALU.add)\
                    .then_inc(turn_done, 1)
        NKC = NKV // P
        lw = carve({"bc": R8 * S, "placeq": T * NQ, "placek": T * NKV, "rn": T * D, "w": T * 2, "ws": 1 + NKC,
                    "qT": NBF * S, "kT": NBF * S, "v": T * HF * DH, "pr": 4 * 4 * P, "pT": 2 * 4 * P, "nm": 4 * 4,
                    "sums": 4 * 4, "rec": 2 * 4, "o": T * HF * DH, "placeT": T * P, "xq": NQ, "xk": NKV,
                    "kh": NBF * NKV, "qh": NBF * NQ, "vh": NKC * HF * DH, "routed": D})
        bc1 = lw["bc"].rearrange("p (r q) -> p r q", r=R8)
        placeq = lw["placeq"].rearrange("p (t i) -> p t i", t=T)
        placek = lw["placek"].rearrange("p (t i) -> p t i", t=T)
        rn1 = lw["rn"].rearrange("p (t d) -> p t d", t=T)
        w1 = lw["w"].rearrange("p (k t) -> p t k", k=2)
        qT_l = lw["qT"].rearrange("p (i q) -> p i q", i=NBF)
        kT_l = lw["kT"].rearrange("p (i q) -> p i q", i=NBF)
        v_l = lw["v"].rearrange("p (t n) -> p t n", t=T)
        pr_l = lw["pr"].rearrange("p (n k) -> p n k", n=4)
        pT_l = lw["pT"].rearrange("p (n k) -> p n k", n=2)
        nm_l = lw["nm"].rearrange("p (n k) -> p n k", n=4)
        sums_l = lw["sums"].rearrange("p (n k) -> p n k", n=4)
        rec_l = lw["rec"].rearrange("p (n k) -> p n k", n=2)
        o_l = lw["o"].rearrange("p (t n) -> p t n", t=T)
        oT_l = qT_l
        kh = lw["kh"].rearrange("p (i k) -> p i k", i=NBF)
        qh = lw["qh"].rearrange("p (i q) -> p i q", i=NBF)
        vh = lw["vh"].rearrange("p (c n) -> p c n", c=NKC)
        oh, ohT = lw["placek"][:, 0:HF * DH], lw["placeq"]
        LITEMS = [("q", i) for i in range(NBF)] + [("k", i) for i in range(NBF)] + [("v", i) for i in range(T)]
        ITEM_BANK = [0, 1, 3, 4, 5, 6, 7, 2]
        HL = len(LITEMS) // 2
        NVL = 2 * NBF

        def item_bank(n):
            return bank(ITEM_BANK[n if n < NVL else n - 6])

        UL, UH = 2 * T, 4
        UT = UL + UH
        l_x = Signal(sem("l_x"), 1)
        l_rn = Signal(sem("l_rn"), 1)
        l_proj = Signal(sem("l_proj"), len(LITEMS), 1)
        l_even, l_odd = Signal(sem("l_even"), HL), Signal(sem("l_odd"), HL)
        l_placed = Signal(sem("l_placed"), 1)
        l_gath = Signal(sem("l_gath"), 1, 1)
        l_gx, l_gturn = Signal(sem("l_gx"), 1), Signal(sem("l_gturn"), 1)
        l_hproj = Signal(sem("l_hproj"), 5)
        l_ha, l_hd = Signal(sem("l_ha"), 2), Signal(sem("l_hd"), 3)
        l_scores, l_max = Signal(sem("l_scores"), UT), Signal(sem("l_max"), UT)
        l_probs, l_turned = Signal(sem("l_probs"), UT, 4), Signal(sem("l_turned"), UT, 4)
        l_pT = Signal(sem("l_pT"), UT, 4)
        l_av, l_o = Signal(sem("l_av"), UT, 4), Signal(sem("l_o"), UT, 4)
        l_oturn, l_oT = Signal(sem("l_oturn"), NBF + 1), Signal(sem("l_oT"), NBF + 1)
        l_light = Signal(sem("l_light"), 1)
        l_added = Signal(sem("l_added"), 1, 1)
        l_heavy, l_routed = Signal(sem("l_heavy"), 1), Signal(sem("l_routed"), 1)
        l_out = Signal(sem("l_out"), 1)

        def blocks_of(u):
            if u < UL:
                return [(2 * i + u % 2, 0) for i in range(4)], u // 2
            j = u - UL
            return [(4 * (j // 2) + 2 * i + j % 2, c) for i in range(2) for c in range(NKC)], None

        def route1_pool(pool, step, use, done):
            pool.wait_ge(w_ready, 2)
            pool.wait_ge(xnT_ready, xnT_count(3))
            with pool.Fori(0, B) as b:
                pool.wait_ge(l_proj.sem, l_proj.at(b, 0))
                pool.tensor_copy(x_in[:, :], xnT[:, ds(b * S, S)]).then_inc(l_x.sem, 1)
                pool.wait_ge(l_gath.sem, l_gath.at(b, 0))
                pool.tensor_copy(rn1, rn[:, ds(b * T, T), :])
                for kind in range(2):
                    ins_ = pool.tensor_copy(w1[:, :, kind:kind + 1], col_w[:, :, ds(b + kind * B, 1)])
                ins_.then_inc(l_rn.sem, 1)

        def route1_tensor(pe, use, done):
            pe.wait_ge(mats_loaded[4], 16)
            for s in (l_proj, l_gath, l_turned, l_av):
                pe.sem_inc(s.sem, s.ahead)
            descent_tensor(pe, 1, R8)
            pe.wait_ge(b_read, B + R8)

            def items(b, first, past):
                for n in range(first, past):
                    kind, i = LITEMS[n]
                    if n == 6:
                        pe.wait_ge(l_added.sem, l_added.at(b, 0))
                    if n == 7:
                        pe.wait_ge(turn_done, b + done)
                    if n >= NVL:
                        s = (l_even, l_odd)[n % 2]
                        pe.wait_ge(s.sem, s.at(b, (n - 6) // 2 + 1))
                    to = item_bank(n)
                    if kind == "v":
                        ins_ = pe.matmul(to, x_in[:, i * P:i * P + P], mat("L1_ffn_wv_light", 0, HF * DH),
                                         start=True, stop=True)
                    else:
                        ins_ = pe.matmul(to, mat(f"L1_ffn_w{kind}_light", i * P), x_in[:, :], start=True, stop=True)
                    ins_.then_inc(l_proj.sem, 1)

            def scores(b, u):
                pe.wait_ge(l_probs.sem, l_probs.at(b, u - 1))
                if u == UL:
                    pe.wait_ge(l_ha.sem, l_ha.at(b, 2))
                    pe.wait_ge(l_hd.sem, l_hd.at(b, 1))
                blocks, w = blocks_of(u)
                for i in range(4 if u < UL else 2):
                    h = blocks[i * (1 if u < UL else NKC)][0]
                    at = slice(DH * (h % 2), DH * (h % 2) + DH)
                    if u < UL:
                        q, k, n = qT_l[at, h // 2, w * P:w * P + P], kT_l[at, h // 2, w * P:w * P + P], P
                    else:
                        q, k, n = qh[at, h // 2, :], kh[at, h // 2, :], NKV
                    ins_ = pe.matmul(bank(u % 2)[:, i * n:i * n + n], q, k, start=True, stop=True)
                ins_.then_inc(l_scores.sem, 1)

            def turn_probs(b, u):
                pe.wait_ge(l_probs.sem, l_probs.at(b, u + 1))
                pe.wait_ge(l_pT.sem, l_pT.at(b, u - 1))
                for i in range(4):
                    ins_ = pe.transpose(bank(4 + u % 2)[:, i * P:i * P + P], pr_l[:, u % 4, i * P:i * P + P], ident[:, :])
                ins_.then_inc(l_turned.sem, 1)

            def av(b, u):
                pe.wait_ge(l_pT.sem, l_pT.at(b, u + 1))
                pe.wait_ge(l_o.sem, l_o.at(b, u))
                if u == UL:
                    pe.wait_ge(l_hd.sem, l_hd.at(b, 3))
                blocks, w = blocks_of(u)
                for i, (h, c) in enumerate(blocks):
                    v = v_l[:, w, h * DH:h * DH + DH] if u < UL else vh[:, c, h * DH:h * DH + DH]
                    j = i if u < UL else i // NKC
                    ins_ = pe.matmul(bank(6)[:, j * DH:j * DH + DH], pT_l[:, u % 2, i * P:i * P + P], v,
                                     start=(u < UL or c == 0), stop=(u < UL or c == NKC - 1))
                ins_.then_inc(l_av.sem, 1)

            def gather(b):
                pe.wait_ge(l_placed.sem, l_placed.at(b, 1))
                pe.wait_ge(l_rn.sem, l_rn.at(b, 1))
                for t in range(T):
                    pe.matmul(bank(2)[:, 0:NQ], rn1[:, t, :], placeq[:, t, :], start=(t == 0), stop=(t == T - 1))
                for t in range(T):
                    pe.matmul(bank(2)[:, NQ:NQ + NKV], rn1[:, t, :], placek[:, t, :], start=(t == 0), stop=(t == T - 1))
                for j in range(1 + NKC):
                    for t in range(T):
                        place = placeq[:, t, :] if j == 0 else placek[:, t, (j - 1) * P:j * P]
                        pe.matmul(bank(2)[:, NQ + NKV + j:NQ + NKV + j + 1], place,
                                  w1[:, t, 0:1] if j == 0 else w1[:, t, 1:2], start=(t == 0), stop=(t == T - 1))
                for t in range(T):
                    ins_ = pe.transpose(bank(3)[:, t * P:t * P + P], placeq[:, t, :], ident[:, :])
                ins_.then_inc(l_gath.sem, 1)

            def routed_keys(b, pair):
                for j in range(2):
                    ins_ = pe.matmul(bank(2 + pair)[:, j * NKV:j * NKV + NKV],
                                     mat("L1_ffn_wk_heavy", (2 * pair + j) * P), lw["xk"], start=True, stop=True)
                ins_.then_inc(l_hproj.sem, 1)

            def routed_values(b, c, to):
                pe.matmul(to, lw["xk"][:, c * P:c * P + P], mat("L1_ffn_wv_heavy", 0, HF * DH), start=True, stop=True)\
                    .then_inc(l_hproj.sem, 1)

            def projections(b, u):
                if u == 6:
                    pe.wait_ge(l_gx.sem, l_gx.at(b, 1))
                    for i in range(NBF):
                        ins_ = pe.matmul(bank(7)[:, i * NQ:i * NQ + NQ], mat("L1_ffn_wq_heavy", i * P), lw["xq"],
                                         start=True, stop=True)
                    ins_.then_inc(l_hproj.sem, 1)
                    routed_keys(b, 0)
                if u == 7:
                    pe.wait_ge(l_ha.sem, l_ha.at(b, 1))
                    routed_values(b, 0, bank(7))
                if u == 8:
                    pe.wait_ge(l_ha.sem, l_ha.at(b, 2))
                    routed_values(b, 1, bank(2))

            def turn_block(b, i):
                if i == 0:
                    pe.wait_ge(l_o.sem, l_o.at(b, UL))
                    pe.wait_ge(l_hd.sem, l_hd.at(b, 3))
                if i >= 2:
                    pe.wait_ge(l_oT.sem, l_oT.at(b, i - 1))
                for t in range(T):
                    ins_ = pe.transpose(bank(2 + i % 2)[:, t * P:t * P + P], o_l[:, t, i * P:i * P + P], ident[:, :])
                ins_.then_inc(l_oturn.sem, 1)

            with pe.Fori(0, B) as b:
                pe.wait_ge(l_x.sem, l_x.at(b, 1))
                items(b, 0, NVL + 2)
                pe.wait_ge(l_even.sem, l_even.at(b, NVL // 2))
                pe.wait_ge(l_odd.sem, l_odd.at(b, NVL // 2))
                for u in range(UT + 3):
                    if u == 2:
                        items(b, NVL + 2, len(LITEMS))
                        pe.wait_ge(l_odd.sem, l_odd.at(b, HL - 1))
                    if u == 3:
                        pe.wait_ge(l_even.sem, l_even.at(b, HL))
                        pe.wait_ge(l_odd.sem, l_odd.at(b, HL))
                    if u == 7:
                        pe.wait_ge(l_gturn.sem, l_gturn.at(b, 1))
                        routed_keys(b, 1)
                    if u < UT:
                        scores(b, u)
                    if u >= 3:
                        av(b, u - 3)
                    if 2 <= u < UT + 2:
                        turn_probs(b, u - 2)
                    if u == 5:
                        gather(b)
                    projections(b, u)
                    if 10 <= u < 10 + NBF:
                        turn_block(b, u - 10)
                pe.wait_ge(l_oT.sem, l_oT.at(b, NBF))
                for t in range(T):
                    if t == 1:
                        pe.wait_ge(l_o.sem, l_o.at(b, UT))
                        for i in range(NBF):
                            ins_ = pe.transpose(bank(4)[:, i * P:i * P + P], oh[:, i * P:i * P + P], ident[:, :])
                        ins_.then_inc(l_oturn.sem, 1)
                    for i in range(NBF):
                        ins_ = pe.matmul(bank(7)[:, t * P:t * P + P], oT_l[:, i, t * P:t * P + P],
                                         mat("L1_ffn_wo_light", i * P), start=(i == 0), stop=(i == NBF - 1))
                ins_.then_inc(l_light.sem, 1)
                pe.wait_ge(l_oT.sem, l_oT.at(b, NBF + 1))
                for i in range(NBF):
                    ins_ = pe.matmul(bank(5)[:, 0:D], ohT[:, i * P:i * P + P], mat("L1_ffn_wo_heavy", i * P),
                                     start=(i == 0), stop=(i == NBF - 1))
                ins_.then_inc(l_heavy.sem, 1)
                pe.wait_ge(l_routed.sem, l_routed.at(b, 1))
                for t in range(T):
                    ins_ = pe.matmul(bank(2)[:, t * P:t * P + P], lw["placeT"][:, t * P:t * P + P], lw["routed"],
                                     start=True, stop=True)
                ins_.then_inc(l_out.sem, 1)

        def route1_scalar(act, step, use, done):
            for s in (l_probs, l_pT):
                act.sem_inc(s.sem, s.ahead)
            descent_scalar(act, 1)
            rms_scalar(act, RMS[1])

            def probs(b, u):
                act.wait_ge(l_max.sem, l_max.at(b, u + 1))
                act.wait_ge(l_turned.sem, l_turned.at(b, u - 3))
                act.wait_ge(l_o.sem, l_o.at(b, u - 3))
                n = P if u < UL else NKV
                for i in range(4 * P // n):
                    ins_ = act.activation(pr_l[:, u % 4, i * n:i * n + n], bank(u % 2)[:, i * n:i * n + n], ACT.Exp,
                                          bias=nm_l[:, u % 4, i:i + 1], accum_out=sums_l[:, u % 4, i:i + 1])
                ins_.then_inc(l_probs.sem, 1)

            def copy_pT(b, u):
                act.wait_ge(l_turned.sem, l_turned.at(b, u + 1))
                act.wait_ge(l_av.sem, l_av.at(b, u - 1))
                act.copy(pT_l[:, u % 2, :], bank(4 + u % 2)).then_inc(l_pT.sem, 1)

            def evacuate(b, first, past):
                for n in range(first, past, 2):
                    kind, i = LITEMS[n]
                    act.wait_ge(l_proj.sem, l_proj.at(b, n + 1))
                    dst = {"q": qT_l, "k": kT_l, "v": v_l}[kind][:, i, :]
                    (act.mul(dst, item_bank(n), DH ** -0.5) if kind == "q" else act.copy(dst, item_bank(n)))\
                        .then_inc(l_even.sem, 1)

            with act.Fori(0, B) as b:
                evacuate(b, 0, NVL + 2)
                for u in range(UT + 2):
                    if u == 2:
                        evacuate(b, NVL + 2, len(LITEMS))
                    if u >= 2:
                        copy_pT(b, u - 2)
                    if u < UT:
                        probs(b, u)
                    if 11 <= u < 11 + NBF:
                        act.wait_ge(l_oturn.sem, l_oturn.at(b, u - 10))
                        act.copy(oT_l[:, u - 11, :], bank(2 + (u - 11) % 2)).then_inc(l_oT.sem, 1)
                    if u == 5:
                        act.wait_ge(l_gath.sem, l_gath.at(b, 1))
                        act.mul(lw["xq"], bank(2)[:, 0:NQ], col("L1_ffn_gamma_heavy"))
                        act.mul(lw["xk"], bank(2)[:, NQ:NQ + NKV], col("L1_ffn_gamma_heavy"))
                        act.copy(lw["ws"], bank(2)[:, NQ + NKV:NQ + NKV + 1 + NKC]).then_inc(l_gx.sem, 1)
                    if u == 6:
                        act.wait_ge(l_hproj.sem, l_hproj.at(b, 1))
                        act.mul(lw["qh"], bank(7), DH ** -0.5).then_inc(l_ha.sem, 1)
                        act.wait_ge(l_hproj.sem, l_hproj.at(b, 2))
                        act.copy(lw["kh"][:, 0:S], bank(2)).then_inc(l_ha.sem, 1)
                act.wait_ge(l_oturn.sem, l_oturn.at(b, NBF))
                act.copy(oT_l[:, NBF - 1, :], bank(3)).then_inc(l_oT.sem, 1)
                act.wait_ge(l_oturn.sem, l_oturn.at(b, NBF + 1))
                act.copy(ohT, bank(4)).then_inc(l_oT.sem, 1)

        def route1_vector(dve, step, use, done):
            dve.sem_inc(l_o.sem, l_o.ahead)
            dve.sem_inc(l_added.sem, l_added.ahead)
            descent_vector(dve, step, 1, bc1, R8)

            def max_of(b, u):
                dve.wait_ge(l_scores.sem, l_scores.at(b, u + 1))
                dve.wait_ge(l_probs.sem, l_probs.at(b, u - 3))
                n = 4 if u < UL else 2
                dve.tensor_reduce(nm_l[:, u % 4, 0:n], bank(u % 2).rearrange("p (i k) -> p i k", i=n), X, ALU.max,
                                  negate=True).then_inc(l_max.sem, 1)

            def norm_o(b, u):
                dve.wait_ge(l_av.sem, l_av.at(b, u + 1))
                blocks, w = blocks_of(u)
                n = 4 if u < UL else 2
                step(dve.reciprocal(rec_l[:, u % 2, 0:n], sums_l[:, u % 4, 0:n]))
                if u < UL:
                    dst = o_l[:, w, :].rearrange("p (i r e) -> p i r e", r=2, e=DH)[:, :, u % 2, :]
                else:
                    j = u - UL
                    four = oh[:, (j // 2) * 4 * DH:(j // 2 + 1) * 4 * DH]
                    dst = four.rearrange("p (i r e) -> p i r e", r=2, e=DH)[:, :, j % 2, :]
                dve.tensor_tensor(dst, bank(6)[:, 0:n * DH].rearrange("p (i e) -> p i e", i=n),
                                  rec_l[:, u % 2, 0:n].unsqueeze(2).to_broadcast([P, n, DH]), ALU.mult)\
                    .then_inc(l_o.sem, 1)

            def evacuate(b, n):
                kind, i = LITEMS[n]
                dve.wait_ge(l_proj.sem, l_proj.at(b, n + 1))
                dst, src = {"q": qT_l, "k": kT_l, "v": v_l}[kind][:, i, :], item_bank(n)
                (dve.tensor_scalar(dst, src, DH ** -0.5, None, ALU.mult) if kind == "q"
                 else dve.tensor_copy(dst, src)).then_inc(l_odd.sem, 1)

            with step.loop(B, 2 * RANK_STEPS + UT) as b:
                for n in range(1, NVL + 2, 2):
                    evacuate(b, n)
                    if n == 1:
                        place_tokens(dve, step, placeq, NQ, 1)
                    if n in (3, 5):
                        rank_tile(dve, step, bc1, b + B, n // 2 - 1)
                for u in range(UT + 3):
                    if u < UT:
                        max_of(b, u)
                    if u == 1:
                        evacuate(b, len(LITEMS) - 1)
                        rank_tile(dve, step, bc1, b + B, 2)
                    if u >= 3:
                        norm_o(b, u - 3)
                    if u == 6:
                        dve.wait_ge(l_gath.sem, l_gath.at(b, 1))
                        dve.tensor_copy(lw["placeT"], bank(3)).then_inc(l_gturn.sem, 1)
                    if u == 7:
                        dve.wait_ge(l_hproj.sem, l_hproj.at(b, 3))
                        dve.tensor_copy(lw["kh"][:, S:2 * S], bank(3)).then_inc(l_hd.sem, 1)
                        dve.wait_ge(l_hproj.sem, l_hproj.at(b, 4))
                        dve.wait_ge(l_gx.sem, l_gx.at(b, 1))
                        dve.tensor_scalar(vh[:, 0, :], bank(7), lw["ws"][:, 1:2], None, ALU.mult).then_inc(l_hd.sem, 1)
                    if u == 8:
                        dve.wait_ge(l_hproj.sem, l_hproj.at(b, 5))
                        dve.tensor_scalar(vh[:, 1, :], bank(2), lw["ws"][:, 2:3], None, ALU.mult).then_inc(l_hd.sem, 1)
                    if u == 3:
                        rank_tile(dve, step, bc1, b + B, 3)
                    if u == T:
                        place_tokens(dve, step, placek, NKV)
                        dve.sem_inc(l_placed.sem, 1)
                    if u >= UT - 3 and u < UT - 3 + T:
                        rank_tile(dve, step, bc1, b + 1, u - (UT - 3), 1)
                xb = x[:, ds(b * T, T), :]
                gate = tg[:, 5:6]
                dve.wait_ge(l_light.sem, l_light.at(b, 1))
                dve.scalar_tensor_tensor(out=xb, in0=bank(7).rearrange("p (t d) -> p t d", t=T), scalar=gate, in1=xb,
                                         op0=ALU.mult, op1=ALU.add).then_inc(l_added.sem, 1)
                dve.wait_ge(l_heavy.sem, l_heavy.at(b, 1))
                dve.tensor_scalar(lw["routed"], bank(5)[:, 0:D], lw["ws"][:, 0:1], None, ALU.mult)\
                    .then_inc(l_routed.sem, 1)
                dve.wait_ge(l_out.sem, l_out.at(b, 1))
                dve.wait_ge(l_added.sem, l_added.at(b, 1))
                dve.scalar_tensor_tensor(out=xb, in0=bank(2).rearrange("p (t d) -> p t d", t=T), scalar=gate, in1=xb,
                                         op0=ALU.mult, op1=ALU.add).then_inc(turn_done, 1)

        W2, W3 = 3 * FF, 2 * FF + NF
        mw = carve({"w": 2 * W2, "h": 2 * NF * S, "sg": 2 * S, "acc": NT * D, "y": 2 * T * D, "lg": NT * 16, "pr": NT * 16,
                    "mx": NT * 2, "sm": NT * 2, "cw": NT * E, "top": NT * E, "idx": NT * E, "idxf": NT * E,
                    "hot": NT * E})
        wts = mw["w"].rearrange("p (n k) -> p n k", n=2)
        h_m = mw["h"].rearrange("p (n f q) -> p n f q", n=2, f=NF)
        sg = mw["sg"].rearrange("p (n q) -> p n q", n=2)
        acc = mw["acc"].rearrange("p (n d) -> p n d", n=NT)
        y_m = mw["y"].rearrange("p (n t d) -> p n t d", n=2, t=T)
        cw = mw["cw"].rearrange("p (n e) -> p n e", n=NT)
        IB = 2 * B

        class Experts:

            def __init__(self, n):
                self.loaded = [sem(f"e{n}_loaded{i}") for i in range(2)]
                self.logits = sem(f"e{n}_logits")
                self.sm = sem(f"e{n}_sm")
                self.exps = sem(f"e{n}_exps")
                self.pre = Signal(sem(f"e{n}_pre"), IB * NF)
                self.act = Signal(sem(f"e{n}_act"), IB * NF)
                self.h = Signal(sem(f"e{n}_h"), IB * NF)
                self.y = Signal(sem(f"e{n}_y"), IB, 2)
                self.acc = Signal(sem(f"e{n}_acc"), IB, 2)

        ex = [Experts(2), Experts(3)]

        def moe_sync(sp, which, done):
            src, n = (ins["experts2"], W2) if which == 0 else (ins["experts3"], W3)
            s = ex[which]
            sp.wait_ge(turn_done, done)
            for i in range(2):
                sp.dma_start(wts[:, i, 0:n], src[:, i, :]).then_inc(s.loaded[i], 16)
            with sp.Fori(0, E // 2 - 1) as r:
                for i in range(2):
                    sp.wait_ge(s.y.sem, s.y.at(r, (i + 1) * B))
                    sp.dma_start(wts[:, i, 0:n], src[:, ds(2 * r + (2 + i), 1), :].rearrange("p a n -> p (a n)"))\
                        .then_inc(s.loaded[i], 16)

        def moe_tensor(pe, which, done):
            s = ex[which]
            pe.wait_ge(turn_done, done)
            pe.wait_ge(mats_loaded[5], 16)
            pe.sem_inc(s.y.sem, s.y.ahead)
            n = 16 if which == 0 else 8
            name = "L2_ffn_w_router" if which == 0 else "L3_ffn_gate_w"
            for i in range(NT):
                if i % T == 0:
                    pe.wait_ge(xnT_ready, xnT_count(5 + 2 * which) - B + i // T + 1)
                ins_ = pe.matmul(bank(7)[:, i * n:i * n + n], xnT[:, i * P:i * P + P], mat(name, 0, n),
                                 start=True, stop=True)
            ins_.then_inc(s.logits, 1)

            def up(r, i):
                e, b = divmod(i, B)
                if b == 0:
                    pe.wait_ge(s.loaded[e], r * 16 + 16)
                for f in range(NF):
                    k = i * NF + f
                    if which == 0:
                        if k >= 2:
                            pe.wait_ge(s.h.sem, s.h.at(r, k - 1))
                        pe.matmul(bank(2 * (k % 2)), wts[:, e, f * P:f * P + P], xnT[:, b * S:b * S + S],
                                  start=True, stop=True)
                        ins_ = pe.matmul(bank(2 * (k % 2) + 1), wts[:, e, FF + f * P:FF + f * P + P],
                                         xnT[:, b * S:b * S + S], start=True, stop=True)
                    else:
                        if k >= 4:
                            pe.wait_ge(s.act.sem, s.act.at(r, k - 3))
                        ins_ = pe.matmul(bank(k % 4), wts[:, e, f * P:f * P + P], xnT[:, b * S:b * S + S],
                                         start=True, stop=True)
                    ins_.then_inc(s.pre.sem, 1)

            def down(r, i):
                e = i // B
                pe.wait_ge(s.acc.sem, s.acc.at(r, i - 1))
                ready = s.h if which == 0 else s.act
                pe.wait_ge(ready.sem, ready.at(r, (i + 1) * NF))
                off = 2 * FF if which == 0 else FF
                for t in range(T):
                    for f in range(NF):
                        ins_ = pe.matmul(bank(4 + i % 2)[:, t * P:t * P + P], h_m[:, i % 2, f, t * P:t * P + P],
                                         wts[:, e, off + f * P:off + f * P + P], start=(f == 0), stop=(f == NF - 1))
                ins_.then_inc(s.y.sem, 1)

            with pe.Fori(0, E // 2) as r:
                for i in range(IB + 1):
                    if i < IB:
                        up(r, i)
                    if i >= 1:
                        down(r, i - 1)

        def moe_scalar(act, which, done):
            s = ex[which]
            act.wait_ge(s.sm, 1)
            lg = mw["lg"].rearrange("p (n k e) -> p n k e", n=NT, e=E)
            pr = mw["pr"].rearrange("p (n k e) -> p n k e", n=NT, e=E)
            if which == 0:
                act.activation(pr[:, :, 0, :], lg[:, :, 0, :], ACT.Exp)
                act.activation(pr[:, :, 1, :], lg[:, :, 1, :], ACT.Exp, scale=1.0 / 0.1).then_inc(s.exps, 1)
            else:
                act.activation(mw["pr"][:, 0:NT * E], mw["lg"][:, 0:NT * E], ACT.Exp).then_inc(s.exps, 1)
            with act.Fori(0, E // 2) as r:
                for i in range(IB):
                    for f in range(NF):
                        k = i * NF + f
                        act.wait_ge(s.pre.sem, s.pre.at(r, k + 1))
                        if which == 0:
                            if k >= 2:
                                act.wait_ge(s.h.sem, s.h.at(r, k - 1))
                            act.activation(sg[:, k % 2, :], bank(2 * (k % 2)), ACT.Silu).then_inc(s.act.sem, 1)
                        else:
                            if f == 0:
                                act.wait_ge(s.y.sem, s.y.at(r, i - 1))
                            act.activation(h_m[:, i % 2, f, :], bank(k % 4), ACT.Gelu, bias=wts[:, i // B, 2 * FF + f:2 * FF + f + 1])\
                                .then_inc(s.act.sem, 1)

        def moe_vector(dve, step, which, done):
            s = ex[which]
            dve.wait_ge(turn_done, done)
            step(dve.memset(mw["acc"], 0.0))
            dve.sem_inc(s.acc.sem, s.acc.ahead)
            dve.wait_ge(s.logits, 1)
            if which == 0:
                lg = mw["lg"].rearrange("p (n e) -> p n e", e=E)
                pr = mw["pr"].rearrange("p (n e) -> p n e", e=E)
                mx, sm = mw["mx"], mw["sm"]
                n2 = 2 * NT
                step(dve.tensor_copy(mw["lg"], bank(7)[:, 0:NT * 16]))
                step(dve.tensor_reduce(mx, lg, X, ALU.max))
                dve.tensor_tensor(lg, lg, mx.unsqueeze(2).to_broadcast([P, n2, E]), ALU.subtract).then_inc(s.sm, 1)
                dve.wait_ge(s.exps, 1)
                step(dve.tensor_reduce(sm, pr, X, ALU.add))
                step(dve.reciprocal(sm, sm))
                step(dve.tensor_tensor(pr, pr, sm.unsqueeze(2).to_broadcast([P, n2, E]), ALU.mult))
                both = mw["pr"].rearrange("p (n k e) -> p n k e", n=NT, e=E)
                step(dve.tensor_tensor(cw, both[:, :, 0, :], both[:, :, 1, :], ALU.mult))
                step(dve.tensor_reduce(sm[:, 0:NT], cw, X, ALU.add))
                step(dve.tensor_scalar(sm[:, 0:NT], sm[:, 0:NT], 1e-9, None, ALU.add))
                step(dve.reciprocal(sm[:, 0:NT], sm[:, 0:NT]))
                step(dve.tensor_tensor(cw, cw, sm[:, 0:NT].unsqueeze(2).to_broadcast([P, NT, E]), ALU.mult))
            else:
                lg = mw["lg"][:, 0:NT * E].rearrange("p (n e) -> p n e", e=E)
                top = mw["top"].rearrange("p (n e) -> p n e", e=E)
                idx = mw["idx"].bitcast(U32).rearrange("p (n e) -> p n e", e=E)
                idxf = mw["idxf"].rearrange("p (n e) -> p n e", e=E)
                hot = mw["hot"].rearrange("p (n e) -> p n e", e=E)
                ex8 = mw["pr"][:, 0:NT * E].rearrange("p (n e) -> p n e", e=E)
                sm = mw["sm"][:, 0:NT]
                step(dve.tensor_tensor(lg, bank(7)[:, 0:NT * E].rearrange("p (n e) -> p n e", e=E),
                                       row("L3_ffn_gate_b", 0, E).unsqueeze(1).to_broadcast([P, NT, E]), ALU.add))
                for i in range(NT):
                    step.mark(dve.max(top[:, i, :], lg[:, i, :]))
                step.wait()
                for i in range(NT):
                    step.mark(dve.max_index(idx[:, i, :], top[:, i, :], lg[:, i, :]))
                step.wait()
                step(dve.tensor_copy(mw["idxf"], mw["idx"].bitcast(U32)))
                picks = pick[:, :].unsqueeze(1).to_broadcast([P, NT, E])
                step(dve.tensor_tensor(hot, picks, idxf[:, :, 0:1].to_broadcast([P, NT, E]), ALU.is_equal))
                step(dve.tensor_tensor(cw, picks, idxf[:, :, 1:2].to_broadcast([P, NT, E]), ALU.is_equal))
                step(dve.tensor_tensor(hot, hot, cw, ALU.add))
                dve.tensor_tensor(lg, lg, top[:, :, 0:1].to_broadcast([P, NT, E]), ALU.subtract).then_inc(s.sm, 1)
                dve.wait_ge(s.exps, 1)
                step(dve.tensor_tensor(cw, ex8, hot, ALU.mult))
                step(dve.tensor_reduce(sm, cw, X, ALU.add))
                step(dve.reciprocal(sm, sm))
                step(dve.tensor_tensor(cw, cw, sm.unsqueeze(2).to_broadcast([P, NT, E]), ALU.mult))

            def gate(r, i):
                for f in range(NF):
                    k = i * NF + f
                    dve.wait_ge(s.act.sem, s.act.at(r, k + 1))
                    if f == 0:
                        dve.wait_ge(s.y.sem, s.y.at(r, i - 1))
                    dve.tensor_tensor(h_m[:, i % 2, f, :], sg[:, k % 2, :], bank(2 * (k % 2) + 1), ALU.mult)\
                        .then_inc(s.h.sem, 1)

            def add_up(r, i):
                e, b = divmod(i, B)
                dve.wait_ge(s.y.sem, s.y.at(r, i + 1))
                src = bank(4 + i % 2).rearrange("p (t d) -> p t d", t=T)
                if which == 1:
                    bias = rows[:, ds(ROW_AT["L3_ffn_b2"][0] + (2 * r + e) * D, D)].unsqueeze(1).to_broadcast([P, T, D])
                    step(dve.tensor_tensor(y_m[:, i % 2], src, bias, ALU.add))
                    src = y_m[:, i % 2]
                for t in range(T):
                    n = b * T + t
                    ins_ = dve.scalar_tensor_tensor(out=acc[:, n, :], in0=src[:, t, :], scalar=cw[:, n, ds(2 * r + e, 1)],
                                                    in1=acc[:, n, :], op0=ALU.mult, op1=ALU.add)
                ins_.then_inc(s.acc.sem, 1)

            with step.loop(E // 2, IB * which) as r:
                for i in range(IB + 1):
                    if which == 0 and i < IB:
                        gate(r, i)
                    if i >= 1:
                        add_up(r, i - 1)
            dve.wait_ge(s.acc.sem, s.acc.at(E // 2 - 1, IB))
            n = 6 + which
            for b in range(B):
                at = slice(b * T, b * T + T)
                dve.scalar_tensor_tensor(out=x[:, at, :], in0=acc[:, at, :], scalar=tg[:, n:n + 1], in1=x[:, at, :],
                                         op0=ALU.mult, op1=ALU.add).then_inc(x_new if which == 0 else x_final, 1)
            if which == 0:
                dve.wait_ge(x_new, B)
                dve.sem_inc(turn_done, 1)

        def moe2_sync(sp, use, done):
            moe_sync(sp, 0, done)

        def moe3_sync(sp, use, done):
            moe_sync(sp, 1, done)

        def moe2_tensor(pe, use, done):
            moe_tensor(pe, 0, done)

        def moe3_tensor(pe, use, done):
            moe_tensor(pe, 1, done)

        def moe2_scalar(act, step, use, done):
            moe_scalar(act, 0, done)

        def moe3_scalar(act, step, use, done):
            moe_scalar(act, 1, done)

        def moe2_vector(dve, step, use, done):
            moe_vector(dve, step, 0, done)

        def moe3_vector(dve, step, use, done):
            moe_vector(dve, step, 1, done)

        def setup_pool(pool, step):
            pool.memset(ident[:, :], 0.0)
            pool.memset(head_of_row[:, :], 1.0)
            pool.memset(expo[:, :], -0.5)
            step(pool.memset(head_of_key[:, :, :], 1.0))
            pool.affine_select(out=ident[:, :], in_=ident[:, :], compare_op=ALU.not_equal, fill=1.0, base=0,
                               pattern=[[-1, P]], channel_multiplier=1).then_inc(consts_ready, 1)
            step(pool.affine_select(out=head_of_row[:, :], in_=head_of_row[:, :], compare_op=ALU.is_ge, fill=0.0, base=0,
                                    pattern=[[-DK, H]], channel_multiplier=1))
            pool.affine_select(out=head_of_row[:, :], in_=head_of_row[:, :], compare_op=ALU.is_ge, fill=0.0,
                               base=DK - 1, pattern=[[DK, H]], channel_multiplier=-1).then_inc(consts_ready, 1)
            step(pool.affine_select(out=head_of_key[:, :, :], in_=head_of_key[:, :, :], compare_op=ALU.is_ge, fill=0.0,
                                    base=0, pattern=[[P, NCH], [-KC, HH]], channel_multiplier=1))
            step(pool.affine_select(out=head_of_key[:, :, :], in_=head_of_key[:, :, :], compare_op=ALU.is_ge, fill=0.0,
                                    base=KC - 1, pattern=[[-P, NCH], [KC, HH]], channel_multiplier=-1))
            pool.sem_inc(consts_ready, 1)

        def routing_constants(pool, step):
            pool.wait_ge(small_loaded, 32)
            pool.memset(earlier[:, :, :], 1.0)
            pool.memset(tokens[:, :, :, :], 0.0)
            pool.memset(junk[:, :], 0.0)
            def of_k(which, k):
                return ((k_inv[:, which, :], S, 1.0 / k), (k_log[:, which:which + 1], 1, float(np.log(k))),
                        (k_col[:, which:which + 1], 1, float(k * np.exp(LIFT))),
                        (k_exp[:, which:which + 1], 1, float(np.log(k) + LIFT)),
                        (k_ln[:, which:which + 1], 1, float(np.exp(-LIFT) / k)))

            for which in range(2):
                for buf, _, value in of_k(which, K_OF[which][1]):
                    pool.memset(buf, value)
            step(pool.memset(row_of[:, :, :], 1.0))
            for which in range(2):
                for buf, n, value in of_k(which, K_OF[which][0]):
                    ins_ = pool.affine_select(out=buf, in_=buf, compare_op=ALU.is_ge, fill=value, base=-B,
                                              pattern=[[0, n]], channel_multiplier=1)
            step(ins_)
            pool.affine_select(out=earlier[:, :, :], in_=earlier[:, :, :], compare_op=ALU.is_gt, fill=0.0, base=0,
                               pattern=[[P, T], [-1, S]], channel_multiplier=1)
            pool.affine_select(out=row_of[:, :, :], in_=row_of[:, :, :], compare_op=ALU.is_equal, fill=0.0, base=0,
                               pattern=[[-1, 2 * B], [0, P]], channel_multiplier=1)
            pool.iota(slot_no[:, :], [[1, NKV]], base=0, channel_multiplier=0, allow_small_or_imprecise_dtypes=True)
            pool.iota(pick[:, :], [[1, 8]], base=0, channel_multiplier=0, allow_small_or_imprecise_dtypes=True)
            for kind, (name, base) in enumerate((("L0_ffn_routing_token", 0), ("L1_ffn_q_routing_token", 0),
                                                 ("L1_ffn_kv_routing_token", B))):
                for b in range(B):
                    ins_ = pool.tensor_copy(tokens[:, kind, b, base + b:base + b + 1], col(name))
            ins_.then_inc(routing_ready, 1)

        def setup_sync(sp):
            sp.dma_start(ctxT[:, :, :], ins["ctxT"]).then_inc(ctx_loaded, 16)
            load_matrices(sp, 0)
            sp.dma_start(x[:, :, :], ins["x"]).then_inc(x_loaded, 16)
            sp.dma_start(cols[:, :], ins["cols"]).then_inc(small_loaded, 16)
            sp.dma_start(rows[:, :], ins["rows"].to_broadcast([P, NROW])).then_inc(small_loaded, 16)

        def gates(act):
            act.wait_ge(small_loaded, 32)
            act.activation(tg[:, :], row("g_xattn", 0, 8), ACT.Tanh).then_inc(gates_ready, 1)
            for i, layer in enumerate(("L2", "L3")):
                act.mul(bq_s[:, i:i + 1], col(layer + "_xattn_bq"), float(DK) ** -0.5).then_inc(bq_scaled, 1)

        def setup_vector(dve):
            dve.wait_ge(x_loaded, 16)
            dve.sem_inc(o_read.sem, o_read.ahead)
            dve.sem_inc(turn_done, 1)

        ENGINE_PARTS = {
            "sync": {"attend": attend_sync, "moe2": moe2_sync, "moe3": moe3_sync},
            "gpsimd": {"norm": norm_pool, "kv": kv_pool, "attend": attend_pool, "ffn0": ffn0_pool,
                       "gated": gated_pool, "route0": route0_pool, "self": self_pool,
                       "route1": route1_pool},
            "scalar": {"norm": norm_scalar, "kv": kv_scalar, "attend": attend_scalar, "ffn0": ffn0_scalar,
                       "gated": gated_scalar, "route0": route0_scalar, "self": self_scalar,
                       "route1": route1_scalar, "moe2": moe2_scalar, "moe3": moe3_scalar},
            "tensor": {"norm": norm_tensor, "kv": kv_tensor, "attend": attend_tensor, "ffn0": ffn0_tensor,
                       "gated": gated_tensor, "route0": route0_tensor, "self": self_tensor,
                       "route1": route1_tensor, "moe2": moe2_tensor, "moe3": moe3_tensor},
            "vector": {"norm": norm_vector, "attend": attend_vector, "ffn0": ffn0_vector, "gated": gated_vector,
                        "route0": route0_vector, "self": self_vector,
                       "route1": route1_vector, "moe2": moe2_vector, "moe3": moe3_vector},
        }

        def layers(name, *args):
            done = 1
            for part, use in LAYERS:
                f = ENGINE_PARTS[name].get(part)
                if f:
                    f(*args, use, done)
                done += TURNS[part]

        block = ctx.enter_context(nc.Block())

        @block.sync
        def _(sp):
            setup_sync(sp)
            layers("sync", sp)
            for b in range(B):
                sp.wait_ge(x_final, b + 1)
                sp.dma_start(out[:, b * T:b * T + T, :], x[:, b * T:b * T + T, :]).then_inc(stored, 16)
            sp.wait_ge(stored, 16 * B)

        @block.gpsimd
        def _(pool):
            step = Steps(pool, pool_step)
            setup_pool(pool, step)
            layers("gpsimd", pool, step)

        @block.scalar
        def _(act):
            layers("scalar", act, Steps(act, act_step))

        @block.tensor
        def _(pe):
            layers("tensor", pe)

        @block.vector
        def _(dve):
            setup_vector(dve)
            layers("vector", dve, Steps(dve, dve_step))


def _blocks(w):
    n = w.shape[0] // 128
    return w.reshape(n, 128, -1).transpose(1, 0, 2).reshape(128, -1)


def _rows128(w):
    out = np.zeros((128, w.shape[1]), w.dtype)
    out[:w.shape[0]] = w
    return out


def lay_out(v):
    v = {k: np.asarray(a) for k, a in v.items()}
    m = {n: v[n].T for n in ("L0_xattn_Wq", "L0_xattn_Wk", "L0_xattn_Wv", "L0_xattn_Wo", "L0_xattn_W1",
                             "L0_ffn_w1_l", "L0_ffn_w1_h", "L3_xattn_Wq", "L3_xattn_Wk", "L3_xattn_Wv", "L3_xattn_Wo")}
    m["L0_xattn_W2"] = _blocks(v["L0_xattn_W2"].T)
    m["L0_ffn_w2_l"] = _rows128(v["L0_ffn_w2_l"].T)
    m["L0_ffn_w2_h"] = _blocks(v["L0_ffn_w2_h"].T)
    inner = v["L1_xattn_Wq"].shape[1]
    m["L1_xattn_Wk"], m["L1_xattn_Wv"] = v["L1_xattn_Wkv"][:, :inner], v["L1_xattn_Wkv"][:, inner:]
    hid = v["L1_ffn_wq_light"].shape[1]
    m["L1_ffn_wk_light"], m["L1_ffn_wv_light"] = v["L1_ffn_wkv_light"][:, :hid], v["L1_ffn_wkv_light"][:, hid:]
    kv = v["L1_ffn_wkv_heavy"].reshape(HF, 2, DH, D)
    m["L1_ffn_wk_heavy"], m["L1_ffn_wv_heavy"] = (kv[:, i].reshape(hid, D).T for i in range(2))
    for n in ("L1_xattn_Wo", "L1_ffn_wo_light", "L1_ffn_wo_heavy"):
        m[n] = _blocks(v[n])
    mats = np.concatenate([m[n] if n in m else v[n] for n, _ in MATS], axis=1)
    cols = np.concatenate([v[n].reshape(-1, 128).T if v[n].size >= 128 else _rows128(v[n].reshape(-1, 1))
                           for n, _ in COLS], axis=1)
    rows = np.concatenate([v[n].reshape(-1) for n, _ in ROWS]).reshape(1, -1)
    w1 = v["L3_ffn_w1"].transpose(1, 0, 2)
    up = [v["L2_ffn_w_gate"].transpose(1, 0, 2), v["L2_ffn_w_up"].transpose(1, 0, 2)]
    down = [v[n].reshape(E, NF, 128, D).transpose(2, 0, 1, 3).reshape(128, E, NF * D)
            for n in ("L2_ffn_w_down", "L3_ffn_w2")]
    return {
        "x": v["x"].reshape(NT, P, D).transpose(1, 0, 2),
        "ctxT": v["ctx_1024"].transpose(2, 0, 1),
        "bias": v["fside_Bx16xSxS2_0"].reshape(B, H, T, P, KC).transpose(0, 2, 3, 1, 4).reshape(NT, P, H * KC),
        "mask": v["mask_Bx1xSxS2_ik1"].reshape(NT, P, KC),
        "mats": mats, "cols": cols, "rows": rows,
        "experts2": np.concatenate([up[0], up[1], down[0]], axis=2),
        "experts3": np.concatenate([w1, down[1], v["L3_ffn_b1"].reshape(E, NF, 128).transpose(2, 0, 1)], axis=2),
    }


def build(nc, arrays):
    ins = {n: nc.dram_tensor(f"in_{n}_dram", a.shape, mybir.dt.from_np(a.dtype), kind="ExternalInput").ap()
           for n, a in arrays.items()}
    out = nc.dram_tensor("out_0_dram", (P, NT, D), F32, kind="ExternalOutput").ap()
    flamingo_kernel(nc, ins, out)


def kernel(**inputs):
    import concourse.bacc as _bacc
    from concourse.bass_utils import run_bass_kernel_spmd as _run

    arrays = {n: np.ascontiguousarray(a) for n, a in lay_out(inputs).items()}
    nc = _bacc.Bacc("TRN2", target_bir_lowering=False, num_devices=1)
    build(nc, arrays)
    r = _run(nc, [{f"in_{n}_dram": a for n, a in arrays.items()}], core_ids=[0])
    return r.results[0]["out_0_dram"].transpose(1, 0, 2).reshape(B, S, D)
```
